# Optimizing a Trainium2 kernel written in Bass

```python
import numpy as np
import jax
import jax.numpy as jnp

def _softmax(x, axis=-1):
    return jax.nn.softmax(x, axis=axis)

def _gelu(x):
    return jax.nn.gelu(x, approximate=True)

def _silu(x):
    return jax.nn.silu(x)

def _sigmoid(x):
    return jax.nn.sigmoid(x)

def _layernorm(x, axis=-1, eps=1e-05):
    m = jnp.mean(x, axis=axis, keepdims=True)
    v = jnp.var(x, axis=axis, keepdims=True)
    return (x - m) / jnp.sqrt(v + eps)

def _scatter_add(tgt, idx, src, axis=0):
    return tgt.at[idx].add(src)

def _segment_sum(src, seg, n):
    return jax.ops.segment_sum(src, seg, n)
kernel_name = 'mk_gnn_preln_d2_gnn_r16_206b36'

def setup_inputs(seed: int=0):
    np.random.seed(seed)
    _w = jnp.asarray

    def _rec_inputs():
        import jax
        import jax.numpy as jnp
        _gk = jax.random.key(seed)
        x = -0.0003713 + 1 * jax.random.normal(jax.random.fold_in(_gk, 1), (6250, 128), jnp.float32)
        src = jax.random.randint(jax.random.fold_in(_gk, 2), (200000,), 0, 6250, jnp.int32)
        dst = jnp.minimum((6250 * jax.random.uniform(jax.random.fold_in(_gk, 3), (200000,)) ** 2.0).astype(jnp.int32), 99999)
        _o = jnp.argsort(dst, stable=True)
        src = src[_o]
        dst = dst[_o]
        edge_attr_16 = 0.000196303 + 1.00016 * jax.random.normal(jax.random.fold_in(_gk, 11), (200000, 16), jnp.float32)
        return (x, src, dst, edge_attr_16)
    x, src, dst, edge_attr_16 = _rec_inputs()

    def _L0_gnn_setup():
        import jax, jax.numpy as jnp
        import numpy as np
        N_NODES = 6250
        LN_EPS = 1e-05

        def _mean_aggregate(h, src, dst):
            msgs = h[src]
            summed = jax.ops.segment_sum(msgs, dst, num_segments=N_NODES)
            cnt = jax.ops.segment_sum(jnp.ones_like(dst, dtype=h.dtype), dst, num_segments=N_NODES)
            return summed / jnp.maximum(cnt, 1.0)[:, None]

        def _sage_conv(h, src, dst, W_l, W_r, b):
            agg = _mean_aggregate(h, src, dst)
            return agg @ W_l.T + h @ W_r.T + b
        key = jax.random.key(seed)
        ks = jax.random.split(key, 10)
        d_in, d_hid, d_out = (128, 256, 128)
        n_edges = 100000
        x = jax.random.normal(ks[0], (N_NODES, d_in), dtype=jnp.float32)
        edge_index = jax.random.randint(ks[1], (2, n_edges), 0, N_NODES, dtype=jnp.int32)
        s1 = 1.0 / np.sqrt(d_in)
        s2 = 1.0 / np.sqrt(d_hid)
        return {'x': x, 'edge_index': edge_index, 'W1l': jax.random.uniform(ks[2], (d_hid, d_in), jnp.float32, -s1, s1), 'W1r': jax.random.uniform(ks[3], (d_hid, d_in), jnp.float32, -s1, s1), 'b1': jnp.zeros((d_hid,), jnp.float32), 'W2l': jax.random.uniform(ks[4], (d_out, d_hid), jnp.float32, -s2, s2), 'W2r': jax.random.uniform(ks[5], (d_out, d_hid), jnp.float32, -s2, s2), 'b2': jnp.zeros((d_out,), jnp.float32), 'gamma': jnp.ones((d_out,), jnp.float32), 'beta': jnp.zeros((d_out,), jnp.float32)}
    _L0_gnn_all = _L0_gnn_setup()
    _L0_gnn_in = {k: v for k, v in _L0_gnn_all.items() if k in ('W1l', 'W1r', 'b1', 'W2l', 'W2r', 'b2', 'gamma', 'beta')}
    del _L0_gnn_all

    def _L1_gnn_setup():
        import jax, jax.numpy as jnp
        import numpy as np
        NEG_SLOPE = 0.2

        def _gat_edge_forward(x, edge_index, edge_attr, W, W_edge, att_src, att_dst, att_edge, bias):
            N = x.shape[0]
            H, C = att_src.shape
            src, dst = (edge_index[0], edge_index[1])
            ones = jnp.ones((edge_attr.shape[0],), dtype=x.dtype)
            cnt = jax.ops.segment_sum(ones, dst, num_segments=N)
            attr_sum = jax.ops.segment_sum(edge_attr, dst, num_segments=N)
            loop_attr = attr_sum / jnp.maximum(cnt, 1.0)[:, None]
            loop_idx = jnp.arange(N, dtype=edge_index.dtype)
            src_all = jnp.concatenate([src, loop_idx])
            dst_all = jnp.concatenate([dst, loop_idx])
            attr_all = jnp.concatenate([edge_attr, loop_attr], axis=0)
            x_l = (x @ W).reshape(N, H, C)
            a_src = jnp.einsum('nhc,hc->nh', x_l, att_src)
            a_dst = jnp.einsum('nhc,hc->nh', x_l, att_dst)
            e = (attr_all @ W_edge).reshape(-1, H, C)
            a_edge = jnp.einsum('ehc,hc->eh', e, att_edge)
            logits = jax.nn.leaky_relu(a_src[src_all] + a_dst[dst_all] + a_edge, NEG_SLOPE)
            m = jax.ops.segment_max(logits, dst_all, num_segments=N)
            p = jnp.exp(logits - m[dst_all])
            denom = jax.ops.segment_sum(p, dst_all, num_segments=N)
            alpha = p / denom[dst_all]
            msgs = alpha[:, :, None] * x_l[src_all]
            out = jax.ops.segment_sum(msgs, dst_all, num_segments=N)
            return out.reshape(N, H * C) + bias
        key = jax.random.key(seed)
        ks = jax.random.split(key, 8)
        N, E, DIN, EDIM, H, C = (6250, 100000, 128, 16, 4, 32)
        s = 1.0 / np.sqrt(DIN)
        return {'x': jax.random.normal(ks[0], (N, DIN), jnp.float32), 'edge_index': jax.random.randint(ks[1], (2, E), 0, N, jnp.int64), 'edge_attr': jax.random.normal(ks[2], (E, EDIM), jnp.float32), 'W': jax.random.normal(ks[3], (DIN, H * C), jnp.float32) * s, 'W_edge': jax.random.normal(ks[4], (EDIM, H * C), jnp.float32) * (1.0 / np.sqrt(EDIM)), 'att_src': jax.random.normal(ks[5], (H, C), jnp.float32) * 0.1, 'att_dst': jax.random.normal(ks[6], (H, C), jnp.float32) * 0.1, 'att_edge': jax.random.normal(ks[7], (H, C), jnp.float32) * 0.1, 'bias': jnp.zeros((H * C,), jnp.float32)}
    _L1_gnn_all = _L1_gnn_setup()
    _L1_gnn_in = {k: v for k, v in _L1_gnn_all.items() if k in ('W', 'W_edge', 'att_src', 'att_dst', 'att_edge', 'bias')}
    del _L1_gnn_all
    return {'x': x, 'src': src, 'dst': dst, 'edge_attr_16': edge_attr_16, 'L0_gnn_W1l': _L0_gnn_in['W1l'], 'L0_gnn_W1r': _L0_gnn_in['W1r'], 'L0_gnn_b1': _L0_gnn_in['b1'], 'L0_gnn_W2l': _L0_gnn_in['W2l'], 'L0_gnn_W2r': _L0_gnn_in['W2r'], 'L0_gnn_b2': _L0_gnn_in['b2'], 'L0_gnn_gamma': _L0_gnn_in['gamma'], 'L0_gnn_beta': _L0_gnn_in['beta'], 'L1_gnn_W': _L1_gnn_in['W'], 'L1_gnn_W_edge': _L1_gnn_in['W_edge'], 'L1_gnn_att_src': _L1_gnn_in['att_src'], 'L1_gnn_att_dst': _L1_gnn_in['att_dst'], 'L1_gnn_att_edge': _L1_gnn_in['att_edge'], 'L1_gnn_bias': _L1_gnn_in['bias']}

def reference(x, src, dst, edge_attr_16, L0_gnn_W1l, L0_gnn_W1r, L0_gnn_b1, L0_gnn_W2l, L0_gnn_W2r, L0_gnn_b2, L0_gnn_gamma, L0_gnn_beta, L1_gnn_W, L1_gnn_W_edge, L1_gnn_att_src, L1_gnn_att_dst, L1_gnn_att_edge, L1_gnn_bias):
    import jax
    import jax.numpy as jnp

    def _L0_gnn_ref(x, edge_index, W1l, W1r, b1, W2l, W2r, b2, gamma, beta):
        import jax, jax.numpy as jnp
        import numpy as np
        N_NODES = 6250
        LN_EPS = 1e-05

        def _mean_aggregate(h, src, dst):
            msgs = h[src]
            summed = jax.ops.segment_sum(msgs, dst, num_segments=N_NODES)
            cnt = jax.ops.segment_sum(jnp.ones_like(dst, dtype=h.dtype), dst, num_segments=N_NODES)
            return summed / jnp.maximum(cnt, 1.0)[:, None]

        def _sage_conv(h, src, dst, W_l, W_r, b):
            agg = _mean_aggregate(h, src, dst)
            return agg @ W_l.T + h @ W_r.T + b
        src, dst = (edge_index[0], edge_index[1])
        h = jax.nn.relu(_sage_conv(x, src, dst, W1l, W1r, b1))
        h = _sage_conv(h, src, dst, W2l, W2r, b2)
        h = h + x
        mu = jnp.mean(h, axis=-1, keepdims=True)
        var = jnp.mean(jnp.square(h - mu), axis=-1, keepdims=True)
        return (h - mu) * jax.lax.rsqrt(var + LN_EPS) * gamma + beta

    def _L1_gnn_ref(x, edge_index, edge_attr, W, W_edge, att_src, att_dst, att_edge, bias):
        import jax, jax.numpy as jnp
        import numpy as np
        NEG_SLOPE = 0.2

        def _gat_edge_forward(x, edge_index, edge_attr, W, W_edge, att_src, att_dst, att_edge, bias):
            N = x.shape[0]
            H, C = att_src.shape
            src, dst = (edge_index[0], edge_index[1])
            ones = jnp.ones((edge_attr.shape[0],), dtype=x.dtype)
            cnt = jax.ops.segment_sum(ones, dst, num_segments=N)
            attr_sum = jax.ops.segment_sum(edge_attr, dst, num_segments=N)
            loop_attr = attr_sum / jnp.maximum(cnt, 1.0)[:, None]
            loop_idx = jnp.arange(N, dtype=edge_index.dtype)
            src_all = jnp.concatenate([src, loop_idx])
            dst_all = jnp.concatenate([dst, loop_idx])
            attr_all = jnp.concatenate([edge_attr, loop_attr], axis=0)
            x_l = (x @ W).reshape(N, H, C)
            a_src = jnp.einsum('nhc,hc->nh', x_l, att_src)
            a_dst = jnp.einsum('nhc,hc->nh', x_l, att_dst)
            e = (attr_all @ W_edge).reshape(-1, H, C)
            a_edge = jnp.einsum('ehc,hc->eh', e, att_edge)
            logits = jax.nn.leaky_relu(a_src[src_all] + a_dst[dst_all] + a_edge, NEG_SLOPE)
            m = jax.ops.segment_max(logits, dst_all, num_segments=N)
            p = jnp.exp(logits - m[dst_all])
            denom = jax.ops.segment_sum(p, dst_all, num_segments=N)
            alpha = p / denom[dst_all]
            msgs = alpha[:, :, None] * x_l[src_all]
            out = jax.ops.segment_sum(msgs, dst_all, num_segments=N)
            return out.reshape(N, H * C) + bias
        return _gat_edge_forward(x, edge_index, edge_attr, W, W_edge, att_src, att_dst, att_edge, bias)
    edge_index = jnp.stack([src, dst])
    h = jnp.maximum(_layernorm(x, axis=-1), 0.0)
    x = x + _L0_gnn_ref(h, edge_index, L0_gnn_W1l, L0_gnn_W1r, L0_gnn_b1, L0_gnn_W2l, L0_gnn_W2r, L0_gnn_b2, L0_gnn_gamma, L0_gnn_beta)
    h = jnp.maximum(_layernorm(x, axis=-1), 0.0)
    x = x + _L1_gnn_ref(h, edge_index, edge_attr_16, L1_gnn_W, L1_gnn_W_edge, L1_gnn_att_src, L1_gnn_att_dst, L1_gnn_att_edge, L1_gnn_bias)
    return x

_drawn_inputs = setup_inputs


def setup_inputs(seed=0):
    import zlib

    import numpy as np

    out = dict(_drawn_inputs(seed))
    spreads = {'L0_gnn_b1': (0.0, 0.1),
     'L0_gnn_b2': (0.0, 0.1),
     'L0_gnn_gamma': (1.0, 0.2),
     'L0_gnn_beta': (0.0, 0.1),
     'L1_gnn_bias': (0.0, 0.1)}
    factors = {'L1_gnn_att_dst': 14.77}
    for name, (base, spread) in spreads.items():
        noise = np.random.default_rng([zlib.crc32(name.encode()), seed]).standard_normal(out[name].shape)
        drawn = base * np.exp(spread * noise) if base else spread * noise
        out[name] = jnp.asarray(drawn.astype(out[name].dtype))
    for name, factor in factors.items():
        out[name] = (out[name] * factor).astype(out[name].dtype)
    return out
```

```python
from contextlib import ExitStack

import concourse.bass as bass
import numpy as np
from concourse import mybir
from concourse.alu_op_type import AluOpType as ALU

F32 = mybir.dt.float32
I32 = mybir.dt.int32
BF16 = mybir.dt.bfloat16
I16 = mybir.dt.int16
ACT = mybir.ActivationFunctionType
AX = mybir.AxisListType
DVE_ONLY = (mybir.EngineType.DVE,)

P = 128
N_NODES, D = 6250, 128
N_EDGES, D_EDGE = 200000, 16
D_HID = 256
HEADS, C_HEAD = 4, 32
N_BLK = -(-N_NODES // P)
QUAD = 4
NB = -(-N_BLK // QUAD) * QUAD
TAIL = N_NODES - (N_BLK - 1) * P

J = 15
TRI = 3
NT = J // TRI
MAX_CHUNKS = (N_EDGES + N_BLK * (P - 1)) // P
N_GRP = 2 * -(-MAX_CHUNKS // (2 * J))
KC = -(-N_GRP * J // P)
NK = KC * P
assert NK >= (N_GRP + 1) * J
E_PAD = KC * P * P
SENTINEL = 16384

HW = C_HEAD + 1
XW = HEADS * HW
MW = XW + 2 * HEADS
BIG = float(2.0 ** 100)
EPS = 1e-5
SLOPE = 0.2

EP, ES = 125, 32
E_STEPS = N_EDGES // (EP * ES)
assert E_STEPS * EP * ES == N_EDGES and 2 * E_STEPS <= N_GRP


def hold(eng, semaphore, value):
    eng.wait_ge(semaphore, value)
    eng.nop(nofuse=True)


class Chain:

    def __init__(self, eng, semaphore, i=None, per=0):
        self.eng, self.semaphore, self.i, self.per, self.n = eng, semaphore, i, per, 0

    def count(self):
        return self.n if self.i is None else self.i * self.per + self.n

    def link(self, ins, alone=False):
        ins.then_inc(self.semaphore, 1)
        self.n += 1
        if alone:
            hold(self.eng, self.semaphore, self.count())
        else:
            self.eng.wait_ge(self.semaphore, self.count())

    def end(self):
        assert self.i is None or self.n == self.per, (self.n, self.per)


def build(nc, x, src, dst, edge_attr, W1l, W1r, b1, W2l, W2r, b2, gamma, beta,
          W, W_edge, att_src, att_dst, att_edge, bias, out, dbg=None, stop=99):
    with ExitStack() as top:
        stages = []

        def sb(name, shape, dt=F32, at=top):
            return at.enter_context(nc.sbuf_tensor(f"{name}_{len(stages)}", shape, dt))

        def ps(name, shape, at):
            return at.enter_context(nc.psum_tensor(f"{name}_{len(stages)}", shape, F32))

        def sem(name, at):
            return at.enter_context(nc.semaphore(f"{name}_{len(stages)}"))

        src_pad = nc.dram_tensor("src_pad", [E_PAD], I32).ap()
        dst_pad = nc.dram_tensor("dst_pad", [E_PAD], I32).ap()
        ae_tab = nc.dram_tensor("ae_tab", [N_EDGES * HEADS + 4 * P * HEADS], F32).ap()
        h_tab = nc.dram_tensor("h_tab", [NB * P, D], F32).ap()
        y_tab = nc.dram_tensor("y_tab", [NB * P, D], F32).ap()
        x_tab = nc.dram_tensor("x_tab", [NB * P, XW], F32).ap()

        RCNT = sb("RCNT", [P, NB])
        NOEDGE = sb("NOEDGE", [P, NB])
        ADST = sb("ADST", [P, NB, HEADS])
        SRC = sb("SRC", [P, NK], I32)
        REL = sb("REL", [P, NK], BF16)
        KEY = sb("KEY", [P, NK])
        LAST = sb("LAST", [P, NK], BF16)
        BLK = sb("BLK", [1, N_GRP + 1, 16], I16)
        LINK = sb("LINK", [1, NK])
        WHOLE = sb("WHOLE", [1, NK])
        ek4i = sb("ek4i", [P, KC], I32)
        ident = sb("ident", [P, P])
        rowi = sb("rowi", [P, P])
        coli = sb("coli", [P, 1])
        ones = sb("ones", [P, P])
        W1T = sb("W1T", [P, 2, D_HID])
        W2T = sb("W2T", [P, 2, 2, D])
        WX = sb("WX", [P, XW + HEADS])
        BD = sb("BD", [P, 8, HEADS])
        b1c = sb("b1c", [P, 2])
        b2row = sb("b2row", [1, 2 * D])
        gam = sb("gam", [P, D])
        bet = sb("bet", [P, D])
        bia = sb("bia", [P, D])
        eps = sb("eps", [P, 1])

        def stage(body):
            stages.append(body.__name__)
            with ExitStack() as at, nc.Block() as block:
                body(at, block)

        def prepare(at, block):
            s_in = sem("p_in", at)
            s_w = sem("p_w", at)
            s_rows = sem("p_rows", at)
            s_io = sem("p_io", at)
            s_g1 = sem("p_g1", at)
            s_gs = sem("p_gs", at)
            s_gd = sem("p_gd", at)
            s_gn = sem("p_gn", at)
            s_d = sem("p_d", at)
            s_p = sem("p_p", at)
            s_kl = sem("p_kl", at)
            s_at = sem("p_at", at)
            s_pad = sem("p_pad", at)
            s_b = sem("p_b", at)
            s_e = sem("p_e", at)
            NTURN = -(-KC // 4)
            dstf = sb("dstf", [P, NK], F32, at)

            irow = sb("irow", [P, P], I32, at)
            icol = sb("icol", [P, 1], I32, at)
            kio = sb("kio", [P, NK], F32, at)
            kpc = sb("kpc", [P, KC], F32, at)
            padt = sb("padt", [P, P], I32, at)
            zero = sb("zero", [P, P], I32, at)
            rows = sb("rows", [P, KC, P], I32, at)
            rowsf = sb("rowsf", [P, KC, P], F32, at)
            srows = sb("srows", [P, KC, P], I32, at)
            nrows = sb("nrows", [P, KC, P], I32, at)
            first = sb("first", [P, KC], F32, at)
            thr = sb("thr", [P, N_BLK + 1], F32, at)
            tcol = sb("tcol", [P, 1], F32, at)
            cmp3 = sb("cmp3", [P, N_BLK + 1, KC], F32, at)
            cnt1 = sb("cnt1", [P, N_BLK + 1], F32, at)
            t1 = sb("t1", [P, 1], F32, at)
            t1i = sb("t1i", [P, 1], I32, at)
            brow = sb("brow", [P, P], I32, at)
            browf = sb("browf", [P, P], F32, at)
            bcmp = sb("bcmp", [P, P], F32, at)
            bcnt = sb("bcnt", [P, 1], F32, at)
            start = sb("start", [P, 1], F32, at)
            eq0 = sb("eq0", [P, P], F32, at)
            eqd = sb("eqd", [P, P], F32, at)
            equ = sb("equ", [P, P], F32, at)
            lt = sb("lt", [P, P], F32, at)
            nch = sb("nch", [P, 1], F32, at)
            nci = sb("nci", [P, 1], I32, at)
            q = sb("q", [P, 1], F32, at)
            dq = sb("dq", [P, 2], F32, at)
            GE = sb("GE", [P, NK], F32, at)
            BK = sb("BK", [P, NK], F32, at)
            ek = sb("ek", [P, KC], F32, at)
            eki = sb("eki", [P, KC], I32, at)
            ek1i = sb("ek1i", [P, KC], I32, at)
            KL = sb("KL", [1, NK], F32, at)
            wl = sb("wl", [P, 2, D], F32, at)
            wr = sb("wr", [P, 2, D], F32, at)
            w2l = sb("w2l", [P, D_HID], F32, at)
            w2r = sb("w2r", [P, D_HID], F32, at)
            wt = sb("wt", [P, D], F32, at)
            we = sb("we", [P, D], F32, at)
            ats = sb("ats", [P, D], F32, at)
            atd = sb("atd", [P, D], F32, at)
            ate = sb("ate", [P, D], F32, at)
            wm = sb("wm", [P, 3, D], F32, at)
            mr = sb("mr", [P, HEADS], F32, at)
            m8 = sb("m8", [P, 8], F32, at)
            pg = sb("pg", [P, 1], F32, at)
            pgi = sb("pgi", [P, 1], I32, at)
            psm = ps("psm", [P, 512], at)
            psb = ps("psb", [P, 4, 512], at)
            pst = ps("pst", [P, 2, 512], at)

            n_tail = E_PAD - N_EDGES
            tail_cols = 112
            assert n_tail % tail_cols == 0 and n_tail // tail_cols <= P
            tail_rows = n_tail // tail_cols

            @block.sync
            def _(sp):
                sp.dma_start(dst_pad[0:N_EDGES].rearrange("(a b) -> a b", a=400),
                             dst.rearrange("(a b) -> a b", a=400)).then_inc(s_in, 16)
                sp.dma_start(src_pad[0:N_EDGES].rearrange("(a b) -> a b", a=400),
                             src.rearrange("(a b) -> a b", a=400)).then_inc(s_in, 16)
                sp.wait_ge(s_pad, 2)
                sp.dma_start(dst_pad[N_EDGES:].rearrange("(a b) -> a b", b=tail_cols),
                             padt[0:tail_rows, 0:tail_cols]).then_inc(s_in, 16)
                sp.dma_start(src_pad[N_EDGES:].rearrange("(a b) -> a b", b=tail_cols),
                             zero[0:tail_rows, 0:tail_cols]).then_inc(s_in, 16)
                sp.wait_ge(s_in, 64)
                sp.dma_start(rows[:], dst_pad.rearrange("(c p e) -> p c e", p=P, e=P)).then_inc(s_rows, 16)
                sp.wait_ge(s_d, 14)
                sp.dma_start(KL[:], KEY[P - 1:P, :]).then_inc(s_kl, 16)
                sp.dma_start(ae_tab[N_EDGES * HEADS:].rearrange("(a b) -> a b", a=16),
                             zero[0:16, :].bitcast(F32)).then_inc(s_at, 16)
                sp.wait_ge(s_at, 16)

            @block.scalar
            def _(act):
                act.dma_start(wl[:], W1l.rearrange("(m p) f -> p m f", p=P)).then_inc(s_w, 16)
                act.dma_start(wr[:], W1r.rearrange("(m p) f -> p m f", p=P)).then_inc(s_w, 16)
                act.dma_start(w2l[:], W2l).then_inc(s_w, 16)
                act.dma_start(w2r[:], W2r).then_inc(s_w, 16)
                act.dma_start(wt[:], W).then_inc(s_w, 16)
                for r in range(8):
                    act.dma_start(we[16 * r:16 * r + 16, :], W_edge).then_inc(s_w, 16)
                for t, a in ((ats, att_src), (atd, att_dst), (ate, att_edge)):
                    row = a.rearrange("h c -> (h c)").rearrange("(o f) -> o f", o=1)
                    act.dma_start(t[:], row.to_broadcast([P, D])).then_inc(s_w, 16)
                for t, a in ((gam, gamma), (bet, beta), (bia, bias)):
                    act.dma_start(t[:], a.rearrange("(o f) -> o f", o=1).to_broadcast([P, D])).then_inc(s_w, 16)
                with nc.allow_non_contiguous_dma(reason="256 words"):
                    act.dma_start(b1c[:], b1.rearrange("(m p) -> p m", p=P)).then_inc(s_w, 16)
                act.wait_ge(s_b, 1)
                act.dma_start(b2row[:, D:], b2.rearrange("(o f) -> o f", o=1)).then_inc(s_w, 16)

            @block.gpsimd
            def _(pool):
                pool.memset(padt[:], SENTINEL).then_inc(s_pad, 1)
                pool.memset(zero[:], 0).then_inc(s_pad, 1)
                pool.iota(irow[:], pattern=[[1, P]], base=0, channel_multiplier=0).then_inc(s_io, 1)
                pool.iota(icol[:], pattern=[[0, 1]], base=0, channel_multiplier=1).then_inc(s_io, 1)
                pool.iota(kio[:], pattern=[[1, NK]], base=0, channel_multiplier=0,
                          allow_small_or_imprecise_dtypes=True).then_inc(s_io, 1)
                pool.iota(kpc[:], pattern=[[P * P, KC]], base=0, channel_multiplier=P,
                          allow_small_or_imprecise_dtypes=True).then_inc(s_io, 1)
                pool.wait_ge(s_d, 4)
                pool.indirect_dma_start(
                    brow[0:N_BLK + 1, :], None, dst_pad.rearrange("(r e) -> r e", e=P),
                    bass.IndirectOffsetOnAxis(ap=t1i[0:N_BLK + 1, :], axis=0)).then_inc(s_g1, 16)
                pool.wait_ge(s_d, 9)
                flat_s = src_pad.rearrange("(o e) -> o e", o=1)
                flat_d = dst_pad.rearrange("(o e) -> o e", o=1)
                for c in range(KC):
                    pool.indirect_dma_start(srows[:, c, :], None, flat_s, bass.IndirectOffsetOnAxis(
                        ap=eki[:, c:c + 1], axis=1)).then_inc(s_gs, 16)
                pool.wait_ge(s_d, 10)
                for c in range(KC):
                    pool.indirect_dma_start(rows[:, c, :], None, flat_d, bass.IndirectOffsetOnAxis(
                        ap=eki[:, c:c + 1], axis=1)).then_inc(s_gd, 16)
                for c in range(KC):
                    pool.indirect_dma_start(nrows[:, c, :], None, flat_d, bass.IndirectOffsetOnAxis(
                        ap=ek1i[:, c:c + 1], axis=1)).then_inc(s_gn, 16)

            @block.vector
            def _(dve):
                own = sem("p_own", at)
                n = [0]

                def link(ins):
                    n[0] += 1
                    ins.then_inc(own, 1)
                    dve.wait_ge(own, n[0])

                steps = [0]

                def step(ins=None):
                    steps[0] += 1
                    ins.then_inc(s_d, 1)
                    dve.wait_ge(s_d, steps[0])

                dve.memset(b2row[:], 0.0).then_inc(s_b, 1)
                dve.memset(dq[:], 1.0)
                dve.memset(eps[:], EPS)
                link(dve.memset(BLK[:], 0))
                step(dve.memset(ones[:], 1.0))
                dve.wait_ge(s_io, 4)
                dve.tensor_copy(rowi[:], irow[:])
                link(dve.tensor_copy(coli[:], icol[:]))
                dve.tensor_scalar(thr[:], rowi[:, 0:N_BLK + 1], float(P), None, ALU.mult)
                dve.tensor_scalar(tcol[:], coli[:], float(P), None, ALU.mult)
                dve.tensor_scalar(eqd[:], rowi[:], 1.0, coli[:], ALU.add, ALU.is_equal)
                dve.tensor_scalar(equ[:], rowi[:], -1.0, coli[:], ALU.add, ALU.is_equal)
                dve.tensor_scalar(lt[:], rowi[:], coli[:], None, ALU.is_gt)
                link(dve.tensor_scalar(ident[:], rowi[:], coli[:], None, ALU.is_equal))
                link(dve.tensor_tensor(eqd[:], eqd[:], ident[:], ALU.subtract))
                step(dve.tensor_tensor(equ[:], ident[:], equ[:], ALU.subtract))
                dve.wait_ge(s_rows, 16)
                link(dve.tensor_copy(first[:], rows[:, :, 0]))
                link(dve.tensor_tensor(
                    cmp3[:], first[:, None, :].to_broadcast([P, N_BLK + 1, KC]),
                    thr[:, :, None].to_broadcast([P, N_BLK + 1, KC]), ALU.is_lt))
                step(dve.tensor_reduce(cnt1[:], cmp3[:], AX.X, ALU.add))
                dve.wait_ge(s_p, 1)
                link(dve.tensor_scalar(t1[0:N_BLK + 1, :], psm[0:N_BLK + 1, 0:1], -1.0, 0.0, ALU.add, ALU.max))
                step(dve.tensor_copy(t1i[0:N_BLK + 1, :], t1[0:N_BLK + 1, :]))
                dve.wait_ge(s_g1, 16)
                link(dve.tensor_copy(browf[0:N_BLK + 1, :], brow[0:N_BLK + 1, :]))
                link(dve.tensor_scalar(bcmp[0:N_BLK + 1, :], browf[0:N_BLK + 1, :], tcol[0:N_BLK + 1, :],
                                       None, ALU.is_lt))
                link(dve.tensor_reduce(bcnt[0:N_BLK + 1, :], bcmp[0:N_BLK + 1, :], AX.X, ALU.add))
                step(dve.tensor_scalar(start[0:N_BLK + 1, :], t1[0:N_BLK + 1, :], float(P),
                                       bcnt[0:N_BLK + 1, :], ALU.mult, ALU.add))
                dve.wait_ge(s_p, 2)
                link(dve.tensor_scalar(nch[0:N_BLK, :], psm[0:N_BLK, 1:2], float(P - 1), None, ALU.add))
                link(dve.tensor_copy(nci[0:N_BLK, :], nch[0:N_BLK, :]))
                link(dve.tensor_scalar(nci[0:N_BLK, :], nci[0:N_BLK, :], 7, None, ALU.arith_shift_right))
                step(dve.tensor_copy(nch[0:N_BLK, :], nci[0:N_BLK, :]))
                dve.wait_ge(s_p, 3)
                link(dve.tensor_copy(nch[0:N_BLK, :], psm[0:N_BLK, 2:3]))
                link(dve.tensor_scalar(q[0:N_BLK, :], nch[0:N_BLK, :], -float(P), start[0:N_BLK, :],
                                       ALU.mult, ALU.add))
                step(dve.tensor_scalar(GE[0:N_BLK, :], kio[0:N_BLK, :], nch[0:N_BLK, :], None, ALU.is_ge))
                dve.wait_ge(s_p, 4)
                step(dve.tensor_copy(dq[0:N_BLK, 0:1], psm[0:N_BLK, 3:4]))
                dve.wait_ge(s_p, 5)
                link(dve.tensor_tensor(ek[:], kpc[:], psm[:, 4:4 + 2 * KC:2], ALU.add))
                link(dve.tensor_scalar(ek[:], ek[:], float(N_EDGES), None, ALU.min))
                link(dve.tensor_copy(eki[:], ek[:]))
                link(dve.tensor_scalar(ek4i[:], ek[:], float(HEADS), None, ALU.mult))
                step(dve.tensor_scalar(ek1i[:], ek[:], 1.0, None, ALU.add))
                dve.wait_ge(s_p, 6)
                step(dve.tensor_scalar(BK[:].rearrange("p (b k) -> p b k", b=4),
                                       psb[:, :, 0:NK // 4], -1.0, float(P), ALU.add, ALU.mult))
                link(dve.tensor_scalar(BLK[:, 0:N_GRP, 0:J], BK[0:1, 0:N_GRP * J].rearrange("o (g j) -> o g j", j=J),
                                       1.0 / P, None, ALU.mult))
                def turn(rows_i, s_rows_in, evacuate, s0):
                    dve.wait_ge(s_rows_in, 16 * KC)
                    link(dve.tensor_copy(rowsf[:], rows_i[:]))
                    step(dve.tensor_copy(rowsf[:, 0, :], rows_i[:, 0, :]))
                    for i in range(NTURN):
                        w = min(4, KC - 4 * i) * P
                        dve.wait_ge(s_p, s0 + i)
                        evacuate(slice(512 * i, 512 * i + w), pst[:, i % 2, 0:w]).then_inc(s_e, 1)
                    dve.wait_ge(s_e, s0 - 7 + NTURN)

                turn(srows, s_gs, lambda c, t: dve.tensor_copy(SRC[:, c], t), 7)
                step(dve.memset(bcnt[:], 0.0))
                turn(rows, s_gd, lambda c, t: dve.tensor_copy(dstf[:, c], t), 7 + NTURN)
                link(dve.tensor_tensor(KEY[:], dstf[:], BK[:], ALU.subtract))
                link(dve.tensor_scalar(KEY[:], KEY[:], P - 0.5, None, ALU.min))
                dve.tensor_copy(REL[:], KEY[:])
                link(dve.tensor_tensor(KEY[:], KEY[:], BK[:], ALU.add))
                step(dve.tensor_scalar(KEY[:], KEY[:], 2 * BIG, None, ALU.mult))
                dve.wait_ge(s_kl, 16)
                dve.memset(LINK[:, 0:1], -BIG)
                dve.tensor_tensor(LINK[:, 1:], KL[:, 0:NK - 1], KEY[0:1, 1:], ALU.subtract)
                link(dve.tensor_tensor(WHOLE[:], KEY[0:1, :], KL[:], ALU.subtract))
                turn(nrows, s_gn, lambda c, t: dve.tensor_tensor(
                    LAST[:, c], dstf[:, c], t, ALU.not_equal), 7 + 2 * NTURN)
                dve.wait_ge(s_w, 16 * 21)
                WXh = WX[:, 0:XW].rearrange("p (h c) -> p h c", h=HEADS)
                dve.tensor_copy(WXh[:, :, 0:C_HEAD], wt[:].rearrange("p (h c) -> p h c", h=HEADS))
                dve.tensor_tensor(wm[:, 0, :], wt[:], ats[:], ALU.mult)
                dve.tensor_tensor(wm[:, 1, :], wt[:], atd[:], ALU.mult)
                link(dve.tensor_tensor(wm[:, 2, :], we[:], ate[:], ALU.mult))
                wmh = wm[:].rearrange("p t (h c) -> p t h c", h=HEADS)
                dve.tensor_reduce(WXh[:, :, C_HEAD], wmh[:, 0], AX.X, ALU.add)
                dve.tensor_reduce(WX[:, XW:], wmh[:, 1], AX.X, ALU.add)
                dve.tensor_reduce(mr[:], wmh[:, 2], AX.X, ALU.add)
                link(dve.tensor_scalar(pgi[:], icol[:], 4, None, ALU.arith_shift_right))
                link(dve.tensor_copy(pg[:], pgi[:]))
                link(dve.tensor_scalar(m8[:], rowi[:, 0:8], pg[:], None, ALU.is_equal))
                link(dve.tensor_tensor(BD[:], m8[:, :, None].to_broadcast([P, 8, HEADS]),
                                       mr[:, None, :].to_broadcast([P, 8, HEADS]), ALU.mult))
                dve.wait_ge(s_p, 7 + 3 * NTURN)
                link(dve.tensor_copy(W1T[:].rearrange("p a b -> p (a b)"), psb[:, 0, :]))
                link(dve.tensor_copy(W2T[:].rearrange("p m l o -> p (m l o)"), psb[:, 1, :]))

            @block.tensor
            def _(pe):
                pe.wait_ge(s_d, 3)
                pe.matmul(psm[0:N_BLK + 1, 0:1], cnt1[:], ones[:, 0:1], start=True, stop=True).then_inc(s_p, 1)
                pe.wait_ge(s_d, 5)
                pe.matmul(psm[0:N_BLK, 1:2], eqd[0:N_BLK + 1, 0:N_BLK], start[0:N_BLK + 1, :],
                          start=True, stop=True).then_inc(s_p, 1)
                pe.wait_ge(s_d, 6)
                pe.matmul(psm[0:N_BLK, 2:3], lt[0:N_BLK, 0:N_BLK], nch[0:N_BLK, :],
                          start=True, stop=True).then_inc(s_p, 1)
                pe.wait_ge(s_d, 7)
                pe.matmul(psm[0:N_BLK, 3:4], equ[0:N_BLK, 0:N_BLK], q[0:N_BLK, :],
                          start=True, stop=True).then_inc(s_p, 1)
                pe.wait_ge(s_d, 8)
                for c in range(KC):
                    mm = pe.matmul(psm[:, 4 + 2 * c:6 + 2 * c], GE[0:N_BLK, c * P:(c + 1) * P], dq[0:N_BLK, :],
                                   start=True, stop=True)
                mm.then_inc(s_p, 1)
                for c in range(4):
                    mm = pe.matmul(psb[:, c, 0:NK // 4], ones[0:N_BLK, :], GE[0:N_BLK, c * NK // 4:(c + 1) * NK // 4],
                                   start=True, stop=True)
                mm.then_inc(s_p, 1)
                for t, s in enumerate((11, 13, 15)):
                    pe.wait_ge(s_d, s)
                    for i in range(NTURN):
                        if t * NTURN + i >= 2:
                            pe.wait_ge(s_e, t * NTURN + i - 1)
                        for c in range(4 * i, min(4 * i + 4, KC)):
                            mm = pe.transpose(pst[:, i % 2, (c % 4) * P:(c % 4) * P + P], rowsf[:, c, :], ident[:])
                        mm.then_inc(s_p, 1)
                pe.wait_ge(s_w, 16 * 21)
                pe.wait_ge(s_d, 10)
                for m in range(2):
                    pe.transpose(psb[:, 0, m * P:m * P + P], wl[:, m, :], ident[:])
                    pe.transpose(psb[:, 0, (2 + m) * P:(3 + m) * P], wr[:, m, :], ident[:])
                    pe.transpose(psb[:, 1, 2 * m * P:(2 * m + 1) * P], w2l[:, m * P:m * P + P], ident[:])
                    mm = pe.transpose(psb[:, 1, (2 * m + 1) * P:(2 * m + 2) * P], w2r[:, m * P:m * P + P], ident[:])
                mm.then_inc(s_p, 1)

        stage(prepare)
        X = sb("X", [P, NB, D])
        H = sb("H", [P, NB, XW])
        ACC = sb("ACC", [P, NB, MW])
        AE = sb("AE", [P, HEADS, NK])


        def first_norm(at, block):
            s_x = sem("n_x", at)
            s_z = sem("n_z", at)
            s_v = sem("n_v", at)
            s_a = sem("n_a", at)
            s_h = sem("n_h", at)
            s_t = sem("n_t", at)
            own = sem("n_own", at)
            st = sb("st", [P, QUAD, 6], F32, at)
            mv = sb("mv", [P, QUAD, 2], F32, at)
            sd = sb("sd", [P, QUAD], F32, at)
            rs = sb("rs", [P, QUAD], F32, at)
            T = sb("T", [P, QUAD, D], F32, at)
            full = N_BLK - 1
            tab = h_tab.rearrange("(b p) f -> p b f", p=P)

            @block.sync
            def _(sp):
                half = full // 2
                xb = x[0:full * P].rearrange("(b p) f -> p b f", p=P)
                sp.dma_start(X[:, 0:half, :], xb[:, 0:half, :]).then_inc(s_x, 16)
                sp.wait_ge(s_z, 1)
                sp.dma_start(X[0:TAIL, full, :], x[full * P:, :]).then_inc(s_x, 16)
                with sp.Fori(0, NB // QUAD) as i:
                    sp.wait_ge(s_h, i + 1)
                    sp.dma_start(tab[:, bass.ds(i * QUAD, QUAD), :],
                                 H[:, bass.ds(i * QUAD, QUAD), 0:D]).then_inc(s_t, 16)
                sp.wait_ge(s_t, 16 * (NB // QUAD))

            @block.scalar
            def _(act):
                half = full // 2
                xb = x[0:full * P].rearrange("(b p) f -> p b f", p=P)
                act.dma_start(X[:, half:full, :], xb[:, half:, :]).then_inc(s_x, 16)
                with act.Fori(0, NB // QUAD) as i:
                    act.wait_ge(s_v, i + 1)
                    act.activation(sd[:], mv[:, :, 1], ACT.Sqrt, bias=eps[:]).then_inc(s_a, 1)

            @block.vector
            def _(dve):
                dve.memset(X[:, full:, :], 0.0).then_inc(s_z, 1)
                dve.wait_ge(s_z, 1)
                dve.wait_ge(s_x, 48)
                with dve.Fori(0, NB // QUAD) as i:
                    c = Chain(dve, own, i, 4)
                    quad = bass.ds(i * QUAD, QUAD)
                    for n in range(QUAD):
                        last = dve.bn_stats(st[:, n, :], X[:, bass.ds(i * QUAD + n, 1), :])
                    c.link(last, alone=True)
                    for n in range(QUAD):
                        last = dve.bn_aggr(mv[:, n, :], st[:, n, :])
                    last.then_inc(s_v, 1)
                    dve.wait_ge(s_v, i + 1)
                    c.link(dve.tensor_tensor(T[:], X[:, quad, :], mv[:, :, 0:1].to_broadcast([P, QUAD, D]),
                                             ALU.subtract))
                    dve.wait_ge(s_a, i + 1)
                    c.link(dve.reciprocal(rs[:], sd[:]))
                    dve.scalar_tensor_tensor(H[:, quad, 0:D], T[:], 0.0, rs[:, :, None].to_broadcast([P, QUAD, D]),
                                             ALU.max, ALU.mult).then_inc(s_h, 1)
                    dve.wait_ge(s_h, i + 1)
                    c.link(dve.memset(T[:, 0, 0:1], 0.0))
                    c.end()

        stage(first_norm)

        def gather_sums(table, edge_terms):
            def body(at, block):
                s_i = sem("g_i", at)
                s_g = [sem(f"g_g{u}", at) for u in range(2)]
                s_o = sem("g_o", at)
                s_m = sem("g_m", at)
                s_c = sem("g_c", at)
                s_one = sem("g_one", at)
                own = sem("g_own", at)
                idx = sb("idx", [P, 2, J], I32, at)
                G = sb("G", [P, 2, J, D + 1], F32, at)
                OH = sb("OH", [P, 2, J, P], F32, at)
                psu = ps("psu", [P, 2, 512], at)
                if edge_terms:
                    s_at = [sem(f"e_at{u}", at) for u in range(2)]
                    s_et = sem("e_t", at)
                    s_ec = sem("e_c", at)
                    s_em = sem("e_m", at)
                    s_eo = sem("e_o", at)
                    s_es = sem("e_s", at)
                    at_in = sb("at_in", [P, 2, ES * D_EDGE], F32, at)
                    at_t = sb("at_t", [P, 4, P], F32, at)
                    ae_o = sb("ae_o", [P, ES * HEADS], F32, at)
                    pet = ps("pet", [P, 4, P], at)
                    pem = ps("pem", [P, 512], at)
                    attr = edge_attr.rearrange("(p e) d -> p (e d)", p=EP)
                    aeo = ae_tab[0:N_EDGES * HEADS].rearrange("(p e) -> p e", p=EP)

                @block.gpsimd
                def _(pool):
                    with pool.Fori(0, N_GRP // 2) as i:
                        for u in range(2):
                            g = 2 * i + u
                            pool.wait_ge(s_i, g + 1)
                            hold(pool, s_m, g * NT + NT)
                            for j in range(J):
                                pool.indirect_dma_start(
                                    G[:, u, j, 0:D], None, table, bass.IndirectOffsetOnAxis(
                                        ap=idx[:, u, j:j + 1], axis=0)).then_inc(s_g[u], 16)

                if edge_terms:
                    @block.sync
                    def _(sp):
                        with sp.Fori(0, E_STEPS // 2) as i:
                            for u in range(2):
                                t = 2 * i + u
                                sp.wait_ge(s_et, t + 1)
                                sp.dma_start(at_in[0:EP, u, :], attr[:, bass.ds(t * ES * D_EDGE, ES * D_EDGE)]
                                             ).then_inc(s_at[u], 16)

                @block.scalar
                def _(act):
                    def group(i, u, terms):
                        g = 2 * i + u
                        act.wait_ge(s_m, g * NT + 2 * NT)
                        act.copy(idx[:, 1 - u, :], SRC[:, bass.ds(g * J + J, J)]).then_inc(s_i, 1)
                        if terms:
                            act.wait_ge(s_et, g + 3)
                            act.copy(at_t[:, :, 0:EP], pet[:, :, 0:EP]).then_inc(s_ec, 1)
                            act.wait_ge(s_em, g + 1)
                            act.copy(ae_o[0:EP, :], pem[0:EP, 0:ES * HEADS]).then_inc(s_eo, 1)
                            act.wait_ge(s_eo, g + 2)
                            act.dma_start(aeo[:, bass.ds(g * ES * HEADS, ES * HEADS)],
                                          ae_o[0:EP, :]).then_inc(s_es, 16)
                            act.wait_ge(s_es, 16 * (g + 1))

                    act.copy(idx[:, 0, :], SRC[:, 0:J]).then_inc(s_i, 1)
                    done = E_STEPS // 2 if edge_terms else 0
                    if edge_terms:
                        with act.Fori(0, done) as i:
                            for u in range(2):
                                group(i, u, True)
                    with act.Fori(done, N_GRP // 2) as i:
                        for u in range(2):
                            group(i, u, False)

                @block.tensor
                def _(pe):
                    def group(i, u, terms):
                        g = 2 * i + u
                        if terms:
                            pe.wait_ge(s_at[u], 16 * (i + 1))
                            pe.wait_ge(s_eo, g + 1)
                            for n in range(4):
                                mm = pe.transpose(pet[:, n, 0:EP], at_in[0:EP, u, n * P:n * P + P],
                                                  ident[0:EP, 0:EP])
                            mm.then_inc(s_et, 1)
                        pe.wait_ge(s_g[u], 16 * J * (i + 1))
                        pe.wait_ge(s_o, g + 1)
                        for t in range(NT):
                            pe.wait_ge(s_c, g * NT + t + 1)
                            for j in range(TRI * t, TRI * t + TRI):
                                k = (NT * u + t) % 2, (j % TRI) * MW
                                mm = pe.matmul(psu[:, k[0], k[1]:k[1] + D + 1], OH[:, u, j, :], G[:, u, j, :],
                                               start=True, stop=True)
                            mm.then_inc(s_m, 1)
                            if terms and t == 1:
                                pe.wait_ge(s_ec, g + 1)
                                for n in range(4):
                                    mm = pe.matmul(pem[0:EP, n * 32:n * 32 + 32], at_t[:, n, 0:EP],
                                                   BD[:].rearrange("p e h -> p (e h)"), start=True, stop=True)
                                mm.then_inc(s_em, 1)

                    pe.sem_inc(s_m, 2 * NT)
                    done = E_STEPS // 2 if edge_terms else 0
                    pe.wait_ge(s_one, 1)
                    if edge_terms:
                        pe.sem_inc(s_et, 2)
                        pe.sem_inc(s_eo, 1)
                        with pe.Fori(0, done) as i:
                            for u in range(2):
                                group(i, u, True)
                    with pe.Fori(done, N_GRP // 2) as i:
                        for u in range(2):
                            group(i, u, False)

                @block.vector
                def _(dve):
                    def one_hot(g, u):
                        dve.wait_ge(s_m, g * NT + NT)
                        dve.tensor_tensor(OH[:, u], rowi[:, None, :].to_broadcast([P, J, P]),
                                          REL[:, bass.ds(g * J, J)][:, :, None].to_broadcast([P, J, P]),
                                          ALU.is_equal).then_inc(s_o, 1)

                    dve.memset(G[:, :, :, D:], 1.0).then_inc(s_one, 1)
                    dve.memset(ACC[:], 0.0).then_inc(s_one, 1)
                    dve.wait_ge(s_one, 2)
                    dve.sem_inc(s_c, 2)
                    dve.wait_ge(s_m, NT)
                    dve.tensor_tensor(OH[:, 0], rowi[:, None, :].to_broadcast([P, J, P]),
                                      REL[:, 0:J][:, :, None].to_broadcast([P, J, P]),
                                      ALU.is_equal).then_inc(s_o, 1)
                    with dve.Fori(0, N_GRP // 2) as i:
                        for u in range(2):
                            g = 2 * i + u
                            one_hot(g + 1, 1 - u)
                            c = Chain(dve, own, i, 2 * (J - NT))
                            c.n = u * (J - NT)
                            for j in range(J):
                                if j % 8 == 0:
                                    _, blk = nc.values_load_multi_w_load_instructions(
                                        BLK[0:1, bass.ds(g, 1), j:j + 8], engines=DVE_ONLY,
                                        min_val=0, max_val=NB - 1)
                                if j % TRI == 0:
                                    dve.wait_ge(s_m, g * NT + j // TRI + 1 + 2 * NT)
                                a = ACC[:, bass.ds(blk[j % 8], 1), 0:D + 1]
                                k = (NT * u + j // TRI) % 2, (j % TRI) * MW
                                add = dve.tensor_tensor(a, psu[:, k[0], k[1]:k[1] + D + 1][:, None, :], a, ALU.add)
                                if j % TRI == TRI - 1:
                                    add.then_inc(s_c, 1)
                                    dve.wait_ge(s_c, g * NT + j // TRI + 3)
                                else:
                                    c.link(add)
            return body

        stage(gather_sums(h_tab, True))

        def hidden(at, block):
            PAIR = 2
            NP2 = NB // PAIR
            s_a = sem("d_a", at)
            s_s = sem("d_s", at)
            s_t = sem("d_t", at)
            s_e = sem("d_e", at)
            s_p = sem("d_p", at)
            s_h = sem("d_h", at)
            s_o = sem("d_o", at)
            s_y = sem("d_y", at)
            s_b = sem("d_b", at)
            s_d = [sem(f"d_d{u}", at) for u in range(2)]
            s_r = sem("d_r", at)
            s_d = sem("d_d", at)
            s_f = sem("d_f", at)
            s_ag = sem("d_ag", at)
            s_at = sem("d_at", at)
            s_ac = sem("d_ac", at)
            own = sem("d_own", at)
            A2 = sb("A2", [P, 2, PAIR, D], F32, at)
            H2 = sb("H2", [P, 2, PAIR, D], F32, at)
            TT = sb("TT", [P, 2, 2 * PAIR * D], F32, at)
            HID = sb("HID", [P, 2, 2, PAIR * P], F32, at)
            Y2 = sb("Y2", [P, 2, PAIR, D], F32, at)
            CNT = sb("CNT", [P, NB], F32, at)
            b2all = sb("b2all", [P, D], F32, at)
            aer = sb("aer", [P, KC, P * HEADS], F32, at)
            pt = ps("pt", [P, 2, 512], at)
            ph = ps("ph", [P, 2, 512], at)
            po = ps("po", [P, 2, 512], at)
            ytab = y_tab.rearrange("(b p) f -> p b f", p=P)

            @block.sync
            def _(sp):
                sp.dma_start(b2all[:], b2.rearrange("(o f) -> o f", o=1).to_broadcast([P, D])).then_inc(s_r, 16)
                sp.sem_inc(s_f, 2)
                with sp.Fori(0, NP2 // 2) as i:
                    for u in range(2):
                        t = 2 * i + u
                        sp.wait_ge(s_y, t + 3)
                        sp.dma_start(ytab[:, bass.ds(t * PAIR, PAIR), :], Y2[:, u]).then_inc(s_d, 16)
                        sp.wait_ge(s_d, 16 * (t + 1))
                        sp.sem_inc(s_f, 1)

            @block.gpsimd
            def _(pool):
                pool.wait_ge(s_r, 16)
                with pool.Fori(0, NP2) as t:
                    hold(pool, s_s, t + 1)
                    pair = bass.ds(t * PAIR, PAIR)
                    pool.tensor_tensor(H[:, pair, 0:D], H[:, pair, 0:D],
                                       b2all[:, None, :].to_broadcast([P, PAIR, D]), ALU.add).then_inc(s_b, 1)
                flat = ae_tab.rearrange("(o e) -> o e", o=1)
                for c in range(KC):
                    pool.indirect_dma_start(aer[:, c, :], None, flat, bass.IndirectOffsetOnAxis(
                        ap=ek4i[:, c:c + 1], axis=1)).then_inc(s_ag, 16)

            @block.scalar
            def _(act):
                def stage_h(t, u):
                    act.copy(H2[:, u], H[:, bass.ds(t * PAIR, PAIR), 0:D]).then_inc(s_s, 1)

                def step(t, u, ahead=True, following=True):
                    if ahead:
                        hold(act, s_t, t + 1)
                        stage_h(t + 2, u)
                    if following:
                        act.wait_ge(s_t, t + 2)
                        act.wait_ge(s_p, t + 1)
                        act.copy(TT[:, 1 - u], pt[:, 1 - u]).then_inc(s_e, 1)
                    act.wait_ge(s_p, t + 2)
                    act.wait_ge(s_o, t + 1)
                    for m in range(2):
                        last = act.activation(HID[:, u, m], ph[:, u, m * 256:(m + 1) * 256], ACT.Relu,
                                              bias=b1c[:, m:m + 1])
                    last.then_inc(s_h, 1)

                stage_h(0, 0)
                stage_h(1, 1)
                act.wait_ge(s_t, 1)
                act.copy(TT[:, 0], pt[:, 0]).then_inc(s_e, 1)
                with act.Fori(0, NP2 // 2 - 1) as i:
                    for u in range(2):
                        step(2 * i + u, u)
                step(NP2 - 2, 0, ahead=False)
                step(NP2 - 1, 1, ahead=False, following=False)
                for n in range(KC):
                    act.wait_ge(s_at, n + 1)
                    act.copy(AE[:, :, n * P:(n + 1) * P], pt[:, n % 2].rearrange("p (h k) -> p h k", h=HEADS)
                             ).then_inc(s_ac, 1)

            @block.tensor
            def _(pe):
                def turn(t, u, fresh=False):
                    pe.wait_ge(s_a, t + 1)
                    pe.wait_ge(s_s, t + 1)
                    if not fresh:
                        pe.wait_ge(s_e, t - 1)
                    for n in range(PAIR):
                        pe.transpose(pt[:, u, n * P:n * P + P], A2[:, u, n], ident[:])
                        mm = pe.transpose(pt[:, u, (PAIR + n) * P:(PAIR + n + 1) * P], H2[:, u, n], ident[:])
                    mm.then_inc(s_t, 1)

                def first(t, u):
                    pe.wait_ge(s_e, t + 1)
                    pe.wait_ge(s_h, t)
                    for m in range(2):
                        o = ph[:, u, m * 256:(m + 1) * 256]
                        pe.matmul(o, W1T[:, 0, m * P:m * P + P], TT[:, u, 0:256], start=True, stop=False)
                        mm = pe.matmul(o, W1T[:, 1, m * P:m * P + P], TT[:, u, 256:512], start=False, stop=True)
                    mm.then_inc(s_p, 1)

                def second(t, u):
                    pe.wait_ge(s_h, t + 2)
                    pe.wait_ge(s_y, t + 1)
                    for n in range(PAIR):
                        for m in range(2):
                            mm = pe.matmul(po[:, u, n * 256:(n + 1) * 256], HID[:, u, m, n * P:n * P + P],
                                           W2T[:, m].rearrange("p l o -> p (l o)"), start=(m == 0), stop=(m == 1))
                    mm.then_inc(s_o, 1)

                pe.sem_inc(s_p, 1)
                pe.sem_inc(s_h, 1)
                pe.sem_inc(s_o, 2)
                turn(0, 0, fresh=True)
                turn(1, 1, fresh=True)
                first(0, 0)
                with pe.Fori(0, NP2 // 2 - 1) as i:
                    for u in range(2):
                        t = 2 * i + u
                        turn(t + 2, u)
                        first(t + 1, 1 - u)
                        second(t, u)
                first(NP2 - 1, 1)
                second(NP2 - 2, 0)
                second(NP2 - 1, 1)
                pe.wait_ge(s_ag, 16 * KC)
                for n in range(KC):
                    if n >= 2:
                        pe.wait_ge(s_ac, n - 1)
                    row = aer[:, n, :].rearrange("k (e h) -> k h e", h=HEADS)
                    for h in range(HEADS):
                        mm = pe.transpose(pt[:, n % 2, h * P:h * P + P], row[:, h], ident[:])
                    mm.then_inc(s_at, 1)

            @block.vector
            def _(dve):
                c = Chain(dve, own)
                c.link(dve.tensor_copy(CNT[:], ACC[:, :, D]))
                c.link(dve.tensor_scalar(RCNT[:], CNT[:], 1.0, None, ALU.max))
                c.link(dve.reciprocal(RCNT[:], RCNT[:]))
                c.link(dve.tensor_scalar(NOEDGE[:], CNT[:], 0.5, -BIG, ALU.is_lt, ALU.mult))

                def mean(t, u):
                    dve.tensor_tensor(A2[:, u], ACC[:, bass.ds(t * PAIR, PAIR), 0:D],
                                      RCNT[:, bass.ds(t * PAIR, PAIR)][:, :, None].to_broadcast([P, PAIR, D]),
                                      ALU.mult).then_inc(s_a, 1)

                def finish(t, u):
                    o = po[:, u].rearrange("p (n l o) -> p n l o", n=PAIR, l=2)
                    dve.wait_ge(s_o, t + 3)
                    hold(dve, s_f, t + 1)
                    dve.tensor_copy(Y2[:, u], o[:, :, 0])
                    dve.wait_ge(s_b, t + 1)
                    h = H[:, bass.ds(t * PAIR, PAIR), 0:D]
                    dve.tensor_tensor(h, o[:, :, 1], h, ALU.add).then_inc(s_y, 1)

                dve.sem_inc(s_y, 2)
                mean(0, 0)
                mean(1, 1)
                with dve.Fori(0, NP2 // 2 - 1) as i:
                    for u in range(2):
                        t = 2 * i + u
                        dve.wait_ge(s_t, t + 1)
                        mean(t + 2, u)
                        finish(t, u)
                finish(NP2 - 2, 0)
                finish(NP2 - 1, 1)

        stage(hidden)
        stage(gather_sums(y_tab, False))

        def second_norm(at, block):
            NQ = NB // QUAD
            s_v = sem("s_v", at)
            s_a = sem("s_a", at)
            s_h = sem("s_h", at)
            s_t = sem("s_t", at)
            s_e = sem("s_e", at)
            s_p = sem("s_p", at)
            s_x = sem("s_x", at)
            s_d = sem("s_d", at)
            own = sem("s_own", at)
            st = sb("st", [P, QUAD, 6], F32, at)
            mv = sb("mv", [P, QUAD, 2], F32, at)
            sd = sb("sd", [P, QUAD], F32, at)
            rs = sb("rs", [P, QUAD], F32, at)
            U = sb("U", [P, QUAD, D], F32, at)
            V = sb("V", [P, 2, QUAD, D], F32, at)
            HT = sb("HT", [P, 2, QUAD * P], F32, at)
            pt = ps("pt", [P, 2, 512], at)
            pw = ps("pw", [P, 2, 2, 512], at)
            WA = XW + HEADS
            tab = x_tab.rearrange("(b p) f -> p b f", p=P)

            @block.sync
            def _(sp):
                with sp.Fori(0, NQ) as i:
                    sp.wait_ge(s_x, i + 3)
                    quad = bass.ds(i * QUAD, QUAD)
                    sp.dma_start(tab[:, quad, :], H[:, quad, :]).then_inc(s_d, 16)
                sp.wait_ge(s_d, 16 * NQ)

            def quads(eng, step):
                with eng.Fori(0, NQ // 2) as i:
                    for u in range(2):
                        step(2 * i + u, u, i)
                step(NQ - 1, 0, NQ // 2)

            @block.scalar
            def _(act):
                def deviations(q, u, i):
                    for n in range(2):
                        act.wait_ge(s_v, 2 * q + n + 1)
                        act.activation(sd[:], mv[:, :, 1], ACT.Sqrt, bias=eps[:]).then_inc(s_a, 1)

                def products(q, u, i):
                    act.wait_ge(s_t, q + 1)
                    act.wait_ge(s_p, q + 1)
                    act.copy(HT[:, u], pt[:, u]).then_inc(s_e, 1)
                    act.wait_ge(s_p, q + 3)
                    act.nop(nofuse=True)
                    o = pw[:, u, :, 0:2 * WA].rearrange("p a (b w) -> p a b w", b=2)
                    for n in range(2):
                        act.copy(H[:, bass.ds(q * QUAD + 2 * n, 2), :], o[:, n, :, 0:XW])
                    for n in range(2):
                        last = act.copy(ADST[:, bass.ds(q * QUAD + 2 * n, 2), :], o[:, n, :, XW:])
                    last.then_inc(s_x, 1)

                def step(q, u, i):
                    deviations(q, u, i)
                    products(q, u, i)
                quads(act, step)

            @block.tensor
            def _(pe):
                def step(q, u, i):
                    pe.wait_ge(s_h, q + 1)
                    pe.wait_ge(s_x, q + 1)
                    for n in range(QUAD):
                        mm = pe.transpose(pt[:, u, n * P:n * P + P], V[:, u, n], ident[:])
                    mm.then_inc(s_t, 1)
                    pe.wait_ge(s_e, q + 1)
                    for n in range(QUAD):
                        mm = pe.matmul(pw[:, u, n // 2, (n % 2) * WA:(n % 2 + 1) * WA], HT[:, u, n * P:n * P + P],
                                       WX[:], start=True, stop=True)
                    mm.then_inc(s_p, 1)
                pe.sem_inc(s_p, 2)
                pe.sem_inc(s_x, 2)
                quads(pe, step)

            @block.vector
            def _(dve):
                def step(q, u, i):
                    c = Chain(dve, own, q, 12)
                    quad = bass.ds(q * QUAD, QUAD)
                    wide = [P, QUAD, D]

                    def norm(n, t, blocks):
                        for b in range(QUAD):
                            last = dve.bn_stats(st[:, b, :], blocks(b))
                        c.link(last, alone=True)
                        for b in range(QUAD):
                            last = dve.bn_aggr(mv[:, b, :], st[:, b, :])
                        last.then_inc(s_v, 1)
                        dve.wait_ge(s_v, 2 * q + n + 1)
                        c.link(dve.tensor_tensor(t, blocks(None), mv[:, :, 0:1].to_broadcast(wide), ALU.subtract))
                        dve.wait_ge(s_a, 2 * q + n + 1)
                        c.link(dve.reciprocal(rs[:], sd[:]))

                    r = rs[:, :, None].to_broadcast(wide)
                    c.link(dve.tensor_tensor(U[:], ACC[:, quad, 0:D], RCNT[:, quad][:, :, None].to_broadcast(wide),
                                             ALU.mult))
                    c.link(dve.tensor_tensor(U[:], U[:], H[:, quad, 0:D], ALU.add), alone=True)
                    norm(0, U[:], lambda b: U[:] if b is None else U[:, b])
                    c.link(dve.tensor_tensor(U[:], U[:], r, ALU.mult))
                    c.link(dve.tensor_tensor(U[:], U[:], gam[:, None, :].to_broadcast(wide), ALU.mult))
                    c.link(dve.tensor_tensor(U[:], U[:], bet[:, None, :].to_broadcast(wide), ALU.add))
                    c.link(dve.tensor_tensor(X[:, quad, :], X[:, quad, :], U[:], ALU.add), alone=True)
                    norm(1, U[:], lambda b: X[:, quad] if b is None else X[:, bass.ds(q * QUAD + b, 1), :])
                    dve.wait_ge(s_x, q + 1)
                    dve.scalar_tensor_tensor(V[:, u], U[:], 0.0, r, ALU.max, ALU.mult).then_inc(s_h, 1)
                    dve.wait_ge(s_h, q + 1)
                    c.end()
                quads(dve, step)

        stage(second_norm)

        def attention(at, block):
            R = J * HEADS
            s_i = sem("a_i", at)
            s_g = [sem(f"a_g{u}", at) for u in range(2)]
            s_o = sem("a_o", at)
            s_m = sem("a_m", at)
            s_c = sem("a_c", at)
            s_kb = sem("a_kb", at)
            s_kt = sem("a_kt", at)
            s_kc = sem("a_kc", at)
            s_mk = sem("a_mk", at)
            s_tr = sem("a_tr", at)
            s_te = sem("a_te", at)
            s_x = sem("a_x", at)
            s_l = sem("a_l", at)
            s_lt = sem("a_lt", at)
            s_cm = sem("a_cm", at)
            s_row = sem("a_row", at)
            s_cc = sem("a_cc", at)
            s_col = sem("a_col", at)
            s_r = sem("a_r", at)
            s_rt = sem("a_rt", at)
            s_fd = sem("a_fd", at)
            s_f = sem("a_f", at)
            s_fm = sem("a_fm", at)
            s_fx = sem("a_fx", at)
            s_dl = sem("a_dl", at)
            s_p = sem("a_p", at)
            s_ms = sem("a_ms", at)
            s_mp = sem("a_mp", at)
            s_one = sem("a_one", at)
            own = sem("a_own", at)
            idx = sb("idx", [P, 2, J], I32, at)
            G = sb("G", [P, 2, J, XW], F32, at)
            OH = sb("OH", [P, 2, J, P], F32, at)
            OHT = sb("OHT", [P, J, P], F32, at)
            MSG = sb("MSG", [P, J, MW], F32, at)
            KB = sb("KB", [P, HEADS, J], F32, at)
            L = sb("L", [P, HEADS, J], F32, at)
            PR = sb("PR", [P, HEADS, J], F32, at)
            KT = sb("KT", [R, P], F32, at)
            MS = sb("MS", [R, P + 1], F32, at)
            FS = sb("FS", [R, P], F32, at)
            LS = sb("LS", [R, P], F32, at)
            FW = sb("FW", [R, P], F32, at)
            CM = sb("CM", [R, P], F32, at)
            rows = sb("rows", [1, 2, HEADS, J], F32, at)
            wa = sb("wa", [1, HEADS, J], F32, at)
            wb = sb("wb", [1, HEADS, J], F32, at)
            cin = sb("cin", [1, HEADS, J], F32, at)
            cbk = sb("cbk", [1, HEADS, J], F32, at)
            aa = sb("aa", [1, HEADS, J], F32, at)
            ab = sb("ab", [1, HEADS, J], F32, at)
            last_m = sb("last_m", [1, HEADS], F32, at)
            f0 = sb("f0", [1, HEADS], F32, at)
            f1 = sb("f1", [1, HEADS], F32, at)
            pt = ps("pt", [P, 2, 512], at)
            pu = ps("pu", [P, 2, 512], at)
            px = ps("px", [P, 512], at)
            pl = ps("pl", [P, 512], at)
            pk = ps("pk", [P, 512], at)
            pc = ps("pc", [P, 512], at)
            px_l = px[:, 0:R].rearrange("p (h j) -> p h j", h=HEADS)
            pf = pl[:, 256:256 + HEADS]
            NF = -(-J // 4)

            def jh(t):
                return t.rearrange("p h j -> p j h")

            @block.gpsimd
            def _(pool):
                with pool.Fori(0, N_GRP // 2) as i:
                    for u in range(2):
                        g = 2 * i + u
                        pool.wait_ge(s_i, g + 1)
                        hold(pool, s_m, g * NT + NT)
                        for j in range(J):
                            pool.indirect_dma_start(
                                G[:, u, j, :], None, x_tab, bass.IndirectOffsetOnAxis(
                                    ap=idx[:, u, j:j + 1], axis=0)).then_inc(s_g[u], 16)

            @block.scalar
            def _(act):
                def ahead(g, u):
                    act.copy(KB[:], KEY[:, bass.ds(g * J, J)][:, None, :].to_broadcast([P, HEADS, J])
                             ).then_inc(s_kb, 1)
                    act.wait_ge(s_kt, g + 1)
                    act.wait_ge(s_mk, g + 1)
                    act.copy(KT[:], pk[0:R, 0:P]).then_inc(s_kc, 1)
                    act.wait_ge(s_x, g + 1)
                    for n in range(NF):
                        w = min(4, J - 4 * n)
                        act.wait_ge(s_tr, g * NF + n + 1)
                        act.copy(OHT[:, 4 * n:4 * n + w, :].rearrange("p a b -> p (a b)"), pt[:, n % 2, 0:w * P]
                                 ).then_inc(s_te, 1)

                act.copy(idx[:, 0, :], SRC[:, 0:J]).then_inc(s_i, 1)
                ahead(0, 0)
                with act.Fori(0, N_GRP // 2) as i:
                    for u in range(2):
                        g = 2 * i + u
                        act.wait_ge(s_m, g * NT + 2 * NT)
                        act.copy(idx[:, 1 - u, :], SRC[:, bass.ds(g * J + J, J)]).then_inc(s_i, 1)
                        act.copy(MSG[:, :, XW + HEADS:], jh(AE[:, :, bass.ds(g * J, J)]))
                        act.wait_ge(s_fd, g + 1)
                        act.activation(f1[:], f0[:], ACT.Exp).then_inc(s_f, 1)
                        act.wait_ge(s_dl, g + 1)
                        act.activation(PR[:], L[:], ACT.Exp).then_inc(s_p, 1)
                        act.wait_ge(s_p, g + 1)
                        act.copy(MSG[:, :, C_HEAD:XW:HW], jh(PR[:])).then_inc(s_mp, 1)
                        ahead(g + 1, 1 - u)

            @block.tensor
            def _(pe):
                def ahead(g, u):
                    hold(pe, s_kb, g + 1)
                    pe.transpose(pk[0:R, 0:P], KB[:].rearrange("p h j -> p (h j)"), ident[:]).then_inc(s_kt, 1)
                    pe.wait_ge(s_o, g + 1)
                    for n in range(NF):
                        pe.wait_ge(s_te, g * NF + n + 1)
                        for j in range(4 * n, min(4 * n + 4, J)):
                            mm = pe.transpose(pt[:, n % 2, (j % 4) * P:(j % 4 + 1) * P], OH[:, u, j, :], ident[:])
                        mm.then_inc(s_tr, 1)
                    for j in range(J):
                        if j % 8 == 0:
                            _, blk = nc.values_load_multi_w_load_instructions(
                                BLK[0:1, bass.ds(g, 1), j:j + 8], engines=(mybir.EngineType.PE,),
                                min_val=0, max_val=NB - 1)
                        if j % 4 == 0:
                            pe.wait_ge(s_te, g * NF + j // 4 + 3)
                        mm = pe.matmul(px_l[:, :, j], OHT[:, j, :],
                                       ADST[:, bass.ds(blk[j % 8], 1), :].rearrange("p a h -> p (a h)"),
                                       start=True, stop=True)
                    mm.then_inc(s_x, 1)

                pe.sem_inc(s_m, 2 * NT)
                pe.sem_inc(s_x, 1)
                ahead(0, 0)
                with pe.Fori(0, N_GRP // 2) as i:
                    for u in range(2):
                        g = 2 * i + u
                        hold(pe, s_l, g + 1)
                        pe.transpose(pl[0:R, 0:P], L[:].rearrange("p h j -> p (h j)"), ident[:]).then_inc(s_lt, 1)
                        hold(pe, s_cm, g + 1)
                        pe.matmul(pc[0:1, 0:R], CM[:, 0:1], ident[0:R, 0:R], start=True, stop=True)
                        pe.matmul(pc[0:1, R:2 * R], CM[:, P - 1:P], ident[0:R, 0:R],
                                  start=True, stop=True).then_inc(s_row, 1)
                        pe.wait_ge(s_cc, g + 1)
                        pe.matmul(pc[0:R, 128:129], cin[:].rearrange("o h j -> o (h j)"), ones[0:1, 0:1],
                                  start=True, stop=True)
                        pe.matmul(pc[0:R, 129:130], cbk[:].rearrange("o h j -> o (h j)"), ones[0:1, 0:1],
                                  start=True, stop=True).then_inc(s_col, 1)
                        hold(pe, s_r, g + 1)
                        pe.transpose(pc[:, 192:192 + R], CM[:], ident[0:R, 0:R]).then_inc(s_rt, 1)
                        pe.wait_ge(s_fm, g + 1)
                        pe.matmul(pf, OH[0:1, u, 0, :], f1[:], start=True, stop=True).then_inc(s_fx, 1)
                        ahead(g + 1, 1 - u)
                        pe.wait_ge(s_ms, g + 1)
                        pe.wait_ge(s_mp, g + 1)
                        for t in range(NT):
                            pe.wait_ge(s_c, g * NT + t + 1)
                            for j in range(TRI * t, TRI * t + TRI):
                                k = (NT * u + t) % 2, (j % TRI) * MW
                                mm = pe.matmul(pu[:, k[0], k[1]:k[1] + MW], OH[:, u, j, :], MSG[:, j, :],
                                               start=True, stop=True)
                            mm.then_inc(s_m, 1)

            @block.vector
            def _(dve):
                def one_hot(g, u):
                    dve.tensor_tensor(OH[:, u], rowi[:, None, :].to_broadcast([P, J, P]),
                                      REL[:, bass.ds(g * J, J)][:, :, None].to_broadcast([P, J, P]),
                                      ALU.is_equal).then_inc(s_o, 1)

                c0 = Chain(dve, s_one)
                dve.memset(MS[:], -BIG)
                dve.memset(last_m[:], -BIG)
                dve.memset(aa[:], -BIG)
                dve.memset(ab[:], -BIG)
                dve.memset(wb[:], -BIG)
                c0.link(dve.memset(ACC[:], 0.0))
                dve.sem_inc(s_c, 2)
                dve.sem_inc(s_te, 2)
                dve.sem_inc(s_mk, 1)
                one_hot(0, 0)
                n_own = 11 + J - NT
                with dve.Fori(0, N_GRP // 2) as i:
                    for u in range(2):
                        g = 2 * i + u
                        c = Chain(dve, own, i, 2 * n_own)
                        c.n = u * n_own
                        dve.wait_ge(s_m, g * NT + 2 * NT)
                        one_hot(g + 1, 1 - u)
                        dve.wait_ge(s_kc, g + 1)
                        dve.tensor_tensor(MS[:, 1:P], KT[:, 0:P - 1], KT[:, 1:P], ALU.subtract)
                        dve.tensor_scalar(FS[:], KT[:], KT[:, 0:1], -1.0, ALU.subtract, ALU.mult)
                        dve.tensor_scalar(LS[:], KT[:], KT[:, P - 1:P], None, ALU.subtract).then_inc(s_mk, 1)
                        dve.wait_ge(s_g[u], 16 * J * (i + 1))
                        a_src = G[:, u, :, C_HEAD:XW:HW].rearrange("p j h -> p h j")
                        c.link(dve.tensor_tensor(L[:], a_src, AE[:, :, bass.ds(g * J, J)], ALU.add))
                        dve.wait_ge(s_x, g + 2)
                        c.link(dve.tensor_tensor(L[:], L[:], px_l, ALU.add))
                        dve.scalar_tensor_tensor(L[:], L[:], SLOPE, L[:], ALU.mult, ALU.max).then_inc(s_l, 1)
                        dve.wait_ge(s_lt, g + 1)
                        c.link(dve.tensor_tensor_scan(FW[:], MS[:, 0:P], pl[0:R, 0:P], -BIG, ALU.add, ALU.max))
                        dve.tensor_tensor_scan(CM[:, ::-1], MS[:, P:0:-1], FW[:, ::-1], -BIG,
                                               ALU.add, ALU.max).then_inc(s_cm, 1)
                        dve.tensor_tensor(aa[:, :, 1:], WHOLE[:, bass.ds(g * J, J - 1)][:, None, :].to_broadcast([1, HEADS, J - 1]),
                                          LINK[:, bass.ds(g * J + 1, J - 1)][:, None, :].to_broadcast([1, HEADS, J - 1]), ALU.add)
                        dve.tensor_tensor(ab[:, :, 0:J - 1], WHOLE[:, bass.ds(g * J + 1, J - 1)][:, None, :].to_broadcast([1, HEADS, J - 1]),
                                          LINK[:, bass.ds(g * J + 1, J - 1)][:, None, :].to_broadcast([1, HEADS, J - 1]), ALU.add)
                        c.link(dve.tensor_tensor(wa[:, :, 0:1], last_m[:, :, None],
                                                 LINK[:, bass.ds(g * J, 1)][:, None, :].to_broadcast([1, HEADS, 1]), ALU.add))
                        dve.wait_ge(s_row, g + 1)
                        c.link(dve.tensor_copy(rows[:].rearrange("o a h j -> o (a h j)"), pc[0:1, 0:2 * R]))
                        dve.tensor_tensor(wa[:, :, 1:], rows[:, 1, :, 0:J - 1],
                                          LINK[:, bass.ds(g * J + 1, J - 1)][:, None, :].to_broadcast([1, HEADS, J - 1]), ALU.add)
                        c.link(dve.tensor_tensor(wb[:, :, 0:J - 1], rows[:, 0, :, 1:],
                                                 LINK[:, bass.ds(g * J + 1, J - 1)][:, None, :].to_broadcast([1, HEADS, J - 1]), ALU.add))
                        flat = "o h j -> o (h j)"
                        dve.tensor_tensor_scan(cin[:].rearrange(flat), aa[:].rearrange(flat), wa[:].rearrange(flat),
                                               -BIG, ALU.add, ALU.max)
                        dve.tensor_tensor_scan(cbk[:].rearrange(flat)[:, ::-1], ab[:].rearrange(flat)[:, ::-1],
                                               wb[:].rearrange(flat)[:, ::-1], -BIG, ALU.add, ALU.max).then_inc(s_cc, 1)
                        dve.wait_ge(s_cc, g + 1)
                        dve.scalar_tensor_tensor(last_m[:], cin[:, :, J - 1], WHOLE[:, bass.ds(g * J + J - 1, 1)],
                                                 rows[:, 1, :, J - 1], ALU.add, ALU.max)
                        c.link(dve.scalar_tensor_tensor(f0[:], cbk[:, :, 0], WHOLE[:, bass.ds(g * J, 1)],
                                                        rows[:, 0, :, 0], ALU.add, ALU.max))
                        c.link(dve.tensor_tensor(f0[:], f0[:], cin[:, :, 0], ALU.max))
                        dve.tensor_tensor(f0[:], cin[:, :, 0], f0[:], ALU.subtract).then_inc(s_fd, 1)
                        dve.wait_ge(s_col, g + 1)
                        c.link(dve.scalar_tensor_tensor(CM[:], FS[:], pc[0:R, 128:129], CM[:], ALU.add, ALU.max))
                        dve.scalar_tensor_tensor(CM[:], LS[:], pc[0:R, 129:130], CM[:], ALU.add, ALU.max).then_inc(s_r, 1)
                        dve.wait_ge(s_f, g + 1)
                        dve.tensor_scalar(f1[:], f1[:], -1.0, None, ALU.add).then_inc(s_fm, 1)
                        dve.wait_ge(s_rt, g + 1)
                        pm = pc[:, 192:192 + R].rearrange("p (h j) -> p h j", h=HEADS)
                        dve.tensor_tensor(L[:], L[:], pm, ALU.subtract).then_inc(s_dl, 1)
                        c.link(dve.tensor_tensor(MSG[:, :, XW:XW + HEADS], jh(pm),
                                                 LAST[:, bass.ds(g * J, J)][:, :, None].to_broadcast([P, J, HEADS]),
                                                 ALU.mult))
                        dve.wait_ge(s_p, g + 1)
                        x_l = "p j (h c) -> p j h c"
                        dve.tensor_tensor(MSG[:, :, 0:XW].rearrange(x_l, h=HEADS)[:, :, :, 0:C_HEAD],
                                          G[:, u].rearrange(x_l, h=HEADS)[:, :, :, 0:C_HEAD],
                                          jh(PR[:])[:, :, :, None].to_broadcast([P, J, HEADS, C_HEAD]),
                                          ALU.mult).then_inc(s_ms, 1)
                        for j in range(J):
                            if j % 8 == 0:
                                _, blk = nc.values_load_multi_w_load_instructions(
                                    BLK[0:1, bass.ds(g, 1), j:j + 8], engines=DVE_ONLY,
                                    min_val=0, max_val=NB - 1)
                            if j == 0:
                                dve.wait_ge(s_fx, g + 1)
                                a = ACC[:, bass.ds(blk[0], 1), 0:XW].rearrange("p a (h c) -> p (a h) c", h=HEADS)
                                c.link(dve.scalar_tensor_tensor(a, pf[:, :, None].to_broadcast([P, HEADS, HW]), 1.0, a,
                                                                ALU.add, ALU.mult))
                            if j % TRI == 0:
                                dve.wait_ge(s_m, g * NT + j // TRI + 1 + 2 * NT)
                            a = ACC[:, bass.ds(blk[j % 8], 1), :]
                            k = (NT * u + j // TRI) % 2, (j % TRI) * MW
                            add = dve.tensor_tensor(a, pu[:, k[0], k[1]:k[1] + MW][:, None, :], a, ALU.add)
                            if j % TRI == TRI - 1:
                                add.then_inc(s_c, 1)
                                dve.wait_ge(s_c, g * NT + j // TRI + 3)
                            else:
                                c.link(add)
                        assert c.n == (u + 1) * n_own
        stage(attention)

        def finish(at, block):
            NQ = NB // QUAD
            own = sem("f_own", at)
            s_d = sem("f_d", at)
            s_m = sem("f_m", at)
            s_e = sem("f_e", at)
            s_o = sem("f_o", at)
            s_t = sem("f_t", at)
            shape = [P, NB, HEADS]
            sl = sb("sl", shape, F32, at)
            mr = sb("mr", shape, F32, at)
            mx = sb("mx", shape, F32, at)
            de = sb("de", [P, 2, NB, HEADS], F32, at)
            ex = sb("ex", [P, 2, NB, HEADS], F32, at)
            A = sb("A", [P, QUAD, D], F32, at)
            B = sb("B", [P, QUAD, D], F32, at)
            Hh = H[:].rearrange("p b (h c) -> p b h c", h=HEADS)
            Ah = ACC[:, :, 0:XW].rearrange("p b (h c) -> p b h c", h=HEADS)

            @block.scalar
            def _(act):
                act.wait_ge(s_m, 1)
                act.activation(ex[:], de[:], ACT.Exp).then_inc(s_e, 1)

            @block.vector
            def _(dve):
                c = Chain(dve, s_o)
                wide = RCNT[:, :, None].to_broadcast(shape)
                c.link(dve.tensor_tensor(sl[:], ACC[:, :, XW + HEADS:], wide, ALU.mult))
                c.link(dve.tensor_tensor(sl[:], sl[:], Hh[:, :, :, C_HEAD], ALU.add))
                c.link(dve.tensor_tensor(sl[:], sl[:], ADST[:], ALU.add))
                c.link(dve.scalar_tensor_tensor(sl[:], sl[:], SLOPE, sl[:], ALU.mult, ALU.max))
                c.link(dve.tensor_tensor(mr[:], ACC[:, :, XW:XW + HEADS], NOEDGE[:, :, None].to_broadcast(shape), ALU.add))
                c.link(dve.tensor_tensor(mx[:], mr[:], sl[:], ALU.max))
                dve.tensor_tensor(de[:, 0], mr[:], mx[:], ALU.subtract)
                dve.tensor_tensor(de[:, 1], sl[:], mx[:], ALU.subtract).then_inc(s_m, 1)
                dve.wait_ge(s_e, 1)
                c.link(dve.tensor_tensor(mx[:], Ah[:, :, :, C_HEAD], ex[:, 0], ALU.mult))
                c.link(dve.tensor_tensor(mx[:], mx[:], ex[:, 1], ALU.add))
                c.link(dve.reciprocal(mx[:], mx[:]))
                dve.tensor_tensor(ex[:, 0], ex[:, 0], mx[:], ALU.mult)
                c.link(dve.tensor_tensor(ex[:, 1], ex[:, 1], mx[:], ALU.mult), alone=True)
                with dve.Fori(0, NQ) as i:
                    c = Chain(dve, own, i, 4)
                    quad = bass.ds(i * QUAD, QUAD)

                    def by(n):
                        return ex[:, n, quad, :][:, :, :, None].to_broadcast([P, QUAD, HEADS, C_HEAD])

                    def heads(t):
                        return t.rearrange("p b (h c) -> p b h c", h=HEADS)
                    dve.tensor_tensor(heads(A[:]), Ah[:, quad, :, 0:C_HEAD], by(0), ALU.mult)
                    c.link(dve.tensor_tensor(heads(B[:]), Hh[:, quad, :, 0:C_HEAD], by(1), ALU.mult))
                    c.link(dve.tensor_tensor(A[:], A[:], B[:], ALU.add))
                    c.link(dve.tensor_tensor(A[:], A[:], bia[:, None, :].to_broadcast([P, QUAD, D]), ALU.add))
                    c.link(dve.tensor_tensor(X[:, quad, :], X[:, quad, :], A[:], ALU.add))
                    dve.sem_inc(s_d, 1)
                    c.end()

            @block.sync
            def _(sp):
                full = N_BLK - 1
                o = out[0:full * P].rearrange("(b p) f -> p b f", p=P)
                with sp.Fori(0, full // QUAD) as i:
                    sp.wait_ge(s_d, i + 1)
                    quad = bass.ds(i * QUAD, QUAD)
                    sp.dma_start(o[:, quad, :], X[:, quad, :]).then_inc(s_t, 16)
                sp.wait_ge(s_d, NQ)
                sp.dma_start(out[full * P:, :], X[0:TAIL, full, :]).then_inc(s_t, 16)
                sp.wait_ge(s_t, 16 * (full // QUAD + 1))

        stage(finish)
def debug_out(nc, stage, sem, out, dbg, *ts):
    def body(at, block):
        s = sem("dbg", at)
        @block.sync
        def _(sp):
            for d, t in zip(dbg, ts):
                sp.dma_start(d, t).then_inc(s, 16)
            sp.wait_ge(s, 16*len(ts))
    stage(body)


_INS = ["x", "src", "dst", "edge_attr_16", "L0_gnn_W1l", "L0_gnn_W1r", "L0_gnn_b1", "L0_gnn_W2l", "L0_gnn_W2r",
        "L0_gnn_b2", "L0_gnn_gamma", "L0_gnn_beta", "L1_gnn_W", "L1_gnn_W_edge", "L1_gnn_att_src",
        "L1_gnn_att_dst", "L1_gnn_att_edge", "L1_gnn_bias"]


def kernel(**inputs):
    import concourse.bacc as bacc
    from concourse.bass_utils import run_bass_kernel_spmd as run

    nc = bacc.Bacc("TRN2", target_bir_lowering=False, num_devices=1)
    arrays, args = {}, []
    for name in _INS:
        a = np.ascontiguousarray(inputs[name])
        arrays["in_" + name] = a
        args.append(nc.dram_tensor("in_" + name, a.shape, mybir.dt.from_np(a.dtype), kind="ExternalInput").ap())
    result = nc.dram_tensor("out", (N_NODES, D), F32, kind="ExternalOutput").ap()
    DBG = False
    shapes = [(P, NB, D), (P, NB, XW), (P, NB, HEADS)]
    dbg = [nc.dram_tensor(f"dbg{i}", sh, F32, kind="ExternalOutput").ap() for i, sh in enumerate(shapes)] if DBG else None
    build(nc, *args, result, dbg, 2)
    r = run(nc, [arrays], core_ids=[0])
    if DBG:
        return tuple(r.results[0][f"dbg{i}"] for i in range(len(shapes)))
    return r.results[0]["out"]
```

```python
from contextlib import ExitStack

import concourse.bass as bass
import numpy as np
from concourse import mybir
from concourse.alu_op_type import AluOpType as ALU

F32 = mybir.dt.float32
I32 = mybir.dt.int32
BF16 = mybir.dt.bfloat16
I16 = mybir.dt.int16
ACT = mybir.ActivationFunctionType
AX = mybir.AxisListType
DVE_ONLY = (mybir.EngineType.DVE,)

P = 128
N_NODES, D = 6250, 128
N_EDGES, D_EDGE = 200000, 16
D_HID = 256
HEADS, C_HEAD = 4, 32
N_BLK = -(-N_NODES // P)
QUAD = 4
NB = -(-N_BLK // QUAD) * QUAD
TAIL = N_NODES - (N_BLK - 1) * P

J = 15
TRI = 3
NT = J // TRI
MAX_CHUNKS = (N_EDGES + N_BLK * (P - 1)) // P
N_GRP = 2 * -(-MAX_CHUNKS // (2 * J))
KC = -(-N_GRP * J // P)
NK = KC * P
assert NK >= (N_GRP + 1) * J
E_PAD = KC * P * P
SENTINEL = 16384

HW = C_HEAD + 1
XW = HEADS * HW
MW = XW + 2 * HEADS
BIG = float(2.0 ** 100)
EPS = 1e-5
SLOPE = 0.2

EP, ES = 125, 32
E_STEPS = N_EDGES // (EP * ES)
assert E_STEPS * EP * ES == N_EDGES and 2 * E_STEPS <= N_GRP


def hold(eng, semaphore, value):
    eng.wait_ge(semaphore, value)
    eng.nop(nofuse=True)


class Chain:

    def __init__(self, eng, semaphore, i=None, per=0):
        self.eng, self.semaphore, self.i, self.per, self.n = eng, semaphore, i, per, 0

    def count(self):
        return self.n if self.i is None else self.i * self.per + self.n

    def mark(self, ins):
        ins.then_inc(self.semaphore, 1)
        self.n += 1

    def join(self):
        self.eng.wait_ge(self.semaphore, self.count())

    def link(self, ins, alone=False):
        self.mark(ins)
        if alone:
            hold(self.eng, self.semaphore, self.count())
        else:
            self.join()

    def end(self):
        assert self.i is None or self.n == self.per, (self.n, self.per)


def build(nc, x, src, dst, edge_attr, W1l, W1r, b1, W2l, W2r, b2, gamma, beta,
          W, W_edge, att_src, att_dst, att_edge, bias, out, dbg=None, stop=99):
    with ExitStack() as top:
        stages = []

        def sb(name, shape, dt=F32, at=top):
            return at.enter_context(nc.sbuf_tensor(f"{name}_{len(stages)}", shape, dt))

        def ps(name, shape, at):
            return at.enter_context(nc.psum_tensor(f"{name}_{len(stages)}", shape, F32))

        def sem(name, at):
            return at.enter_context(nc.semaphore(f"{name}_{len(stages)}"))

        src_pad = nc.dram_tensor("src_pad", [E_PAD], I32).ap()
        dst_pad = nc.dram_tensor("dst_pad", [E_PAD], I32).ap()
        ae_tab = nc.dram_tensor("ae_tab", [N_EDGES * HEADS + 4 * P * HEADS], F32).ap()
        h_tab = nc.dram_tensor("h_tab", [NB * P, D], F32).ap()
        y_tab = nc.dram_tensor("y_tab", [NB * P, D], F32).ap()
        x_keep = nc.dram_tensor("x_keep", [P, NB, D], F32).ap()
        x_tab = nc.dram_tensor("x_tab", [NB * P, XW], F32).ap()

        RCNT = sb("RCNT", [P, NB])
        NOEDGE = sb("NOEDGE", [P, NB])
        ADST = sb("ADST", [P, NB, HEADS])
        SRC = sb("SRC", [P, NK], I16)
        REL = sb("REL", [P, NK], BF16)
        KEY = sb("KEY", [P, NK])
        LAST = sb("LAST", [P, NK], BF16)
        BLK = sb("BLK", [1, N_GRP + 2, 16], I16)
        LINK = sb("LINK", [1, NK], BF16)
        WHOLE = sb("WHOLE", [1, NK], BF16)
        OHB = sb("OHB", [P, NK], BF16)
        ek4i = sb("ek4i", [P, KC], I32)
        ident = sb("ident", [P, P])
        rowi = sb("rowi", [P, P])
        coli = sb("coli", [P, 1])
        ones = sb("ones", [P, P])
        W1T = sb("W1T", [P, 2, D_HID])
        W2T = sb("W2T", [P, 2, 2, D])
        WX = sb("WX", [P, XW + HEADS])
        BD = sb("BD", [P, 8, HEADS])
        b1c = sb("b1c", [P, 2])
        b2row = sb("b2row", [1, 2 * D])
        gam = sb("gam", [P, D])
        bet = sb("bet", [P, D])
        bia = sb("bia", [P, D])
        eps = sb("eps", [P, 1])

        def stage(body):
            stages.append(body.__name__)
            with ExitStack() as at, nc.Block() as block:
                body(at, block)

        def prepare(at, block):
            s_in = sem("p_in", at)
            s_w = sem("p_w", at)
            s_rows = sem("p_rows", at)
            s_io = sem("p_io", at)
            s_g1 = sem("p_g1", at)
            s_gs = sem("p_gs", at)
            s_gd = sem("p_gd", at)
            s_gn = sem("p_gn", at)
            s_d = sem("p_d", at)
            s_p = sem("p_p", at)
            s_kl = sem("p_kl", at)
            s_at = sem("p_at", at)
            s_pad = sem("p_pad", at)
            s_b = sem("p_b", at)
            s_e = sem("p_e", at)
            NTURN = -(-KC // 4)
            dstf = sb("dstf", [P, NK], F32, at)

            irow = sb("irow", [P, P], I32, at)
            icol = sb("icol", [P, 1], I32, at)
            kio = sb("kio", [P, NK], F32, at)
            kpc = sb("kpc", [P, KC], F32, at)
            padt = sb("padt", [P, P], I32, at)
            zero = sb("zero", [P, P], I32, at)
            rows = sb("rows", [P, KC, P], I32, at)
            rowsf = sb("rowsf", [P, KC, P], F32, at)
            srows = sb("srows", [P, KC, P], I32, at)
            nrows = sb("nrows", [P, KC, P], I32, at)
            first = sb("first", [P, KC], F32, at)
            thr = sb("thr", [P, N_BLK + 1], F32, at)
            tcol = sb("tcol", [P, 1], F32, at)
            cmp3 = sb("cmp3", [P, N_BLK + 1, KC], F32, at)
            cnt1 = sb("cnt1", [P, N_BLK + 1], F32, at)
            t1 = sb("t1", [P, 1], F32, at)
            t1i = sb("t1i", [P, 1], I32, at)
            brow = sb("brow", [P, P], I32, at)
            browf = sb("browf", [P, P], F32, at)
            bcmp = sb("bcmp", [P, P], F32, at)
            bcnt = sb("bcnt", [P, 1], F32, at)
            start = sb("start", [P, 1], F32, at)
            eq0 = sb("eq0", [P, P], F32, at)
            eqd = sb("eqd", [P, P], F32, at)
            equ = sb("equ", [P, P], F32, at)
            lt = sb("lt", [P, P], F32, at)
            nch = sb("nch", [P, 1], F32, at)
            nci = sb("nci", [P, 1], I32, at)
            q = sb("q", [P, 1], F32, at)
            dq = sb("dq", [P, 2], F32, at)
            GE = sb("GE", [P, NK], F32, at)
            BK = sb("BK", [P, NK], F32, at)
            ek = sb("ek", [P, KC], F32, at)
            eki = sb("eki", [P, KC], I32, at)
            ek1i = sb("ek1i", [P, KC], I32, at)
            KL = sb("KL", [1, NK], F32, at)
            wl = sb("wl", [P, 2, D], F32, at)
            wr = sb("wr", [P, 2, D], F32, at)
            w2l = sb("w2l", [P, D_HID], F32, at)
            w2r = sb("w2r", [P, D_HID], F32, at)
            wt = sb("wt", [P, D], F32, at)
            we = sb("we", [P, D], F32, at)
            ats = sb("ats", [P, D], F32, at)
            atd = sb("atd", [P, D], F32, at)
            ate = sb("ate", [P, D], F32, at)
            wm = sb("wm", [P, 3, D], F32, at)
            mr = sb("mr", [P, HEADS], F32, at)
            m8 = sb("m8", [P, 8], F32, at)
            pg = sb("pg", [P, 1], F32, at)
            pgi = sb("pgi", [P, 1], I32, at)
            psm = ps("psm", [P, 512], at)
            psb = ps("psb", [P, 4, 512], at)
            pst = ps("pst", [P, 2, 512], at)

            n_tail = E_PAD - N_EDGES
            tail_cols = 112
            assert n_tail % tail_cols == 0 and n_tail // tail_cols <= P
            tail_rows = n_tail // tail_cols

            @block.sync
            def _(sp):
                sp.dma_start(dst_pad[0:N_EDGES].rearrange("(a b) -> a b", a=400),
                             dst.rearrange("(a b) -> a b", a=400)).then_inc(s_in, 16)
                sp.dma_start(src_pad[0:N_EDGES].rearrange("(a b) -> a b", a=400),
                             src.rearrange("(a b) -> a b", a=400)).then_inc(s_in, 16)
                sp.wait_ge(s_pad, 2)
                sp.dma_start(dst_pad[N_EDGES:].rearrange("(a b) -> a b", b=tail_cols),
                             padt[0:tail_rows, 0:tail_cols]).then_inc(s_in, 16)
                sp.dma_start(src_pad[N_EDGES:].rearrange("(a b) -> a b", b=tail_cols),
                             zero[0:tail_rows, 0:tail_cols]).then_inc(s_in, 16)
                sp.wait_ge(s_in, 64)
                sp.dma_start(rows[:], dst_pad.rearrange("(c p e) -> p c e", p=P, e=P)).then_inc(s_rows, 16)
                sp.wait_ge(s_d, 14)
                sp.dma_start(KL[:], KEY[P - 1:P, :]).then_inc(s_kl, 16)
                sp.dma_start(ae_tab[N_EDGES * HEADS:].rearrange("(a b) -> a b", a=16),
                             zero[0:16, :].bitcast(F32)).then_inc(s_at, 16)
                sp.wait_ge(s_at, 16)

            @block.scalar
            def _(act):
                act.dma_start(wl[:], W1l.rearrange("(m p) f -> p m f", p=P)).then_inc(s_w, 16)
                act.dma_start(wr[:], W1r.rearrange("(m p) f -> p m f", p=P)).then_inc(s_w, 16)
                act.dma_start(w2l[:], W2l).then_inc(s_w, 16)
                act.dma_start(w2r[:], W2r).then_inc(s_w, 16)
                act.dma_start(wt[:], W).then_inc(s_w, 16)
                for r in range(8):
                    act.dma_start(we[16 * r:16 * r + 16, :], W_edge).then_inc(s_w, 16)
                for t, a in ((ats, att_src), (atd, att_dst), (ate, att_edge)):
                    row = a.rearrange("h c -> (h c)").rearrange("(o f) -> o f", o=1)
                    act.dma_start(t[:], row.to_broadcast([P, D])).then_inc(s_w, 16)
                for t, a in ((gam, gamma), (bet, beta), (bia, bias)):
                    act.dma_start(t[:], a.rearrange("(o f) -> o f", o=1).to_broadcast([P, D])).then_inc(s_w, 16)
                with nc.allow_non_contiguous_dma(reason="256 words"):
                    act.dma_start(b1c[:], b1.rearrange("(m p) -> p m", p=P)).then_inc(s_w, 16)
                act.wait_ge(s_b, 1)
                act.dma_start(b2row[:, D:], b2.rearrange("(o f) -> o f", o=1)).then_inc(s_w, 16)

            @block.gpsimd
            def _(pool):
                pool.memset(padt[:], SENTINEL).then_inc(s_pad, 1)
                pool.memset(zero[:], 0).then_inc(s_pad, 1)
                pool.iota(irow[:], pattern=[[1, P]], base=0, channel_multiplier=0).then_inc(s_io, 1)
                pool.iota(icol[:], pattern=[[0, 1]], base=0, channel_multiplier=1).then_inc(s_io, 1)
                pool.iota(kio[:], pattern=[[1, NK]], base=0, channel_multiplier=0,
                          allow_small_or_imprecise_dtypes=True).then_inc(s_io, 1)
                pool.iota(kpc[:], pattern=[[P * P, KC]], base=0, channel_multiplier=P,
                          allow_small_or_imprecise_dtypes=True).then_inc(s_io, 1)
                pool.wait_ge(s_d, 4)
                pool.indirect_dma_start(
                    brow[0:N_BLK + 1, :], None, dst_pad.rearrange("(r e) -> r e", e=P),
                    bass.IndirectOffsetOnAxis(ap=t1i[0:N_BLK + 1, :], axis=0)).then_inc(s_g1, 16)
                pool.wait_ge(s_d, 9)
                flat_s = src_pad.rearrange("(o e) -> o e", o=1)
                flat_d = dst_pad.rearrange("(o e) -> o e", o=1)
                for c in range(KC):
                    pool.indirect_dma_start(srows[:, c, :], None, flat_s, bass.IndirectOffsetOnAxis(
                        ap=eki[:, c:c + 1], axis=1)).then_inc(s_gs, 16)
                pool.wait_ge(s_d, 10)
                for c in range(KC):
                    pool.indirect_dma_start(rows[:, c, :], None, flat_d, bass.IndirectOffsetOnAxis(
                        ap=eki[:, c:c + 1], axis=1)).then_inc(s_gd, 16)
                for c in range(KC):
                    pool.indirect_dma_start(nrows[:, c, :], None, flat_d, bass.IndirectOffsetOnAxis(
                        ap=ek1i[:, c:c + 1], axis=1)).then_inc(s_gn, 16)

            @block.vector
            def _(dve):
                own = sem("p_own", at)
                n = [0]

                def link(ins):
                    n[0] += 1
                    ins.then_inc(own, 1)
                    dve.wait_ge(own, n[0])

                steps = [0]

                def step(ins=None):
                    steps[0] += 1
                    ins.then_inc(s_d, 1)
                    dve.wait_ge(s_d, steps[0])

                dve.memset(b2row[:], 0.0).then_inc(s_b, 1)
                dve.memset(dq[:], 1.0)
                dve.memset(eps[:], EPS)
                link(dve.memset(BLK[:], 0))
                step(dve.memset(ones[:], 1.0))
                dve.wait_ge(s_io, 4)
                dve.tensor_copy(rowi[:], irow[:])
                link(dve.tensor_copy(coli[:], icol[:]))
                dve.tensor_scalar(thr[:], rowi[:, 0:N_BLK + 1], float(P), None, ALU.mult)
                dve.tensor_scalar(tcol[:], coli[:], float(P), None, ALU.mult)
                dve.tensor_scalar(eqd[:], rowi[:], 1.0, coli[:], ALU.add, ALU.is_equal)
                dve.tensor_scalar(equ[:], rowi[:], -1.0, coli[:], ALU.add, ALU.is_equal)
                dve.tensor_scalar(lt[:], rowi[:], coli[:], None, ALU.is_gt)
                link(dve.tensor_scalar(ident[:], rowi[:], coli[:], None, ALU.is_equal))
                link(dve.tensor_tensor(eqd[:], eqd[:], ident[:], ALU.subtract))
                step(dve.tensor_tensor(equ[:], ident[:], equ[:], ALU.subtract))
                dve.wait_ge(s_rows, 16)
                link(dve.tensor_copy(first[:], rows[:, :, 0]))
                link(dve.tensor_tensor(
                    cmp3[:], first[:, None, :].to_broadcast([P, N_BLK + 1, KC]),
                    thr[:, :, None].to_broadcast([P, N_BLK + 1, KC]), ALU.is_lt))
                step(dve.tensor_reduce(cnt1[:], cmp3[:], AX.X, ALU.add))
                dve.wait_ge(s_p, 1)
                link(dve.tensor_scalar(t1[0:N_BLK + 1, :], psm[0:N_BLK + 1, 0:1], -1.0, 0.0, ALU.add, ALU.max))
                step(dve.tensor_copy(t1i[0:N_BLK + 1, :], t1[0:N_BLK + 1, :]))
                dve.wait_ge(s_g1, 16)
                link(dve.tensor_copy(browf[0:N_BLK + 1, :], brow[0:N_BLK + 1, :]))
                link(dve.tensor_scalar(bcmp[0:N_BLK + 1, :], browf[0:N_BLK + 1, :], tcol[0:N_BLK + 1, :],
                                       None, ALU.is_lt))
                link(dve.tensor_reduce(bcnt[0:N_BLK + 1, :], bcmp[0:N_BLK + 1, :], AX.X, ALU.add))
                step(dve.tensor_scalar(start[0:N_BLK + 1, :], t1[0:N_BLK + 1, :], float(P),
                                       bcnt[0:N_BLK + 1, :], ALU.mult, ALU.add))
                dve.wait_ge(s_p, 2)
                link(dve.tensor_scalar(nch[0:N_BLK, :], psm[0:N_BLK, 1:2], float(P - 1), None, ALU.add))
                link(dve.tensor_copy(nci[0:N_BLK, :], nch[0:N_BLK, :]))
                link(dve.tensor_scalar(nci[0:N_BLK, :], nci[0:N_BLK, :], 7, None, ALU.arith_shift_right))
                step(dve.tensor_copy(nch[0:N_BLK, :], nci[0:N_BLK, :]))
                dve.wait_ge(s_p, 3)
                link(dve.tensor_copy(nch[0:N_BLK, :], psm[0:N_BLK, 2:3]))
                link(dve.tensor_scalar(q[0:N_BLK, :], nch[0:N_BLK, :], -float(P), start[0:N_BLK, :],
                                       ALU.mult, ALU.add))
                step(dve.tensor_scalar(GE[0:N_BLK, :], kio[0:N_BLK, :], nch[0:N_BLK, :], None, ALU.is_ge))
                dve.wait_ge(s_p, 4)
                step(dve.tensor_copy(dq[0:N_BLK, 0:1], psm[0:N_BLK, 3:4]))
                dve.wait_ge(s_p, 5)
                link(dve.tensor_tensor(ek[:], kpc[:], psm[:, 4:4 + 2 * KC:2], ALU.add))
                link(dve.tensor_scalar(ek[:], ek[:], float(N_EDGES), None, ALU.min))
                link(dve.tensor_copy(eki[:], ek[:]))
                link(dve.tensor_scalar(ek4i[:], ek[:], float(HEADS), None, ALU.mult))
                step(dve.tensor_scalar(ek1i[:], ek[:], 1.0, None, ALU.add))
                dve.wait_ge(s_p, 6)
                step(dve.tensor_scalar(BK[:].rearrange("p (b k) -> p b k", b=4),
                                       psb[:, :, 0:NK // 4], -1.0, float(P), ALU.add, ALU.mult))
                dve.tensor_scalar(OHB[:], BK[:], tcol[:], None, ALU.is_equal)
                link(dve.tensor_scalar(BLK[:, 2:N_GRP + 2, 0:J], BK[0:1, 0:N_GRP * J].rearrange("o (g j) -> o g j", j=J),
                                       1.0 / P, None, ALU.mult))
                def turn(rows_i, s_rows_in, evacuate, s0):
                    dve.wait_ge(s_rows_in, 16 * KC)
                    link(dve.tensor_copy(rowsf[:], rows_i[:]))
                    step(dve.tensor_copy(rowsf[:, 0, :], rows_i[:, 0, :]))
                    for i in range(NTURN):
                        w = min(4, KC - 4 * i) * P
                        dve.wait_ge(s_p, s0 + i)
                        evacuate(slice(512 * i, 512 * i + w), pst[:, i % 2, 0:w]).then_inc(s_e, 1)
                    dve.wait_ge(s_e, s0 - 7 + NTURN)

                turn(srows, s_gs, lambda c, t: dve.tensor_copy(SRC[:, c], t), 7)
                step(dve.memset(bcnt[:], 0.0))
                turn(rows, s_gd, lambda c, t: dve.tensor_copy(dstf[:, c], t), 7 + NTURN)
                link(dve.tensor_tensor(KEY[:], dstf[:], BK[:], ALU.subtract))
                link(dve.tensor_scalar(KEY[:], KEY[:], P - 0.5, None, ALU.min))
                dve.tensor_copy(REL[:], KEY[:])
                link(dve.tensor_tensor(KEY[:], KEY[:], BK[:], ALU.add))
                step(dve.tensor_scalar(KEY[:], KEY[:], 2 * BIG, None, ALU.mult))
                dve.wait_ge(s_kl, 16)
                dve.memset(LINK[:, 0:1], -BIG)
                dve.tensor_tensor(LINK[:, 1:], KL[:, 0:NK - 1], KEY[0:1, 1:], ALU.subtract)
                link(dve.tensor_tensor(WHOLE[:], KEY[0:1, :], KL[:], ALU.subtract))
                turn(nrows, s_gn, lambda c, t: dve.tensor_tensor(
                    LAST[:, c], dstf[:, c], t, ALU.not_equal), 7 + 2 * NTURN)
                dve.wait_ge(s_w, 16 * 21)
                WXh = WX[:, 0:XW].rearrange("p (h c) -> p h c", h=HEADS)
                dve.tensor_copy(WXh[:, :, 0:C_HEAD], wt[:].rearrange("p (h c) -> p h c", h=HEADS))
                dve.tensor_tensor(wm[:, 0, :], wt[:], ats[:], ALU.mult)
                dve.tensor_tensor(wm[:, 1, :], wt[:], atd[:], ALU.mult)
                link(dve.tensor_tensor(wm[:, 2, :], we[:], ate[:], ALU.mult))
                wmh = wm[:].rearrange("p t (h c) -> p t h c", h=HEADS)
                dve.tensor_reduce(WXh[:, :, C_HEAD], wmh[:, 0], AX.X, ALU.add)
                dve.tensor_reduce(WX[:, XW:], wmh[:, 1], AX.X, ALU.add)
                dve.tensor_reduce(mr[:], wmh[:, 2], AX.X, ALU.add)
                link(dve.tensor_scalar(pgi[:], icol[:], 4, None, ALU.arith_shift_right))
                link(dve.tensor_copy(pg[:], pgi[:]))
                link(dve.tensor_scalar(m8[:], rowi[:, 0:8], pg[:], None, ALU.is_equal))
                link(dve.tensor_tensor(BD[:], m8[:, :, None].to_broadcast([P, 8, HEADS]),
                                       mr[:, None, :].to_broadcast([P, 8, HEADS]), ALU.mult))
                dve.wait_ge(s_p, 7 + 3 * NTURN)
                link(dve.tensor_copy(W1T[:].rearrange("p a b -> p (a b)"), psb[:, 0, :]))
                link(dve.tensor_copy(W2T[:].rearrange("p m l o -> p (m l o)"), psb[:, 1, :]))

            @block.tensor
            def _(pe):
                pe.wait_ge(s_d, 3)
                pe.matmul(psm[0:N_BLK + 1, 0:1], cnt1[:], ones[:, 0:1], start=True, stop=True).then_inc(s_p, 1)
                pe.wait_ge(s_d, 5)
                pe.matmul(psm[0:N_BLK, 1:2], eqd[0:N_BLK + 1, 0:N_BLK], start[0:N_BLK + 1, :],
                          start=True, stop=True).then_inc(s_p, 1)
                pe.wait_ge(s_d, 6)
                pe.matmul(psm[0:N_BLK, 2:3], lt[0:N_BLK, 0:N_BLK], nch[0:N_BLK, :],
                          start=True, stop=True).then_inc(s_p, 1)
                pe.wait_ge(s_d, 7)
                pe.matmul(psm[0:N_BLK, 3:4], equ[0:N_BLK, 0:N_BLK], q[0:N_BLK, :],
                          start=True, stop=True).then_inc(s_p, 1)
                pe.wait_ge(s_d, 8)
                for c in range(KC):
                    mm = pe.matmul(psm[:, 4 + 2 * c:6 + 2 * c], GE[0:N_BLK, c * P:(c + 1) * P], dq[0:N_BLK, :],
                                   start=True, stop=True)
                mm.then_inc(s_p, 1)
                for c in range(4):
                    mm = pe.matmul(psb[:, c, 0:NK // 4], ones[0:N_BLK, :], GE[0:N_BLK, c * NK // 4:(c + 1) * NK // 4],
                                   start=True, stop=True)
                mm.then_inc(s_p, 1)
                for t, s in enumerate((11, 13, 15)):
                    pe.wait_ge(s_d, s)
                    for i in range(NTURN):
                        if t * NTURN + i >= 2:
                            pe.wait_ge(s_e, t * NTURN + i - 1)
                        for c in range(4 * i, min(4 * i + 4, KC)):
                            mm = pe.transpose(pst[:, i % 2, (c % 4) * P:(c % 4) * P + P], rowsf[:, c, :], ident[:])
                        mm.then_inc(s_p, 1)
                pe.wait_ge(s_w, 16 * 21)
                pe.wait_ge(s_d, 10)
                for m in range(2):
                    pe.transpose(psb[:, 0, m * P:m * P + P], wl[:, m, :], ident[:])
                    pe.transpose(psb[:, 0, (2 + m) * P:(3 + m) * P], wr[:, m, :], ident[:])
                    pe.transpose(psb[:, 1, 2 * m * P:(2 * m + 1) * P], w2l[:, m * P:m * P + P], ident[:])
                    mm = pe.transpose(psb[:, 1, (2 * m + 1) * P:(2 * m + 2) * P], w2r[:, m * P:m * P + P], ident[:])
                mm.then_inc(s_p, 1)

        stage(prepare)
        ACC = sb("ACC", [P, NB, MW])
        AE = sb("AE", [P, HEADS, NK])
        XS = ExitStack()
        H = sb("H", [P, NB, XW], F32, XS)
        X = sb("X", [P, NB, D], F32, XS)


        def first_norm(at, block):
            s_x = sem("n_x", at)
            s_z = sem("n_z", at)
            s_v = sem("n_v", at)
            s_a = sem("n_a", at)
            s_h = sem("n_h", at)
            s_t = sem("n_t", at)
            own = sem("n_own", at)
            st = sb("st", [P, QUAD, 6], F32, at)
            mv = sb("mv", [P, QUAD, 2], F32, at)
            sd = sb("sd", [P, QUAD], F32, at)
            rs = sb("rs", [P, QUAD], F32, at)
            T = sb("T", [P, QUAD, D], F32, at)
            full = N_BLK - 1
            tab = h_tab.rearrange("(b p) f -> p b f", p=P)

            @block.sync
            def _(sp):
                half = full // 2
                xb = x[0:full * P].rearrange("(b p) f -> p b f", p=P)
                sp.dma_start(X[:, 0:half, :], xb[:, 0:half, :]).then_inc(s_x, 16)
                sp.wait_ge(s_z, 1)
                sp.dma_start(X[0:TAIL, full, :], x[full * P:, :]).then_inc(s_x, 16)
                with sp.Fori(0, NB // QUAD) as i:
                    sp.wait_ge(s_h, i + 1)
                    sp.dma_start(tab[:, bass.ds(i * QUAD, QUAD), :],
                                 H[:, bass.ds(i * QUAD, QUAD), 0:D]).then_inc(s_t, 16)
                sp.wait_ge(s_t, 16 * (NB // QUAD))

            @block.scalar
            def _(act):
                half = full // 2
                xb = x[0:full * P].rearrange("(b p) f -> p b f", p=P)
                act.dma_start(X[:, half:full, :], xb[:, half:, :]).then_inc(s_x, 16)
                with act.Fori(0, NB // QUAD) as i:
                    act.wait_ge(s_v, i + 1)
                    act.activation(sd[:], mv[:, :, 1], ACT.Sqrt, bias=eps[:]).then_inc(s_a, 1)

            @block.vector
            def _(dve):
                dve.memset(X[:, full:, :], 0.0).then_inc(s_z, 1)
                dve.wait_ge(s_z, 1)
                dve.wait_ge(s_x, 48)
                with dve.Fori(0, NB // QUAD) as i:
                    c = Chain(dve, own, i, 4)
                    quad = bass.ds(i * QUAD, QUAD)
                    for n in range(QUAD):
                        last = dve.bn_stats(st[:, n, :], X[:, bass.ds(i * QUAD + n, 1), :])
                    c.link(last, alone=True)
                    for n in range(QUAD):
                        last = dve.bn_aggr(mv[:, n, :], st[:, n, :])
                    last.then_inc(s_v, 1)
                    dve.wait_ge(s_v, i + 1)
                    c.link(dve.tensor_tensor(T[:], X[:, quad, :], mv[:, :, 0:1].to_broadcast([P, QUAD, D]),
                                             ALU.subtract))
                    dve.wait_ge(s_a, i + 1)
                    c.link(dve.reciprocal(rs[:], sd[:]))
                    dve.scalar_tensor_tensor(H[:, quad, 0:D], T[:], 0.0, rs[:, :, None].to_broadcast([P, QUAD, D]),
                                             ALU.max, ALU.mult).then_inc(s_h, 1)
                    dve.wait_ge(s_h, i + 1)
                    c.link(dve.memset(T[:, 0, 0:1], 0.0))
                    c.end()

        stage(first_norm)

        def gather_sums(table, edge_terms):
            def body(at, block):
                s_i = sem("g_i", at)
                s_g = [sem(f"g_g{u}", at) for u in range(2)]
                s_o = sem("g_o", at)
                s_m = sem("g_m", at)
                s_c = sem("g_c", at)
                s_one = sem("g_one", at)
                own = sem("g_own", at)
                idx = sb("idx", [P, 2, J], I32, at)
                G = sb("G", [P, 2, J, D + 1], F32, at)
                OH = sb("OH", [P, 2, J, P], F32, at)
                psu = ps("psu", [P, 2, 512], at)
                if edge_terms:
                    s_at = [sem(f"e_at{u}", at) for u in range(2)]
                    s_et = sem("e_t", at)
                    s_ec = sem("e_c", at)
                    s_em = sem("e_m", at)
                    s_eo = sem("e_o", at)
                    s_es = sem("e_s", at)
                    at_in = sb("at_in", [P, 2, ES * D_EDGE], F32, at)
                    at_t = sb("at_t", [P, 4, P], F32, at)
                    ae_o = sb("ae_o", [P, ES * HEADS], F32, at)
                    pet = ps("pet", [P, 4, P], at)
                    pem = ps("pem", [P, 512], at)
                    attr = edge_attr.rearrange("(p e) d -> p (e d)", p=EP)
                    aeo = ae_tab[0:N_EDGES * HEADS].rearrange("(p e) -> p e", p=EP)

                @block.gpsimd
                def _(pool):
                    with pool.Fori(0, N_GRP // 2) as i:
                        for u in range(2):
                            g = 2 * i + u
                            pool.wait_ge(s_i, g + 1)
                            hold(pool, s_m, g * NT + NT)
                            for j in range(J):
                                pool.indirect_dma_start(
                                    G[:, u, j, 0:D], None, table, bass.IndirectOffsetOnAxis(
                                        ap=idx[:, u, j:j + 1], axis=0)).then_inc(s_g[u], 16)

                if edge_terms:
                    @block.sync
                    def _(sp):
                        with sp.Fori(0, E_STEPS // 2) as i:
                            for u in range(2):
                                t = 2 * i + u
                                sp.wait_ge(s_et, t + 1)
                                sp.dma_start(at_in[0:EP, u, :], attr[:, bass.ds(t * ES * D_EDGE, ES * D_EDGE)]
                                             ).then_inc(s_at[u], 16)

                @block.scalar
                def _(act):
                    def group(i, u, terms):
                        g = 2 * i + u
                        act.wait_ge(s_m, g * NT + 2 * NT)
                        act.copy(idx[:, 1 - u, :], SRC[:, bass.ds(g * J + J, J)]).then_inc(s_i, 1)
                        if terms:
                            act.wait_ge(s_et, g + 3)
                            act.copy(at_t[:, :, 0:EP], pet[:, :, 0:EP]).then_inc(s_ec, 1)
                            act.wait_ge(s_em, g + 1)
                            act.copy(ae_o[0:EP, :], pem[0:EP, 0:ES * HEADS]).then_inc(s_eo, 1)
                            act.wait_ge(s_eo, g + 2)
                            act.dma_start(aeo[:, bass.ds(g * ES * HEADS, ES * HEADS)],
                                          ae_o[0:EP, :]).then_inc(s_es, 16)
                            act.wait_ge(s_es, 16 * (g + 1))

                    act.copy(idx[:, 0, :], SRC[:, 0:J]).then_inc(s_i, 1)
                    done = E_STEPS // 2 if edge_terms else 0
                    if edge_terms:
                        with act.Fori(0, done) as i:
                            for u in range(2):
                                group(i, u, True)
                    with act.Fori(done, N_GRP // 2) as i:
                        for u in range(2):
                            group(i, u, False)

                @block.tensor
                def _(pe):
                    def group(i, u, terms):
                        g = 2 * i + u
                        if terms:
                            pe.wait_ge(s_at[u], 16 * (i + 1))
                            pe.wait_ge(s_eo, g + 1)
                            for n in range(4):
                                mm = pe.transpose(pet[:, n, 0:EP], at_in[0:EP, u, n * P:n * P + P],
                                                  ident[0:EP, 0:EP])
                            mm.then_inc(s_et, 1)
                        pe.wait_ge(s_g[u], 16 * J * (i + 1))
                        pe.wait_ge(s_o, g + 1)
                        for t in range(NT):
                            pe.wait_ge(s_c, g * NT + t + 1)
                            for j in range(TRI * t, TRI * t + TRI):
                                k = (NT * u + t) % 2, (j % TRI) * MW
                                mm = pe.matmul(psu[:, k[0], k[1]:k[1] + D + 1], OH[:, u, j, :], G[:, u, j, :],
                                               start=True, stop=True)
                            mm.then_inc(s_m, 1)
                            if terms and t == 1:
                                pe.wait_ge(s_ec, g + 1)
                                for n in range(4):
                                    mm = pe.matmul(pem[0:EP, n * 32:n * 32 + 32], at_t[:, n, 0:EP],
                                                   BD[:].rearrange("p e h -> p (e h)"), start=True, stop=True)
                                mm.then_inc(s_em, 1)

                    pe.sem_inc(s_m, 2 * NT)
                    done = E_STEPS // 2 if edge_terms else 0
                    pe.wait_ge(s_one, 1)
                    if edge_terms:
                        pe.sem_inc(s_et, 2)
                        pe.sem_inc(s_eo, 1)
                        with pe.Fori(0, done) as i:
                            for u in range(2):
                                group(i, u, True)
                    with pe.Fori(done, N_GRP // 2) as i:
                        for u in range(2):
                            group(i, u, False)

                @block.vector
                def _(dve):
                    def one_hot(g, u):
                        dve.wait_ge(s_m, g * NT + NT)
                        dve.tensor_tensor(OH[:, u], rowi[:, None, :].to_broadcast([P, J, P]),
                                          REL[:, bass.ds(g * J, J)][:, :, None].to_broadcast([P, J, P]),
                                          ALU.is_equal).then_inc(s_o, 1)

                    dve.memset(G[:, :, :, D:], 1.0).then_inc(s_one, 1)
                    dve.memset(ACC[:], 0.0).then_inc(s_one, 1)
                    dve.wait_ge(s_one, 2)
                    dve.sem_inc(s_c, 2)
                    dve.wait_ge(s_m, NT)
                    dve.tensor_tensor(OH[:, 0], rowi[:, None, :].to_broadcast([P, J, P]),
                                      REL[:, 0:J][:, :, None].to_broadcast([P, J, P]),
                                      ALU.is_equal).then_inc(s_o, 1)
                    with dve.Fori(0, N_GRP // 2) as i:
                        for u in range(2):
                            g = 2 * i + u
                            one_hot(g + 1, 1 - u)
                            c = Chain(dve, own, i, 2 * (J - NT))
                            c.n = u * (J - NT)
                            for j in range(J):
                                if j % 8 == 0:
                                    _, blk = nc.values_load_multi_w_load_instructions(
                                        BLK[0:1, bass.ds(g + 2, 1), j:j + 8], engines=DVE_ONLY,
                                        min_val=0, max_val=NB - 1)
                                if j % TRI == 0:
                                    dve.wait_ge(s_m, g * NT + j // TRI + 1 + 2 * NT)
                                a = ACC[:, bass.ds(blk[j % 8], 1), 0:D + 1]
                                k = (NT * u + j // TRI) % 2, (j % TRI) * MW
                                add = dve.tensor_tensor(a, psu[:, k[0], k[1]:k[1] + D + 1][:, None, :], a, ALU.add)
                                if j % TRI == TRI - 1:
                                    add.then_inc(s_c, 1)
                                    dve.wait_ge(s_c, g * NT + j // TRI + 3)
                                else:
                                    c.link(add)
            return body

        stage(gather_sums(h_tab, True))

        def hidden(at, block):
            PAIR = 2
            NP2 = NB // PAIR
            s_a = sem("d_a", at)
            s_s = sem("d_s", at)
            s_t = sem("d_t", at)
            s_e = sem("d_e", at)
            s_p = sem("d_p", at)
            s_h = sem("d_h", at)
            s_o = sem("d_o", at)
            s_y = sem("d_y", at)
            s_b = sem("d_b", at)
            s_d = [sem(f"d_d{u}", at) for u in range(2)]
            s_r = sem("d_r", at)
            s_d = sem("d_d", at)
            s_f = sem("d_f", at)
            s_ag = sem("d_ag", at)
            s_at = sem("d_at", at)
            s_ac = sem("d_ac", at)
            own = sem("d_own", at)
            A2 = sb("A2", [P, 2, PAIR, D], F32, at)
            H2 = sb("H2", [P, 2, PAIR, D], F32, at)
            TT = sb("TT", [P, 2, 2 * PAIR * D], F32, at)
            HID = sb("HID", [P, 2, 2, PAIR * P], F32, at)
            Y2 = sb("Y2", [P, 2, PAIR, D], F32, at)
            CNT = sb("CNT", [P, NB], F32, at)
            b2all = sb("b2all", [P, D], F32, at)
            aer = sb("aer", [P, KC, P * HEADS], F32, at)
            pt = ps("pt", [P, 2, 512], at)
            ph = ps("ph", [P, 2, 512], at)
            po = ps("po", [P, 2, 512], at)
            ytab = y_tab.rearrange("(b p) f -> p b f", p=P)

            @block.sync
            def _(sp):
                sp.dma_start(b2all[:], b2.rearrange("(o f) -> o f", o=1).to_broadcast([P, D])).then_inc(s_r, 16)
                sp.sem_inc(s_f, 2)
                with sp.Fori(0, NP2 // 2) as i:
                    for u in range(2):
                        t = 2 * i + u
                        sp.wait_ge(s_y, t + 3)
                        sp.dma_start(ytab[:, bass.ds(t * PAIR, PAIR), :], Y2[:, u]).then_inc(s_d, 16)
                        sp.wait_ge(s_d, 16 * (t + 1))
                        sp.sem_inc(s_f, 1)

            @block.gpsimd
            def _(pool):
                pool.wait_ge(s_r, 16)
                with pool.Fori(0, NP2) as t:
                    hold(pool, s_s, t + 1)
                    pair = bass.ds(t * PAIR, PAIR)
                    pool.tensor_tensor(H[:, pair, 0:D], H[:, pair, 0:D],
                                       b2all[:, None, :].to_broadcast([P, PAIR, D]), ALU.add).then_inc(s_b, 1)
                flat = ae_tab.rearrange("(o e) -> o e", o=1)
                for c in range(KC):
                    pool.indirect_dma_start(aer[:, c, :], None, flat, bass.IndirectOffsetOnAxis(
                        ap=ek4i[:, c:c + 1], axis=1)).then_inc(s_ag, 16)

            @block.scalar
            def _(act):
                def stage_h(t, u):
                    act.copy(H2[:, u], H[:, bass.ds(t * PAIR, PAIR), 0:D]).then_inc(s_s, 1)

                def step(t, u, ahead=True, following=True):
                    if ahead:
                        hold(act, s_t, t + 1)
                        stage_h(t + 2, u)
                    if following:
                        act.wait_ge(s_t, t + 2)
                        act.wait_ge(s_p, t + 1)
                        act.copy(TT[:, 1 - u], pt[:, 1 - u]).then_inc(s_e, 1)
                    act.wait_ge(s_p, t + 2)
                    act.wait_ge(s_o, t + 1)
                    for m in range(2):
                        last = act.activation(HID[:, u, m], ph[:, u, m * 256:(m + 1) * 256], ACT.Relu,
                                              bias=b1c[:, m:m + 1])
                    last.then_inc(s_h, 1)

                stage_h(0, 0)
                stage_h(1, 1)
                act.wait_ge(s_t, 1)
                act.copy(TT[:, 0], pt[:, 0]).then_inc(s_e, 1)
                with act.Fori(0, NP2 // 2 - 1) as i:
                    for u in range(2):
                        step(2 * i + u, u)
                step(NP2 - 2, 0, ahead=False)
                step(NP2 - 1, 1, ahead=False, following=False)
                for n in range(KC):
                    act.wait_ge(s_at, n + 1)
                    act.copy(AE[:, :, n * P:(n + 1) * P], pt[:, n % 2].rearrange("p (h k) -> p h k", h=HEADS)
                             ).then_inc(s_ac, 1)

            @block.tensor
            def _(pe):
                def turn(t, u, fresh=False):
                    pe.wait_ge(s_a, t + 1)
                    pe.wait_ge(s_s, t + 1)
                    if not fresh:
                        pe.wait_ge(s_e, t - 1)
                    for n in range(PAIR):
                        pe.transpose(pt[:, u, n * P:n * P + P], A2[:, u, n], ident[:])
                        mm = pe.transpose(pt[:, u, (PAIR + n) * P:(PAIR + n + 1) * P], H2[:, u, n], ident[:])
                    mm.then_inc(s_t, 1)

                def first(t, u):
                    pe.wait_ge(s_e, t + 1)
                    pe.wait_ge(s_h, t)
                    for m in range(2):
                        o = ph[:, u, m * 256:(m + 1) * 256]
                        pe.matmul(o, W1T[:, 0, m * P:m * P + P], TT[:, u, 0:256], start=True, stop=False)
                        mm = pe.matmul(o, W1T[:, 1, m * P:m * P + P], TT[:, u, 256:512], start=False, stop=True)
                    mm.then_inc(s_p, 1)

                def second(t, u):
                    pe.wait_ge(s_h, t + 2)
                    pe.wait_ge(s_y, t + 1)
                    for n in range(PAIR):
                        for m in range(2):
                            mm = pe.matmul(po[:, u, n * 256:(n + 1) * 256], HID[:, u, m, n * P:n * P + P],
                                           W2T[:, m].rearrange("p l o -> p (l o)"), start=(m == 0), stop=(m == 1))
                    mm.then_inc(s_o, 1)

                pe.sem_inc(s_p, 1)
                pe.sem_inc(s_h, 1)
                pe.sem_inc(s_o, 2)
                turn(0, 0, fresh=True)
                turn(1, 1, fresh=True)
                first(0, 0)
                with pe.Fori(0, NP2 // 2 - 1) as i:
                    for u in range(2):
                        t = 2 * i + u
                        turn(t + 2, u)
                        first(t + 1, 1 - u)
                        second(t, u)
                first(NP2 - 1, 1)
                second(NP2 - 2, 0)
                second(NP2 - 1, 1)
                pe.wait_ge(s_ag, 16 * KC)
                for n in range(KC):
                    if n >= 2:
                        pe.wait_ge(s_ac, n - 1)
                    row = aer[:, n, :].rearrange("k (e h) -> k h e", h=HEADS)
                    for h in range(HEADS):
                        mm = pe.transpose(pt[:, n % 2, h * P:h * P + P], row[:, h], ident[:])
                    mm.then_inc(s_at, 1)

            @block.vector
            def _(dve):
                c = Chain(dve, own)
                c.link(dve.tensor_copy(CNT[:], ACC[:, :, D]))
                c.link(dve.tensor_scalar(RCNT[:], CNT[:], 1.0, None, ALU.max))
                c.link(dve.reciprocal(RCNT[:], RCNT[:]))
                c.link(dve.tensor_scalar(NOEDGE[:], CNT[:], 0.5, -BIG, ALU.is_lt, ALU.mult))

                def mean(t, u):
                    dve.tensor_tensor(A2[:, u], ACC[:, bass.ds(t * PAIR, PAIR), 0:D],
                                      RCNT[:, bass.ds(t * PAIR, PAIR)][:, :, None].to_broadcast([P, PAIR, D]),
                                      ALU.mult).then_inc(s_a, 1)

                def finish(t, u):
                    o = po[:, u].rearrange("p (n l o) -> p n l o", n=PAIR, l=2)
                    dve.wait_ge(s_o, t + 3)
                    hold(dve, s_f, t + 1)
                    dve.tensor_copy(Y2[:, u], o[:, :, 0])
                    dve.wait_ge(s_b, t + 1)
                    h = H[:, bass.ds(t * PAIR, PAIR), 0:D]
                    dve.tensor_tensor(h, o[:, :, 1], h, ALU.add).then_inc(s_y, 1)

                dve.sem_inc(s_y, 2)
                mean(0, 0)
                mean(1, 1)
                with dve.Fori(0, NP2 // 2 - 1) as i:
                    for u in range(2):
                        t = 2 * i + u
                        dve.wait_ge(s_t, t + 1)
                        mean(t + 2, u)
                        finish(t, u)
                finish(NP2 - 2, 0)
                finish(NP2 - 1, 1)

        stage(hidden)
        stage(gather_sums(y_tab, False))

        def second_norm(at, block):
            NQ = NB // QUAD
            s_v = sem("s_v", at)
            s_a = sem("s_a", at)
            s_h = sem("s_h", at)
            s_t = sem("s_t", at)
            s_e = sem("s_e", at)
            s_p = sem("s_p", at)
            s_x = sem("s_x", at)
            s_d = sem("s_d", at)
            own = sem("s_own", at)
            st = sb("st", [P, QUAD, 6], F32, at)
            mv = sb("mv", [P, QUAD, 2], F32, at)
            sd = sb("sd", [P, QUAD], F32, at)
            rs = sb("rs", [P, QUAD], F32, at)
            U = sb("U", [P, QUAD, D], F32, at)
            V = sb("V", [P, 2, QUAD, D], F32, at)
            HT = sb("HT", [P, 2, QUAD * P], F32, at)
            pt = ps("pt", [P, 2, 512], at)
            pw = ps("pw", [P, 2, 2, 512], at)
            WA = XW + HEADS
            tab = x_tab.rearrange("(b p) f -> p b f", p=P)

            @block.sync
            def _(sp):
                with sp.Fori(0, NQ) as i:
                    sp.wait_ge(s_x, i + 3)
                    quad = bass.ds(i * QUAD, QUAD)
                    sp.dma_start(tab[:, quad, :], H[:, quad, :]).then_inc(s_d, 16)
                    sp.dma_start(x_keep[:, quad, :], X[:, quad, :]).then_inc(s_d, 16)
                sp.wait_ge(s_d, 32 * NQ)

            def quads(eng, step):
                with eng.Fori(0, NQ // 2) as i:
                    for u in range(2):
                        step(2 * i + u, u, i)
                step(NQ - 1, 0, NQ // 2)

            @block.scalar
            def _(act):
                def deviations(q, u, i):
                    for n in range(2):
                        act.wait_ge(s_v, 2 * q + n + 1)
                        act.activation(sd[:], mv[:, :, 1], ACT.Sqrt, bias=eps[:]).then_inc(s_a, 1)

                def products(q, u, i):
                    act.wait_ge(s_t, q + 1)
                    act.wait_ge(s_p, q + 1)
                    act.copy(HT[:, u], pt[:, u]).then_inc(s_e, 1)
                    act.wait_ge(s_p, q + 3)
                    act.nop(nofuse=True)
                    o = pw[:, u, :, 0:2 * WA].rearrange("p a (b w) -> p a b w", b=2)
                    for n in range(2):
                        act.copy(H[:, bass.ds(q * QUAD + 2 * n, 2), :], o[:, n, :, 0:XW])
                    for n in range(2):
                        last = act.copy(ADST[:, bass.ds(q * QUAD + 2 * n, 2), :], o[:, n, :, XW:])
                    last.then_inc(s_x, 1)

                def step(q, u, i):
                    deviations(q, u, i)
                    products(q, u, i)
                quads(act, step)

            @block.tensor
            def _(pe):
                def step(q, u, i):
                    pe.wait_ge(s_h, q + 1)
                    pe.wait_ge(s_x, q + 1)
                    for n in range(QUAD):
                        mm = pe.transpose(pt[:, u, n * P:n * P + P], V[:, u, n], ident[:])
                    mm.then_inc(s_t, 1)
                    pe.wait_ge(s_e, q + 1)
                    for n in range(QUAD):
                        mm = pe.matmul(pw[:, u, n // 2, (n % 2) * WA:(n % 2 + 1) * WA], HT[:, u, n * P:n * P + P],
                                       WX[:], start=True, stop=True)
                    mm.then_inc(s_p, 1)
                pe.sem_inc(s_p, 2)
                pe.sem_inc(s_x, 2)
                quads(pe, step)

            @block.vector
            def _(dve):
                def step(q, u, i):
                    c = Chain(dve, own, q, 12)
                    quad = bass.ds(q * QUAD, QUAD)
                    wide = [P, QUAD, D]

                    def norm(n, t, blocks):
                        for b in range(QUAD):
                            last = dve.bn_stats(st[:, b, :], blocks(b))
                        c.link(last, alone=True)
                        for b in range(QUAD):
                            last = dve.bn_aggr(mv[:, b, :], st[:, b, :])
                        last.then_inc(s_v, 1)
                        dve.wait_ge(s_v, 2 * q + n + 1)
                        c.link(dve.tensor_tensor(t, blocks(None), mv[:, :, 0:1].to_broadcast(wide), ALU.subtract))
                        dve.wait_ge(s_a, 2 * q + n + 1)
                        c.link(dve.reciprocal(rs[:], sd[:]))

                    r = rs[:, :, None].to_broadcast(wide)
                    c.link(dve.tensor_tensor(U[:], ACC[:, quad, 0:D], RCNT[:, quad][:, :, None].to_broadcast(wide),
                                             ALU.mult))
                    c.link(dve.tensor_tensor(U[:], U[:], H[:, quad, 0:D], ALU.add), alone=True)
                    norm(0, U[:], lambda b: U[:] if b is None else U[:, b])
                    c.link(dve.tensor_tensor(U[:], U[:], r, ALU.mult))
                    c.link(dve.tensor_tensor(U[:], U[:], gam[:, None, :].to_broadcast(wide), ALU.mult))
                    c.link(dve.tensor_tensor(U[:], U[:], bet[:, None, :].to_broadcast(wide), ALU.add))
                    c.link(dve.tensor_tensor(X[:, quad, :], X[:, quad, :], U[:], ALU.add), alone=True)
                    norm(1, U[:], lambda b: X[:, quad] if b is None else X[:, bass.ds(q * QUAD + b, 1), :])
                    dve.wait_ge(s_x, q + 1)
                    dve.scalar_tensor_tensor(V[:, u], U[:], 0.0, r, ALU.max, ALU.mult).then_inc(s_h, 1)
                    dve.wait_ge(s_h, q + 1)
                    c.end()
                quads(dve, step)

        stage(second_norm)
        XS.close()

        def attention(at, block):
            R = J * HEADS
            UN = 12
            assert N_GRP % UN == 0
            s_i = sem("a_i", at)
            s_g = [sem(f"a_g{u}", at) for u in range(3)]
            s_o = sem("a_o", at)
            s_m = sem("a_m", at)
            s_c = sem("a_c", at)
            s_kb = sem("a_kb", at)
            s_kc = sem("a_kc", at)
            s_mk = sem("a_mk", at)
            s_tr = sem("a_tr", at)
            s_te = sem("a_te", at)
            s_x = sem("a_x", at)
            s_l = sem("a_l", at)
            s_lt = sem("a_lt", at)
            s_cm = sem("a_cm", at)
            s_row = sem("a_row", at)
            s_cc = sem("a_cc", at)
            s_col = sem("a_col", at)
            s_r = sem("a_r", at)
            s_rt = sem("a_rt", at)
            s_fd = sem("a_fd", at)
            s_f = sem("a_f", at)
            s_fm = sem("a_fm", at)
            s_fx = sem("a_fx", at)
            s_dl = sem("a_dl", at)
            s_p = sem("a_p", at)
            s_ms = sem("a_ms", at)
            s_mp = sem("a_mp", at)
            s_one = sem("a_one", at)
            s_at = sem("a_at", at)
            s_ac = sem("a_ac", at)
            s_ad = sem("a_ad", at)
            s_ae = sem("a_ae", at)
            AD = sb("AD", [P, HEADS, NK], F32, at)
            ADT = sb("ADT", [NB, HEADS, P], F32, at)
            ADG = sb("ADG", [P, J, HEADS], F32, at)
            own = sem("a_own", at)
            idx = sb("idx", [P, 3, J], I32, at)
            G = sb("G", [P, 3, J, XW], F32, at)
            OH = sb("OH", [P, 4, J, P], F32, at)
            OHT = sb("OHT", [P, J, P], F32, at)
            MSG = sb("MSG", [P, 2, J, MW], F32, at)
            KB = sb("KB", [P, HEADS, J], F32, at)
            L = sb("L", [P, HEADS, J], F32, at)
            DL = sb("DL", [P, HEADS, J], F32, at)
            PR = sb("PR", [P, HEADS, J], F32, at)
            KT = sb("KT", [R, P], F32, at)
            MS = sb("MS", [R, P + 1], F32, at)
            FS = sb("FS", [R, P], F32, at)
            LS = sb("LS", [R, P], F32, at)
            FW = sb("FW", [R, P], F32, at)
            CM = sb("CM", [R, P], F32, at)
            rows = sb("rows", [1, 2, HEADS, J], F32, at)
            wa = sb("wa", [1, HEADS, J], F32, at)
            wb = sb("wb", [1, HEADS, J], F32, at)
            cin = sb("cin", [1, HEADS, J], F32, at)
            cbk = sb("cbk", [1, HEADS, J], F32, at)
            aa = sb("aa", [1, HEADS, J], F32, at)
            ab = sb("ab", [1, HEADS, J], F32, at)
            last_m = sb("last_m", [1, HEADS], F32, at)
            f0 = sb("f0", [1, HEADS], F32, at)
            f1 = sb("f1", [1, HEADS], F32, at)
            pt = ps("pt", [P, 2, 512], at)
            pu = ps("pu", [P, 3, 512], at)
            px = ps("px", [P, 512], at)
            pl = ps("pl", [P, 512], at)
            pc = ps("pc", [P, 512], at)
            pk = pt[0:R, 1, 384:512]
            assert J == 15
            ws = sb("ws", [1, J], F32, at)
            OHF = OHT[:].rearrange("p j f -> p (j f)")[0:NB, 0:NK]
            px_l = px[:, 0:R].rearrange("p (h j) -> p h j", h=HEADS)
            pm = pc[:, 192:192 + R].rearrange("p (h j) -> p h j", h=HEADS)
            pf = px[:, 256:256 + HEADS]
            CQ, CW = 4, NK // 4
            NF = -(-J // 4)

            def jh(t):
                return t.rearrange("p h j -> p j h")

            def steps(eng, body):
                with eng.Fori(0, N_GRP // UN) as i:
                    for u in range(UN):
                        body(i, u, UN * i + u)

            @block.gpsimd
            def _(pool):
                def step(i, u, g):
                    pool.wait_ge(s_i, g + 1)
                    hold(pool, s_ms, g + 1)
                    for j in range(J):
                        pool.indirect_dma_start(
                            G[:, u % 3, j, :], None, x_tab, bass.IndirectOffsetOnAxis(
                                ap=idx[:, u % 3, j:j + 1], axis=0)).then_inc(s_g[u % 3], 16)
                steps(pool, step)

            @block.scalar
            def _(act):
                def keys(g):
                    act.copy(KB[:], KEY[:, bass.ds(g * J, J)][:, None, :].to_broadcast([P, HEADS, J])
                             ).then_inc(s_kb, 1)

                def turned(g):
                    act.wait_ge(s_x, g + 1)
                    act.copy(ADG[:].rearrange("p j h -> p h j"), AD[:, :, bass.ds(g * J, J)])
                    for n in range(NF):
                        w = min(4, J - 4 * n)
                        act.wait_ge(s_tr, g * NF + n + 1)
                        if n == NF - 1:
                            act.wait_ge(s_mk, g + 1)
                            act.copy(KT[:], pk).then_inc(s_kc, 1)
                        act.copy(OHT[:, 4 * n:4 * n + w, :].rearrange("p a b -> p (a b)"), pt[:, n % 2, 0:w * P]
                                 ).then_inc(s_te, 1)

                for n in range(2):
                    act.copy(idx[:, n, :], SRC[:, n * J:(n + 1) * J]).then_inc(s_i, 1)
                act.wait_ge(s_at, 1)
                act.copy(ADT[:].rearrange("b h p -> b (h p)"), pl[0:NB, :]).then_inc(s_ac, 1)
                for n in range(HEADS * CQ):
                    act.wait_ge(s_ad, n + 1)
                    act.copy(AD[:, n // CQ, (n % CQ) * CW:(n % CQ + 1) * CW], pu[:, n % 2, 0:CW]).then_inc(s_ae, 1)
                act.wait_ge(s_ae, HEADS * CQ)
                keys(0)
                turned(0)

                def step(i, u, g):
                    act.copy(ws[:], WHOLE[:, bass.ds(g * J, J)])
                    act.wait_ge(s_l, g + 1)
                    act.copy(idx[:, (u + 2) % 3, :], SRC[:, bass.ds((g + 2) * J, J)]).then_inc(s_i, 1)
                    keys(g + 1)
                    turned(g + 1)
                    act.wait_ge(s_fx, g + 1)
                    act.copy(MSG[:, u % 2, :, XW + HEADS:], jh(AE[:, :, bass.ds(g * J, J)]))
                    act.wait_ge(s_fd, g + 1)
                    act.activation(f1[:], f0[:], ACT.Exp).then_inc(s_f, 1)
                    act.wait_ge(s_dl, g + 1)
                    act.activation(PR[:], DL[:], ACT.Exp).then_inc(s_p, 1)
                    act.wait_ge(s_p, g + 2)
                    act.copy(MSG[:, u % 2, :, C_HEAD:XW:HW], jh(PR[:])).then_inc(s_mp, 1)
                steps(act, step)

            @block.tensor
            def _(pe):
                def turn_one_hot(g, u, banks):
                    for n in banks:
                        if n == 0:
                            pe.wait_ge(s_o, g + 1)
                        pe.wait_ge(s_te, g * NF + n + 1)
                        for j in range(4 * n, min(4 * n + 4, J)):
                            mm = pe.transpose(pt[:, n % 2, (j % 4) * P:(j % 4 + 1) * P], OH[:, u % 4, j, :], ident[:])
                        if n == NF - 1:
                            hold(pe, s_kb, g + 1)
                            mm = pe.transpose(pk, KB[:].rearrange("p h j -> p (h j)"), ident[:])
                        mm.then_inc(s_tr, 1)

                def spread(g, chunks):
                    if chunks[0] == 0:
                        pe.wait_ge(s_l, g + 1)
                    for j in chunks:
                        if j % 4 == 0:
                            pe.wait_ge(s_te, g * NF + j // 4 + 3)
                        mm = pe.matmul(px_l[:, :, j], OHT[:, j, :], ADG[:, j, :], start=True, stop=True)
                    if chunks[-1] == J - 1:
                        mm.then_inc(s_x, 1)

                def sums(g, u, banks):
                    for t in banks:
                        pe.wait_ge(s_c, (g + 2) * J + (t + 1) * TRI)
                        for j in range(TRI * t, TRI * t + TRI):
                            k = (NT * (u + 2) + t) % 3, (j % TRI) * MW
                            mm = pe.matmul(pu[:, k[0], k[1]:k[1] + MW], OH[:, u % 4, j, :], MSG[:, u % 2, j, :],
                                           start=True, stop=True)
                        mm.then_inc(s_m, 1)

                pe.sem_inc(s_x, 1)
                for h in range(HEADS):
                    mm = pe.transpose(pl[0:NB, h * P:h * P + P], ADST[:, :, h], ident[:])
                mm.then_inc(s_at, 1)
                pe.wait_ge(s_one, 1)
                pe.wait_ge(s_ac, 1)
                for n in range(HEADS * CQ):
                    if n >= 2:
                        pe.wait_ge(s_ae, n - 1)
                    pe.matmul(pu[:, n % 2, 0:CW], ADT[:, n // CQ, :], OHF[:, (n % CQ) * CW:(n % CQ + 1) * CW],
                              start=True, stop=True).then_inc(s_ad, 1)
                pe.wait_ge(s_ae, HEADS * CQ)
                turn_one_hot(0, 0, range(NF))
                spread(0, range(J))
                sums(-2, -2, range(4))

                def step(i, u, g):
                    hold(pe, s_l, g + 2)
                    pe.transpose(pl[0:R, 0:P], L[:].rearrange("p h j -> p (h j)"), ident[:]).then_inc(s_lt, 1)
                    sums(g - 2, u - 2, (4,))
                    turn_one_hot(g + 1, u + 1, (0,))
                    hold(pe, s_cm, g + 1)
                    pe.matmul(pc[0:1, 0:R], CM[:, 0:1], ident[0:R, 0:R], start=True, stop=True)
                    pe.matmul(pc[0:1, R:2 * R], CM[:, P - 1:P], ident[0:R, 0:R],
                              start=True, stop=True).then_inc(s_row, 1)
                    turn_one_hot(g + 1, u + 1, range(1, NF))
                    pe.wait_ge(s_mp, g + 1)
                    pe.wait_ge(s_ms, g + 3)
                    sums(g - 1, u - 1, (0, 1, 2))
                    pe.wait_ge(s_cc, g + 1)
                    pe.matmul(pc[0:R, 128:129], cin[:].rearrange("o h j -> o (h j)"), ones[0:1, 0:1],
                              start=True, stop=True)
                    pe.matmul(pc[0:R, 129:130], cbk[:].rearrange("o h j -> o (h j)"), ones[0:1, 0:1],
                              start=True, stop=True).then_inc(s_col, 1)
                    spread(g + 1, range(4))
                    hold(pe, s_r, g + 1)
                    pe.transpose(pc[:, 192:192 + R], CM[:], ident[0:R, 0:R]).then_inc(s_rt, 1)
                    spread(g + 1, range(4, J - 1))
                    pe.wait_ge(s_fm, g + 1)
                    pe.matmul(pf, OH[0:1, u % 4, 0, :], f1[:], start=True, stop=True).then_inc(s_fx, 1)
                    spread(g + 1, (J - 1,))
                    sums(g - 1, u - 1, (3,))
                steps(pe, step)
                sums(N_GRP - 2, UN - 2, (4,))
                pe.wait_ge(s_ms, N_GRP + 3)
                pe.wait_ge(s_mp, N_GRP + 1)
                sums(N_GRP - 1, UN - 1, range(NT))

            @block.vector
            def _(dve):
                def one_hot(g, u):
                    dve.tensor_tensor(OH[:, u % 4], rowi[:, None, :].to_broadcast([P, J, P]),
                                      REL[:, bass.ds(g * J, J)][:, :, None].to_broadcast([P, J, P]),
                                      ALU.is_equal).then_inc(s_o, 1)

                def messages(g, u):
                    dve.wait_ge(s_p, g + 2)
                    dve.tensor_tensor(MSG[:, u % 2, :, 0:XW].rearrange(x_l, h=HEADS)[:, :, :, 0:C_HEAD],
                                      G[:, u % 3].rearrange(x_l, h=HEADS)[:, :, :, 0:C_HEAD],
                                      jh(PR[:])[:, :, :, None].to_broadcast([P, J, HEADS, C_HEAD]),
                                      ALU.mult).then_inc(s_ms, 1)

                def masks(g):
                    dve.wait_ge(s_kc, g + 1)
                    dve.tensor_tensor(MS[:, 1:P], KT[:, 0:P - 1], KT[:, 1:P], ALU.subtract)
                    dve.tensor_scalar(FS[:], KT[:], KT[:, 0:1], -1.0, ALU.subtract, ALU.mult)
                    dve.tensor_scalar(LS[:], KT[:], KT[:, P - 1:P], None, ALU.subtract).then_inc(s_mk, 1)

                def blocks(g, at_):
                    _, v = nc.values_load_multi_w_load_instructions(
                        BLK[0:1, bass.ds(g + 2, 1), at_:at_ + 8], engines=DVE_ONLY, min_val=0, max_val=NB - 1)
                    blk[at_:at_ + 8] = v

                def sums(g, u, chunks):
                    for j in chunks:
                        if j % TRI == 0:
                            dve.wait_ge(s_m, (g + 2) * NT + j // TRI + 1)
                        dve.wait_ge(s_c, (g + 2) * J + j + 3 * TRI)
                        a = ACC[:, bass.ds(blk[j], 1), :]
                        k = (NT * (u + 2) + j // TRI) % 3, (j % TRI) * MW
                        dve.tensor_tensor(a, pu[:, k[0], k[1]:k[1] + MW][:, None, :], a, ALU.add).then_inc(s_c, 1)

                def scale(c, g):
                    dve.wait_ge(s_fx, g + 2)
                    dve.wait_ge(s_c, (g + 2) * J + 3 * TRI)
                    a = ACC[:, bass.ds(blk[0], 1), 0:XW].rearrange("p a (h c) -> p (a h) c", h=HEADS)
                    c.mark(dve.scalar_tensor_tensor(a, pf[:, :, None].to_broadcast([P, HEADS, HW]), 1.0, a,
                                                    ALU.add, ALU.mult))

                dve.memset(MS[:], -BIG)
                dve.memset(last_m[:], -BIG)
                dve.memset(aa[:], -BIG)
                dve.memset(ab[:], -BIG)
                dve.memset(wb[:], -BIG)
                dve.memset(OH[:, 2:4], 0.0)
                dve.memset(MSG[:], 0.0)
                dve.memset(G[:, 2], 0.0)
                dve.memset(PR[:], 0.0)
                dve.memset(pf, 0.0)
                dve.tensor_copy(OHF, OHB[0:NB, :])
                dve.memset(ACC[:], 0.0).then_inc(s_one, 1)
                dve.wait_ge(s_one, 1)
                dve.sem_inc(s_c, 3 * TRI)
                dve.sem_inc(s_fx, 1)
                dve.sem_inc(s_te, 2)
                dve.sem_inc(s_mk, 1)
                dve.sem_inc(s_l, 1)
                dve.sem_inc(s_ms, 2)
                dve.sem_inc(s_p, 1)
                dve.sem_inc(s_mp, 1)
                one_hot(0, 0)
                one_hot(1, 1)
                masks(0)
                blk = [None] * 16
                n_own = 9
                blocks(-2, 0)
                sums(-2, -2, range(8))
                flat = "o h j -> o (h j)"
                x_l = "p j (h c) -> p j h c"

                def step(i, u, g):
                    c = Chain(dve, own, i, UN * n_own)
                    c.n = u * n_own
                    before = (g - 1, u - 1)

                    def row(t, at_, n, k=HEADS):
                        return t[:, bass.ds(g * J + at_, n)][:, None, :].to_broadcast([1, k, n])

                    messages(g - 1, u - 1)
                    blocks(g - 2, 8)
                    dve.wait_ge(s_g[u % 3], 16 * J * ((UN // 3) * i + u // 3 + 1))
                    a_src = G[:, u % 3, :, C_HEAD:XW:HW].rearrange("p j h -> p h j")
                    c.mark(dve.tensor_tensor(L[:], a_src, AE[:, :, bass.ds(g * J, J)], ALU.add))
                    sums(g - 2, u - 2, (8,))
                    dve.wait_ge(s_x, g + 2)
                    c.join()
                    c.mark(dve.tensor_tensor(L[:], L[:], px_l, ALU.add))
                    sums(g - 2, u - 2, (9,))
                    c.join()
                    dve.scalar_tensor_tensor(L[:], L[:], SLOPE, L[:], ALU.mult, ALU.max).then_inc(s_l, 1)
                    sums(g - 2, u - 2, (10,))
                    dve.wait_ge(s_lt, g + 1)
                    c.mark(dve.tensor_tensor_scan(FW[:], MS[:, 0:P], pl[0:R, 0:P], -BIG, ALU.add, ALU.max))
                    sums(g - 2, u - 2, (11,))
                    c.join()
                    dve.tensor_tensor_scan(CM[:, ::-1], MS[:, P:0:-1], FW[:, ::-1], -BIG,
                                           ALU.add, ALU.max).then_inc(s_cm, 1)
                    sums(g - 2, u - 2, (12,))
                    one_hot(g + 2, u + 2)
                    blocks(g - 1, 0)
                    sums(g - 2, u - 2, (13,))
                    dve.tensor_tensor(aa[:, :, 1:], row(WHOLE, 0, J - 1), row(LINK, 1, J - 1), ALU.add)
                    dve.tensor_tensor(ab[:, :, 0:J - 1], row(WHOLE, 1, J - 1), row(LINK, 1, J - 1), ALU.add)
                    dve.tensor_tensor(wa[:, :, 0:1], last_m[:, :, None], row(LINK, 0, 1), ALU.add)
                    sums(g - 2, u - 2, (14,))
                    dve.wait_ge(s_row, g + 1)
                    c.link(dve.tensor_copy(rows[:].rearrange("o a h j -> o (a h j)"), pc[0:1, 0:2 * R]))
                    scale(c, g - 1)
                    dve.tensor_tensor(wa[:, :, 1:], rows[:, 1, :, 0:J - 1], row(LINK, 1, J - 1), ALU.add)
                    c.link(dve.tensor_tensor(wb[:, :, 0:J - 1], rows[:, 0, :, 1:], row(LINK, 1, J - 1), ALU.add))
                    dve.tensor_tensor_scan(cin[:].rearrange(flat), aa[:].rearrange(flat), wa[:].rearrange(flat),
                                           -BIG, ALU.add, ALU.max)
                    dve.tensor_tensor_scan(cbk[:].rearrange(flat)[:, ::-1], ab[:].rearrange(flat)[:, ::-1],
                                           wb[:].rearrange(flat)[:, ::-1], -BIG, ALU.add, ALU.max).then_inc(s_cc, 1)
                    sums(*before, (0,))
                    dve.wait_ge(s_i, g + 3)
                    dve.wait_ge(s_cc, g + 1)
                    dve.scalar_tensor_tensor(last_m[:], cin[:, :, J - 1], ws[:, J - 1:J],
                                             rows[:, 1, :, J - 1], ALU.add, ALU.max)
                    c.link(dve.scalar_tensor_tensor(f0[:], cbk[:, :, 0], ws[:, 0:1],
                                                    rows[:, 0, :, 0], ALU.add, ALU.max))
                    c.link(dve.tensor_tensor(f0[:], f0[:], cin[:, :, 0], ALU.max))
                    dve.tensor_tensor(f0[:], cin[:, :, 0], f0[:], ALU.subtract).then_inc(s_fd, 1)
                    dve.wait_ge(s_col, g + 1)
                    c.mark(dve.scalar_tensor_tensor(CM[:], FS[:], pc[0:R, 128:129], CM[:], ALU.add, ALU.max))
                    sums(*before, (1,))
                    c.join()
                    dve.scalar_tensor_tensor(CM[:], LS[:], pc[0:R, 129:130], CM[:], ALU.add, ALU.max).then_inc(s_r, 1)
                    sums(*before, (2, 3))
                    dve.wait_ge(s_f, g + 1)
                    dve.tensor_scalar(f1[:], f1[:], -1.0, None, ALU.add).then_inc(s_fm, 1)
                    sums(*before, (4,))
                    dve.wait_ge(s_rt, g + 1)
                    dve.tensor_tensor(DL[:], L[:], pm, ALU.subtract).then_inc(s_dl, 1)
                    sums(*before, (5,))
                    dve.tensor_tensor(MSG[:, u % 2, :, XW:XW + HEADS], jh(pm),
                                      LAST[:, bass.ds(g * J, J)][:, :, None].to_broadcast([P, J, HEADS]), ALU.mult)
                    sums(*before, (6,))
                    masks(g + 1)
                    sums(*before, (7,))
                    assert c.n == (u + 1) * n_own, (c.n, n_own)
                steps(dve, step)
                c = Chain(dve, own, N_GRP // UN, UN * n_own)
                blocks(N_GRP - 2, 8)
                sums(N_GRP - 2, UN - 2, range(8, J))
                messages(N_GRP - 1, UN - 1)
                blocks(N_GRP - 1, 0)
                blocks(N_GRP - 1, 8)
                scale(c, N_GRP - 1)
                c.join()
                sums(N_GRP - 1, UN - 1, range(J))
        stage(attention)

        def finish(at, block):
            NQ = NB // QUAD
            own = sem("f_own", at)
            s_d = sem("f_d", at)
            s_m = sem("f_m", at)
            s_e = sem("f_e", at)
            s_o = sem("f_o", at)
            s_t = sem("f_t", at)
            shape = [P, NB, HEADS]
            sl = sb("sl", shape, F32, at)
            mr = sb("mr", shape, F32, at)
            mx = sb("mx", shape, F32, at)
            de = sb("de", [P, 2, NB, HEADS], F32, at)
            ex = sb("ex", [P, 2, NB, HEADS], F32, at)
            A = sb("A", [P, QUAD, D], F32, at)
            B = sb("B", [P, QUAD, D], F32, at)
            X = sb("X", [P, NB, D], F32, at)
            H = sb("H", [P, NB, XW], F32, at)
            s_x = sem("f_x", at)
            s_h = sem("f_h", at)
            Hh = H[:].rearrange("p b (h c) -> p b h c", h=HEADS)
            Ah = ACC[:, :, 0:XW].rearrange("p b (h c) -> p b h c", h=HEADS)

            @block.scalar
            def _(act):
                act.wait_ge(s_m, 1)
                act.activation(ex[:], de[:], ACT.Exp).then_inc(s_e, 1)

            @block.vector
            def _(dve):
                c = Chain(dve, s_o)
                dve.wait_ge(s_h, 16)
                wide = RCNT[:, :, None].to_broadcast(shape)
                c.link(dve.tensor_tensor(sl[:], ACC[:, :, XW + HEADS:], wide, ALU.mult))
                c.link(dve.tensor_tensor(sl[:], sl[:], Hh[:, :, :, C_HEAD], ALU.add))
                c.link(dve.tensor_tensor(sl[:], sl[:], ADST[:], ALU.add))
                c.link(dve.scalar_tensor_tensor(sl[:], sl[:], SLOPE, sl[:], ALU.mult, ALU.max))
                c.link(dve.tensor_tensor(mr[:], ACC[:, :, XW:XW + HEADS], NOEDGE[:, :, None].to_broadcast(shape), ALU.add))
                c.link(dve.tensor_tensor(mx[:], mr[:], sl[:], ALU.max))
                dve.tensor_tensor(de[:, 0], mr[:], mx[:], ALU.subtract)
                dve.tensor_tensor(de[:, 1], sl[:], mx[:], ALU.subtract).then_inc(s_m, 1)
                dve.wait_ge(s_e, 1)
                c.link(dve.tensor_tensor(mx[:], Ah[:, :, :, C_HEAD], ex[:, 0], ALU.mult))
                c.link(dve.tensor_tensor(mx[:], mx[:], ex[:, 1], ALU.add))
                c.link(dve.reciprocal(mx[:], mx[:]))
                dve.tensor_tensor(ex[:, 0], ex[:, 0], mx[:], ALU.mult)
                c.link(dve.tensor_tensor(ex[:, 1], ex[:, 1], mx[:], ALU.mult), alone=True)
                dve.wait_ge(s_x, 16)
                with dve.Fori(0, NQ) as i:
                    c = Chain(dve, own, i, 4)
                    quad = bass.ds(i * QUAD, QUAD)

                    def by(n):
                        return ex[:, n, quad, :][:, :, :, None].to_broadcast([P, QUAD, HEADS, C_HEAD])

                    def heads(t):
                        return t.rearrange("p b (h c) -> p b h c", h=HEADS)
                    dve.tensor_tensor(heads(A[:]), Ah[:, quad, :, 0:C_HEAD], by(0), ALU.mult)
                    c.link(dve.tensor_tensor(heads(B[:]), Hh[:, quad, :, 0:C_HEAD], by(1), ALU.mult))
                    c.link(dve.tensor_tensor(A[:], A[:], B[:], ALU.add))
                    c.link(dve.tensor_tensor(A[:], A[:], bia[:, None, :].to_broadcast([P, QUAD, D]), ALU.add))
                    c.link(dve.tensor_tensor(X[:, quad, :], X[:, quad, :], A[:], ALU.add))
                    dve.sem_inc(s_d, 1)
                    c.end()

            @block.sync
            def _(sp):
                full = N_BLK - 1
                o = out[0:full * P].rearrange("(b p) f -> p b f", p=P)
                sp.dma_start(H[:], x_tab.rearrange("(b p) f -> p b f", p=P)).then_inc(s_h, 16)
                sp.dma_start(X[:], x_keep).then_inc(s_x, 16)
                with sp.Fori(0, full // QUAD) as i:
                    sp.wait_ge(s_d, i + 1)
                    quad = bass.ds(i * QUAD, QUAD)
                    sp.dma_start(o[:, quad, :], X[:, quad, :]).then_inc(s_t, 16)
                sp.wait_ge(s_d, NQ)
                sp.dma_start(out[full * P:, :], X[0:TAIL, full, :]).then_inc(s_t, 16)
                sp.wait_ge(s_t, 16 * (full // QUAD + 1))

        stage(finish)
def debug_out(nc, stage, sem, out, dbg, *ts):
    def body(at, block):
        s = sem("dbg", at)
        @block.sync
        def _(sp):
            for d, t in zip(dbg, ts):
                sp.dma_start(d, t).then_inc(s, 16)
            sp.wait_ge(s, 16*len(ts))
    stage(body)


_INS = ["x", "src", "dst", "edge_attr_16", "L0_gnn_W1l", "L0_gnn_W1r", "L0_gnn_b1", "L0_gnn_W2l", "L0_gnn_W2r",
        "L0_gnn_b2", "L0_gnn_gamma", "L0_gnn_beta", "L1_gnn_W", "L1_gnn_W_edge", "L1_gnn_att_src",
        "L1_gnn_att_dst", "L1_gnn_att_edge", "L1_gnn_bias"]


def kernel(**inputs):
    import concourse.bacc as bacc
    from concourse.bass_utils import run_bass_kernel_spmd as run

    nc = bacc.Bacc("TRN2", target_bir_lowering=False, num_devices=1)
    arrays, args = {}, []
    for name in _INS:
        a = np.ascontiguousarray(inputs[name])
        arrays["in_" + name] = a
        args.append(nc.dram_tensor("in_" + name, a.shape, mybir.dt.from_np(a.dtype), kind="ExternalInput").ap())
    result = nc.dram_tensor("out", (N_NODES, D), F32, kind="ExternalOutput").ap()
    DBG = False
    shapes = [(P, NB, D), (P, NB, XW), (P, NB, HEADS)]
    dbg = [nc.dram_tensor(f"dbg{i}", sh, F32, kind="ExternalOutput").ap() for i, sh in enumerate(shapes)] if DBG else None
    build(nc, *args, result, dbg, 2)
    r = run(nc, [arrays], core_ids=[0])
    if DBG:
        return tuple(r.results[0][f"dbg{i}"] for i in range(len(shapes)))
    return r.results[0]["out"]
```

```python
from contextlib import ExitStack

import concourse.bass as bass
import numpy as np
from concourse import mybir
from concourse.alu_op_type import AluOpType as ALU

F32 = mybir.dt.float32
I32 = mybir.dt.int32
BF16 = mybir.dt.bfloat16
I16 = mybir.dt.int16
ACT = mybir.ActivationFunctionType
AX = mybir.AxisListType
DVE_ONLY = (mybir.EngineType.DVE,)

P = 128
N_NODES, D = 6250, 128
N_EDGES, D_EDGE = 200000, 16
D_HID = 256
HEADS, C_HEAD = 4, 32
N_BLK = -(-N_NODES // P)
QUAD = 4
NB = -(-N_BLK // QUAD) * QUAD
TAIL = N_NODES - (N_BLK - 1) * P

J = 15
TRI = 3
NT = J // TRI
MAX_CHUNKS = (N_EDGES + N_BLK * (P - 1)) // P
N_GRP = 2 * -(-MAX_CHUNKS // (2 * J))
KC = -(-N_GRP * J // P)
NK = KC * P
assert NK >= (N_GRP + 1) * J
E_PAD = KC * P * P
SENTINEL = 16384

HW = C_HEAD + 1
XW = HEADS * HW
MW = XW + 2 * HEADS
BIG = float(2.0 ** 100)
EPS = 1e-5
SLOPE = 0.2

EP, ES = 125, 32
E_STEPS = N_EDGES // (EP * ES)
assert E_STEPS * EP * ES == N_EDGES and 2 * E_STEPS <= N_GRP


def hold(eng, semaphore, value):
    eng.wait_ge(semaphore, value)
    eng.nop(nofuse=True)


class Chain:

    def __init__(self, eng, semaphore, i=None, per=0):
        self.eng, self.semaphore, self.i, self.per, self.n = eng, semaphore, i, per, 0

    def count(self):
        return self.n if self.i is None else self.i * self.per + self.n

    def mark(self, ins):
        ins.then_inc(self.semaphore, 1)
        self.n += 1

    def join(self):
        self.eng.wait_ge(self.semaphore, self.count())

    def link(self, ins, alone=False):
        self.mark(ins)
        if alone:
            hold(self.eng, self.semaphore, self.count())
        else:
            self.join()

    def end(self):
        assert self.i is None or self.n == self.per, (self.n, self.per)


def scales(dve, c, st, ms, nv, rs, sh, sd, s_v, s_a, s_r, n):
    c.link(dve.tensor_tensor(ms, st[:, :, 1], st[:, :, 4], ALU.subtract))
    c.link(dve.tensor_tensor(ms, ms, ms, ALU.mult))
    c.link(dve.tensor_tensor(nv, st[:, :, 2], st[:, :, 5], ALU.add))
    dve.scalar_tensor_tensor(nv, ms, D / 4.0, nv, ALU.mult, ALU.add).then_inc(s_v, 1)
    dve.wait_ge(s_a, n + 1)
    c.link(dve.tensor_tensor(ms, st[:, :, 1], st[:, :, 4], ALU.add))
    c.link(dve.reciprocal(rs, sd))
    dve.scalar_tensor_tensor(sh, ms, -0.5, rs, ALU.mult, ALU.mult).then_inc(s_r, 1)
    dve.wait_ge(s_r, n + 1)


def build(nc, x, src, dst, edge_attr, W1l, W1r, b1, W2l, W2r, b2, gamma, beta,
          W, W_edge, att_src, att_dst, att_edge, bias, out):
    with ExitStack() as top:
        stages = []

        def sb(name, shape, dt=F32, at=top):
            return at.enter_context(nc.sbuf_tensor(f"{name}_{len(stages)}", shape, dt))

        def ps(name, shape, at):
            return at.enter_context(nc.psum_tensor(f"{name}_{len(stages)}", shape, F32))

        def sem(name, at):
            return at.enter_context(nc.semaphore(f"{name}_{len(stages)}"))

        src_pad = nc.dram_tensor("src_pad", [E_PAD], I32).ap()
        dst_pad = nc.dram_tensor("dst_pad", [E_PAD], I32).ap()
        ae_tab = nc.dram_tensor("ae_tab", [N_EDGES * HEADS + 4 * P * HEADS], F32).ap()
        h_tab = nc.dram_tensor("h_tab", [NB * P, D], F32).ap()
        y_tab = nc.dram_tensor("y_tab", [NB * P, D], F32).ap()
        x_keep = nc.dram_tensor("x_keep", [P, NB, D], F32).ap()
        x_tab = nc.dram_tensor("x_tab", [NB * P, XW], F32).ap()

        RCNT = sb("RCNT", [P, NB])
        NOEDGE = sb("NOEDGE", [P, NB])
        ADST = sb("ADST", [P, NB, HEADS])
        SELF = sb("SELF", [P, NB, HEADS])
        SRC = sb("SRC", [P, NK], I16)
        REL = sb("REL", [P, NK], BF16)
        KEY = sb("KEY", [P, NK])
        LAST = sb("LAST", [P, NK], BF16)
        BLK = sb("BLK", [1, N_GRP + 2, 16], I16)
        LINK = sb("LINK", [1, NK], BF16)
        WHOLE = sb("WHOLE", [1, NK], BF16)
        OHB = sb("OHB", [P, NK], BF16)
        ek4i = sb("ek4i", [P, KC], I32)
        ident = sb("ident", [P, P])
        rowi = sb("rowi", [P, P])
        coli = sb("coli", [P, 1])
        ones = sb("ones", [P, P])
        W1T = sb("W1T", [P, 2, D_HID])
        W2T = sb("W2T", [P, 2, 2, D])
        WX = sb("WX", [P, XW + HEADS])
        BD = sb("BD", [P, 8, HEADS])
        b1c = sb("b1c", [P, 2])
        b2row = sb("b2row", [1, 2 * D])
        gam = sb("gam", [P, D])
        bet = sb("bet", [P, D])
        bia = sb("bia", [P, D])
        eps = sb("eps", [P, 1])

        ACC = sb("ACC", [P, NB, MW])
        AE = sb("AE", [P, HEADS, NK])
        XS = ExitStack()
        H = sb("H", [P, NB, XW], F32, XS)
        X = sb("X", [P, NB, D], F32, XS)

        def stage(body):
            stages.append(body.__name__)
            with ExitStack() as at, nc.Block() as block:
                body(at, block)

        def prepare(at, block):
            s_in = sem("p_in", at)
            s_w = sem("p_w", at)
            s_rows = sem("p_rows", at)
            s_io = sem("p_io", at)
            s_g1 = sem("p_g1", at)
            s_gs = sem("p_gs", at)
            s_gd = sem("p_gd", at)
            s_gn = sem("p_gn", at)
            s_d = sem("p_d", at)
            s_p = sem("p_p", at)
            s_kl = sem("p_kl", at)
            s_at = sem("p_at", at)
            s_pad = sem("p_pad", at)
            s_b = sem("p_b", at)
            s_e = sem("p_e", at)
            s_x = sem("p_x", at)
            s_z = sem("p_z", at)
            s_q = sem("p_q", at)
            s_v = sem("p_v", at)
            s_a = sem("p_a", at)
            s_r = sem("p_r", at)
            s_h = sem("p_h", at)
            s_t = sem("p_t", at)
            NTURN = -(-KC // 4)
            full = N_BLK - 1
            xb = x[0:full * P].rearrange("(b p) f -> p b f", p=P)
            st = sb("st", [P, NB, 6], F32, at)
            nv = sb("nv", [P, NB], F32, at)
            ms = sb("ms", [P, NB], F32, at)
            sd = sb("sd", [P, NB], F32, at)
            rs = sb("rs", [P, NB], F32, at)
            sh = sb("sh", [P, NB], F32, at)
            dstf = sb("dstf", [P, NK], F32, at)

            irow = sb("irow", [P, P], I32, at)
            icol = sb("icol", [P, 1], I32, at)
            kpc = sb("kpc", [P, KC], F32, at)
            padt = sb("padt", [P, P], I32, at)
            zero = sb("zero", [P, P], I32, at)
            rows = sb("rows", [P, KC, P], I32, at)
            rowsf = sb("rowsf", [P, KC, P], F32, at)
            kio = rowsf[:].rearrange("p c e -> p (c e)")
            GE = dstf
            srows = sb("srows", [P, KC, P], I32, at)
            nrows = sb("nrows", [P, KC, P], I32, at)
            first = sb("first", [P, KC], F32, at)
            thr = sb("thr", [P, N_BLK + 1], F32, at)
            tcol = sb("tcol", [P, 1], F32, at)
            cmp3 = sb("cmp3", [P, N_BLK + 1, KC], F32, at)
            cnt1 = sb("cnt1", [P, N_BLK + 1], F32, at)
            t1 = sb("t1", [P, 1], F32, at)
            t1i = sb("t1i", [P, 1], I32, at)
            brow = sb("brow", [P, P], I32, at)
            browf = sb("browf", [P, P], F32, at)
            bcmp = sb("bcmp", [P, P], F32, at)
            bcnt = sb("bcnt", [P, 1], F32, at)
            start = sb("start", [P, 1], F32, at)
            eqd = sb("eqd", [P, P], F32, at)
            equ = sb("equ", [P, P], F32, at)
            lt = sb("lt", [P, P], F32, at)
            nch = sb("nch", [P, 1], F32, at)
            nci = sb("nci", [P, 1], I32, at)
            q = sb("q", [P, 1], F32, at)
            dq = sb("dq", [P, 2], F32, at)
            BK = sb("BK", [P, NK], F32, at)
            ek = sb("ek", [P, KC], F32, at)
            eki = sb("eki", [P, KC], I32, at)
            ek1i = sb("ek1i", [P, KC], I32, at)
            KL = ACC[0:1].rearrange("o b f -> o (b f)")[:, 0:NK]
            wl = sb("wl", [P, 2, D], F32, at)
            wr = sb("wr", [P, 2, D], F32, at)
            w2l = sb("w2l", [P, D_HID], F32, at)
            w2r = sb("w2r", [P, D_HID], F32, at)
            wt = sb("wt", [P, D], F32, at)
            we = sb("we", [P, D], F32, at)
            ats = sb("ats", [P, D], F32, at)
            atd = sb("atd", [P, D], F32, at)
            ate = sb("ate", [P, D], F32, at)
            wm = sb("wm", [P, 3, D], F32, at)
            mr = sb("mr", [P, HEADS], F32, at)
            m8 = sb("m8", [P, 8], F32, at)
            pg = sb("pg", [P, 1], F32, at)
            pgi = sb("pgi", [P, 1], I32, at)
            psm = ps("psm", [P, 512], at)
            psb = ps("psb", [P, 4, 512], at)
            pst = ps("pst", [P, 2, 512], at)

            n_tail = E_PAD - N_EDGES
            tail_cols = 112
            assert n_tail % tail_cols == 0 and n_tail // tail_cols <= P
            tail_rows = n_tail // tail_cols

            @block.sync
            def _(sp):
                sp.dma_start(dst_pad[0:N_EDGES].rearrange("(a b) -> a b", a=400),
                             dst.rearrange("(a b) -> a b", a=400)).then_inc(s_in, 16)
                sp.dma_start(src_pad[0:N_EDGES].rearrange("(a b) -> a b", a=400),
                             src.rearrange("(a b) -> a b", a=400)).then_inc(s_in, 16)
                sp.wait_ge(s_pad, 2)
                sp.dma_start(dst_pad[N_EDGES:].rearrange("(a b) -> a b", b=tail_cols),
                             padt[0:tail_rows, 0:tail_cols]).then_inc(s_in, 16)
                sp.dma_start(src_pad[N_EDGES:].rearrange("(a b) -> a b", b=tail_cols),
                             zero[0:tail_rows, 0:tail_cols]).then_inc(s_in, 16)
                sp.wait_ge(s_in, 64)
                sp.dma_start(rows[:], dst_pad.rearrange("(c p e) -> p c e", p=P, e=P)).then_inc(s_rows, 16)
                sp.dma_start(X[:, 0:full // 2, :], xb[:, 0:full // 2, :]).then_inc(s_x, 16)
                sp.wait_ge(s_z, 1)
                sp.dma_start(X[0:TAIL, full, :], x[full * P:, :]).then_inc(s_x, 16)
                tab = h_tab.rearrange("(b p) f -> p b f", p=P)
                with sp.Fori(0, NB // QUAD) as i:
                    sp.wait_ge(s_h, i + 1)
                    sp.dma_start(tab[:, bass.ds(i * QUAD, QUAD), :],
                                 H[:, bass.ds(i * QUAD, QUAD), 0:D]).then_inc(s_t, 16)
                sp.wait_ge(s_d, 14)
                sp.dma_start(KL, KEY[P - 1:P, :]).then_inc(s_kl, 16)
                sp.dma_start(ae_tab[N_EDGES * HEADS:].rearrange("(a b) -> a b", a=16),
                             zero[0:16, :].bitcast(F32)).then_inc(s_at, 16)
                sp.wait_ge(s_at, 16)
                sp.wait_ge(s_t, 16 * (NB // QUAD))

            @block.scalar
            def _(act):
                act.dma_start(wl[:], W1l.rearrange("(m p) f -> p m f", p=P)).then_inc(s_w, 16)
                act.dma_start(wr[:], W1r.rearrange("(m p) f -> p m f", p=P)).then_inc(s_w, 16)
                act.dma_start(w2l[:], W2l).then_inc(s_w, 16)
                act.dma_start(w2r[:], W2r).then_inc(s_w, 16)
                act.dma_start(wt[:], W).then_inc(s_w, 16)
                for r in range(8):
                    act.dma_start(we[16 * r:16 * r + 16, :], W_edge).then_inc(s_w, 16)
                for t, a in ((ats, att_src), (atd, att_dst), (ate, att_edge)):
                    row = a.rearrange("h c -> (h c)").rearrange("(o f) -> o f", o=1)
                    act.dma_start(t[:], row.to_broadcast([P, D])).then_inc(s_w, 16)
                for t, a in ((gam, gamma), (bet, beta), (bia, bias)):
                    act.dma_start(t[:], a.rearrange("(o f) -> o f", o=1).to_broadcast([P, D])).then_inc(s_w, 16)
                with nc.allow_non_contiguous_dma(reason="256 words"):
                    act.dma_start(b1c[:], b1.rearrange("(m p) -> p m", p=P)).then_inc(s_w, 16)
                act.wait_ge(s_b, 1)
                act.dma_start(b2row[:, D:], b2.rearrange("(o f) -> o f", o=1)).then_inc(s_w, 16)
                act.dma_start(X[:, full // 2:full, :], xb[:, full // 2:, :]).then_inc(s_x, 16)
                act.wait_ge(s_v, 1)
                act.activation(sd[:], nv[:], ACT.Sqrt, bias=eps[:], scale=1.0 / D).then_inc(s_a, 1)
                act.wait_ge(s_r, 1)
                with act.Fori(0, NB // QUAD) as i:
                    for n in range(QUAD):
                        one = bass.ds(i * QUAD + n, 1)
                        last = act.activation(H[:, one, 0:D], X[:, one, :], ACT.Relu, bias=sh[:, one],
                                              scale=rs[:, one])
                    last.then_inc(s_h, 1)

            @block.gpsimd
            def _(pool):
                pool.memset(padt[:], SENTINEL).then_inc(s_pad, 1)
                pool.memset(zero[:], 0).then_inc(s_pad, 1)
                pool.iota(irow[:], pattern=[[1, P]], base=0, channel_multiplier=0).then_inc(s_io, 1)
                pool.iota(icol[:], pattern=[[0, 1]], base=0, channel_multiplier=1).then_inc(s_io, 1)
                pool.iota(kio, pattern=[[1, NK]], base=0, channel_multiplier=0,
                          allow_small_or_imprecise_dtypes=True).then_inc(s_io, 1)
                pool.iota(kpc[:], pattern=[[P * P, KC]], base=0, channel_multiplier=P,
                          allow_small_or_imprecise_dtypes=True).then_inc(s_io, 1)
                pool.wait_ge(s_d, 4)
                pool.indirect_dma_start(
                    brow[0:N_BLK + 1, :], None, dst_pad.rearrange("(r e) -> r e", e=P),
                    bass.IndirectOffsetOnAxis(ap=t1i[0:N_BLK + 1, :], axis=0)).then_inc(s_g1, 16)
                pool.wait_ge(s_d, 9)
                flat_s = src_pad.rearrange("(o e) -> o e", o=1)
                flat_d = dst_pad.rearrange("(o e) -> o e", o=1)
                for c in range(KC):
                    pool.indirect_dma_start(srows[:, c, :], None, flat_s, bass.IndirectOffsetOnAxis(
                        ap=eki[:, c:c + 1], axis=1)).then_inc(s_gs, 16)
                pool.wait_ge(s_d, 10)
                for c in range(KC):
                    pool.indirect_dma_start(rows[:, c, :], None, flat_d, bass.IndirectOffsetOnAxis(
                        ap=eki[:, c:c + 1], axis=1)).then_inc(s_gd, 16)
                for c in range(KC):
                    pool.indirect_dma_start(nrows[:, c, :], None, flat_d, bass.IndirectOffsetOnAxis(
                        ap=ek1i[:, c:c + 1], axis=1)).then_inc(s_gn, 16)

            @block.vector
            def _(dve):
                own = sem("p_own", at)
                n = [0]

                def link(ins):
                    n[0] += 1
                    ins.then_inc(own, 1)
                    dve.wait_ge(own, n[0])

                steps = [0]

                def step(ins=None):
                    steps[0] += 1
                    ins.then_inc(s_d, 1)
                    dve.wait_ge(s_d, steps[0])

                dve.memset(b2row[:], 0.0).then_inc(s_b, 1)
                dve.memset(X[:, full:, :], 0.0).then_inc(s_z, 1)
                dve.memset(dq[:], 1.0)
                dve.memset(eps[:], EPS)
                link(dve.memset(BLK[:], 0))
                step(dve.memset(ones[:], 1.0))
                dve.wait_ge(s_io, 4)
                dve.tensor_copy(rowi[:], irow[:])
                link(dve.tensor_copy(coli[:], icol[:]))
                dve.tensor_scalar(thr[:], rowi[:, 0:N_BLK + 1], float(P), None, ALU.mult)
                dve.tensor_scalar(tcol[:], coli[:], float(P), None, ALU.mult)
                dve.tensor_scalar(eqd[:], rowi[:], 1.0, coli[:], ALU.add, ALU.is_equal)
                dve.tensor_scalar(equ[:], rowi[:], -1.0, coli[:], ALU.add, ALU.is_equal)
                dve.tensor_scalar(lt[:], rowi[:], coli[:], None, ALU.is_gt)
                link(dve.tensor_scalar(ident[:], rowi[:], coli[:], None, ALU.is_equal))
                link(dve.tensor_tensor(eqd[:], eqd[:], ident[:], ALU.subtract))
                step(dve.tensor_tensor(equ[:], ident[:], equ[:], ALU.subtract))
                dve.wait_ge(s_rows, 16)
                link(dve.tensor_copy(first[:], rows[:, :, 0]))
                link(dve.tensor_tensor(
                    cmp3[:], first[:, None, :].to_broadcast([P, N_BLK + 1, KC]),
                    thr[:, :, None].to_broadcast([P, N_BLK + 1, KC]), ALU.is_lt))
                step(dve.tensor_reduce(cnt1[:], cmp3[:], AX.X, ALU.add))
                dve.wait_ge(s_p, 1)
                link(dve.tensor_scalar(t1[0:N_BLK + 1, :], psm[0:N_BLK + 1, 0:1], -1.0, 0.0, ALU.add, ALU.max))
                step(dve.tensor_copy(t1i[0:N_BLK + 1, :], t1[0:N_BLK + 1, :]))
                dve.wait_ge(s_g1, 16)
                link(dve.tensor_copy(browf[0:N_BLK + 1, :], brow[0:N_BLK + 1, :]))
                link(dve.tensor_scalar(bcmp[0:N_BLK + 1, :], browf[0:N_BLK + 1, :], tcol[0:N_BLK + 1, :],
                                       None, ALU.is_lt))
                link(dve.tensor_reduce(bcnt[0:N_BLK + 1, :], bcmp[0:N_BLK + 1, :], AX.X, ALU.add))
                step(dve.tensor_scalar(start[0:N_BLK + 1, :], t1[0:N_BLK + 1, :], float(P),
                                       bcnt[0:N_BLK + 1, :], ALU.mult, ALU.add))
                dve.wait_ge(s_p, 2)
                link(dve.tensor_scalar(nch[0:N_BLK, :], psm[0:N_BLK, 1:2], float(P - 1), None, ALU.add))
                link(dve.tensor_copy(nci[0:N_BLK, :], nch[0:N_BLK, :]))
                link(dve.tensor_scalar(nci[0:N_BLK, :], nci[0:N_BLK, :], 7, None, ALU.arith_shift_right))
                step(dve.tensor_copy(nch[0:N_BLK, :], nci[0:N_BLK, :]))
                dve.wait_ge(s_p, 3)
                link(dve.tensor_copy(nch[0:N_BLK, :], psm[0:N_BLK, 2:3]))
                link(dve.tensor_scalar(q[0:N_BLK, :], nch[0:N_BLK, :], -float(P), start[0:N_BLK, :],
                                       ALU.mult, ALU.add))
                step(dve.tensor_scalar(GE[0:N_BLK, :], kio[0:N_BLK, :], nch[0:N_BLK, :], None, ALU.is_ge))
                dve.wait_ge(s_p, 4)
                step(dve.tensor_copy(dq[0:N_BLK, 0:1], psm[0:N_BLK, 3:4]))
                dve.wait_ge(s_p, 5)
                link(dve.tensor_tensor(ek[:], kpc[:], psm[:, 4:4 + 2 * KC:2], ALU.add))
                link(dve.tensor_scalar(ek[:], ek[:], float(N_EDGES), None, ALU.min))
                link(dve.tensor_copy(eki[:], ek[:]))
                link(dve.tensor_scalar(ek4i[:], ek[:], float(HEADS), None, ALU.mult))
                step(dve.tensor_scalar(ek1i[:], ek[:], 1.0, None, ALU.add))
                dve.wait_ge(s_p, 6)
                step(dve.tensor_scalar(BK[:].rearrange("p (b k) -> p b k", b=4),
                                       psb[:, :, 0:NK // 4], -1.0, float(P), ALU.add, ALU.mult))
                dve.tensor_scalar(OHB[:], BK[:], tcol[:], None, ALU.is_equal)
                link(dve.tensor_scalar(BLK[:, 2:N_GRP + 2, 0:J], BK[0:1, 0:N_GRP * J].rearrange("o (g j) -> o g j", j=J),
                                       1.0 / P, None, ALU.mult))
                dve.wait_ge(s_x, 48)
                dve.wait_ge(s_z, 1)
                with dve.Fori(0, NB // 13) as i:
                    for b in range(13):
                        one = bass.ds(i * 13 + b, 1)
                        last = dve.bn_stats(st[:, one, :], X[:, one, :])
                    last.then_inc(s_q, 1)
                dve.wait_ge(s_q, NB // 13)
                scales(dve, Chain(dve, sem("p_sc", at)), st, ms[:], nv[:], rs[:], sh[:], sd[:], s_v, s_a, s_r, 0)
                def turn(rows_i, s_rows_in, evacuate, s0, n):
                    dve.wait_ge(s_rows_in, 16 * KC)
                    link(dve.tensor_copy(rowsf[:], rows_i[:]))
                    step(dve.tensor_copy(rowsf[:, 0, :], rows_i[:, 0, :]))
                    for i in range(NTURN):
                        w = min(4, KC - 4 * i) * P
                        dve.wait_ge(s_p, s0 + i)
                        evacuate(slice(512 * i, 512 * i + w), pst[:, i % 2, 0:w]).then_inc(s_e, 1)
                    dve.wait_ge(s_e, (n + 1) * NTURN)

                turn(srows, s_gs, lambda c, t: dve.tensor_copy(SRC[:, c], t), 7, 0)
                step(dve.memset(bcnt[:], 0.0))
                turn(rows, s_gd, lambda c, t: dve.tensor_copy(dstf[:, c], t), 7 + NTURN, 1)
                link(dve.tensor_tensor(KEY[:], dstf[:], BK[:], ALU.subtract))
                link(dve.tensor_scalar(KEY[:], KEY[:], P - 0.5, None, ALU.min))
                dve.tensor_copy(REL[:], KEY[:])
                link(dve.tensor_tensor(KEY[:], KEY[:], BK[:], ALU.add))
                step(dve.tensor_scalar(KEY[:], KEY[:], 2 * BIG, None, ALU.mult))
                dve.wait_ge(s_kl, 16)
                dve.memset(LINK[:, 0:1], -BIG)
                dve.tensor_tensor(LINK[:, 1:], KL[:, 0:NK - 1], KEY[0:1, 1:], ALU.subtract)
                link(dve.tensor_tensor(WHOLE[:], KEY[0:1, :], KL, ALU.subtract))
                dve.wait_ge(s_w, 16 * 21)
                WXh = WX[:, 0:XW].rearrange("p (h c) -> p h c", h=HEADS)
                dve.tensor_copy(WXh[:, :, 0:C_HEAD], wt[:].rearrange("p (h c) -> p h c", h=HEADS))
                dve.tensor_tensor(wm[:, 0, :], wt[:], ats[:], ALU.mult)
                dve.tensor_tensor(wm[:, 1, :], wt[:], atd[:], ALU.mult)
                link(dve.tensor_tensor(wm[:, 2, :], we[:], ate[:], ALU.mult))
                wmh = wm[:].rearrange("p t (h c) -> p t h c", h=HEADS)
                dve.tensor_reduce(WXh[:, :, C_HEAD], wmh[:, 0], AX.X, ALU.add)
                dve.tensor_reduce(WX[:, XW:], wmh[:, 1], AX.X, ALU.add)
                dve.tensor_reduce(mr[:], wmh[:, 2], AX.X, ALU.add)
                link(dve.tensor_scalar(pgi[:], icol[:], 4, None, ALU.arith_shift_right))
                link(dve.tensor_copy(pg[:], pgi[:]))
                link(dve.tensor_scalar(m8[:], rowi[:, 0:8], pg[:], None, ALU.is_equal))
                link(dve.tensor_tensor(BD[:], m8[:, :, None].to_broadcast([P, 8, HEADS]),
                                       mr[:, None, :].to_broadcast([P, 8, HEADS]), ALU.mult))
                dve.wait_ge(s_p, 7 + 2 * NTURN)
                link(dve.tensor_copy(W1T[:].rearrange("p a b -> p (a b)"), psb[:, 0, :]))
                link(dve.tensor_copy(W2T[:].rearrange("p m l o -> p (m l o)"), psb[:, 1, :]))
                turn(nrows, s_gn, lambda c, t: dve.tensor_tensor(
                    LAST[:, c], dstf[:, c], t, ALU.not_equal), 8 + 2 * NTURN, 2)

            @block.tensor
            def _(pe):
                pe.wait_ge(s_d, 3)
                pe.matmul(psm[0:N_BLK + 1, 0:1], cnt1[:], ones[:, 0:1], start=True, stop=True).then_inc(s_p, 1)
                pe.wait_ge(s_d, 5)
                pe.matmul(psm[0:N_BLK, 1:2], eqd[0:N_BLK + 1, 0:N_BLK], start[0:N_BLK + 1, :],
                          start=True, stop=True).then_inc(s_p, 1)
                pe.wait_ge(s_d, 6)
                pe.matmul(psm[0:N_BLK, 2:3], lt[0:N_BLK, 0:N_BLK], nch[0:N_BLK, :],
                          start=True, stop=True).then_inc(s_p, 1)
                pe.wait_ge(s_d, 7)
                pe.matmul(psm[0:N_BLK, 3:4], equ[0:N_BLK, 0:N_BLK], q[0:N_BLK, :],
                          start=True, stop=True).then_inc(s_p, 1)
                pe.wait_ge(s_d, 8)
                for c in range(KC):
                    mm = pe.matmul(psm[:, 4 + 2 * c:6 + 2 * c], GE[0:N_BLK, c * P:(c + 1) * P], dq[0:N_BLK, :],
                                   start=True, stop=True)
                mm.then_inc(s_p, 1)
                for c in range(4):
                    mm = pe.matmul(psb[:, c, 0:NK // 4], ones[0:N_BLK, :], GE[0:N_BLK, c * NK // 4:(c + 1) * NK // 4],
                                   start=True, stop=True)
                mm.then_inc(s_p, 1)
                for t, s in enumerate((11, 13, 15)):
                    if t == 2:
                        pe.wait_ge(s_w, 16 * 21)
                        pe.wait_ge(s_d, 10)
                        for m in range(2):
                            pe.transpose(psb[:, 0, m * P:m * P + P], wl[:, m, :], ident[:])
                            pe.transpose(psb[:, 0, (2 + m) * P:(3 + m) * P], wr[:, m, :], ident[:])
                            pe.transpose(psb[:, 1, 2 * m * P:(2 * m + 1) * P], w2l[:, m * P:m * P + P], ident[:])
                            mm = pe.transpose(psb[:, 1, (2 * m + 1) * P:(2 * m + 2) * P], w2r[:, m * P:m * P + P], ident[:])
                        mm.then_inc(s_p, 1)
                    pe.wait_ge(s_d, s)
                    for i in range(NTURN):
                        if t * NTURN + i >= 2:
                            pe.wait_ge(s_e, t * NTURN + i - 1)
                        for c in range(4 * i, min(4 * i + 4, KC)):
                            mm = pe.transpose(pst[:, i % 2, (c % 4) * P:(c % 4) * P + P], rowsf[:, c, :], ident[:])
                        mm.then_inc(s_p, 1)

        stage(prepare)
        def gather_sums(table, edge_terms):
            def body(at, block):
                s_i = sem("g_i", at)
                s_g = [sem(f"g_g{u}", at) for u in range(2)]
                s_o = sem("g_o", at)
                s_m = sem("g_m", at)
                s_c = sem("g_c", at)
                s_one = sem("g_one", at)
                own = sem("g_own", at)
                idx = sb("idx", [P, 2, J], I32, at)
                G = sb("G", [P, 2, J, D + 1], F32, at)
                OH = sb("OH", [P, 2, J, P], F32, at)
                psu = ps("psu", [P, 2, 512], at)
                if edge_terms:
                    s_at = [sem(f"e_at{u}", at) for u in range(2)]
                    s_et = sem("e_t", at)
                    s_ec = sem("e_c", at)
                    s_em = sem("e_m", at)
                    s_eo = sem("e_o", at)
                    s_es = sem("e_s", at)
                    at_in = sb("at_in", [P, 2, ES * D_EDGE], F32, at)
                    at_t = sb("at_t", [P, 4, P], F32, at)
                    ae_o = sb("ae_o", [P, ES * HEADS], F32, at)
                    pet = ps("pet", [P, 4, P], at)
                    pem = ps("pem", [P, 512], at)
                    attr = edge_attr.rearrange("(p e) d -> p (e d)", p=EP)
                    aeo = ae_tab[0:N_EDGES * HEADS].rearrange("(p e) -> p e", p=EP)

                @block.gpsimd
                def _(pool):
                    with pool.Fori(0, N_GRP // 2) as i:
                        for u in range(2):
                            g = 2 * i + u
                            pool.wait_ge(s_i, g + 1)
                            hold(pool, s_m, g * NT + NT)
                            for j in range(J):
                                pool.indirect_dma_start(
                                    G[:, u, j, 0:D], None, table, bass.IndirectOffsetOnAxis(
                                        ap=idx[:, u, j:j + 1], axis=0)).then_inc(s_g[u], 16)

                if edge_terms:
                    @block.sync
                    def _(sp):
                        with sp.Fori(0, E_STEPS // 2) as i:
                            for u in range(2):
                                t = 2 * i + u
                                sp.wait_ge(s_et, t + 1)
                                sp.dma_start(at_in[0:EP, u, :], attr[:, bass.ds(t * ES * D_EDGE, ES * D_EDGE)]
                                             ).then_inc(s_at[u], 16)

                @block.scalar
                def _(act):
                    def group(i, u, terms):
                        g = 2 * i + u
                        act.wait_ge(s_m, g * NT + 2 * NT)
                        act.copy(idx[:, 1 - u, :], SRC[:, bass.ds(g * J + J, J)]).then_inc(s_i, 1)
                        if terms:
                            act.wait_ge(s_et, g + 3)
                            act.copy(at_t[:, :, 0:EP], pet[:, :, 0:EP]).then_inc(s_ec, 1)
                            act.wait_ge(s_em, g + 1)
                            act.copy(ae_o[0:EP, :], pem[0:EP, 0:ES * HEADS]).then_inc(s_eo, 1)
                            act.wait_ge(s_eo, g + 2)
                            act.dma_start(aeo[:, bass.ds(g * ES * HEADS, ES * HEADS)],
                                          ae_o[0:EP, :]).then_inc(s_es, 16)
                            act.wait_ge(s_es, 16 * (g + 1))

                    act.copy(idx[:, 0, :], SRC[:, 0:J]).then_inc(s_i, 1)
                    done = E_STEPS // 2 if edge_terms else 0
                    if edge_terms:
                        with act.Fori(0, done) as i:
                            for u in range(2):
                                group(i, u, True)
                    with act.Fori(done, N_GRP // 2) as i:
                        for u in range(2):
                            group(i, u, False)

                @block.tensor
                def _(pe):
                    def group(i, u, terms):
                        g = 2 * i + u
                        if terms:
                            pe.wait_ge(s_at[u], 16 * (i + 1))
                            pe.wait_ge(s_eo, g + 1)
                            for n in range(4):
                                mm = pe.transpose(pet[:, n, 0:EP], at_in[0:EP, u, n * P:n * P + P],
                                                  ident[0:EP, 0:EP])
                            mm.then_inc(s_et, 1)
                        pe.wait_ge(s_g[u], 16 * J * (i + 1))
                        pe.wait_ge(s_o, g + 1)
                        for t in range(NT):
                            pe.wait_ge(s_c, g * NT + t + 1)
                            for j in range(TRI * t, TRI * t + TRI):
                                k = (NT * u + t) % 2, (j % TRI) * MW
                                mm = pe.matmul(psu[:, k[0], k[1]:k[1] + D + 1], OH[:, u, j, :], G[:, u, j, :],
                                               start=True, stop=True)
                            mm.then_inc(s_m, 1)
                            if terms and t == 1:
                                pe.wait_ge(s_ec, g + 1)
                                for n in range(4):
                                    mm = pe.matmul(pem[0:EP, n * 32:n * 32 + 32], at_t[:, n, 0:EP],
                                                   BD[:].rearrange("p e h -> p (e h)"), start=True, stop=True)
                                mm.then_inc(s_em, 1)

                    pe.sem_inc(s_m, 2 * NT)
                    done = E_STEPS // 2 if edge_terms else 0
                    pe.wait_ge(s_one, 1)
                    if edge_terms:
                        pe.sem_inc(s_et, 2)
                        pe.sem_inc(s_eo, 1)
                        with pe.Fori(0, done) as i:
                            for u in range(2):
                                group(i, u, True)
                    with pe.Fori(done, N_GRP // 2) as i:
                        for u in range(2):
                            group(i, u, False)

                @block.vector
                def _(dve):
                    def one_hot(g, u):
                        dve.wait_ge(s_m, g * NT + NT)
                        dve.tensor_tensor(OH[:, u], rowi[:, None, :].to_broadcast([P, J, P]),
                                          REL[:, bass.ds(g * J, J)][:, :, None].to_broadcast([P, J, P]),
                                          ALU.is_equal).then_inc(s_o, 1)

                    dve.memset(G[:, :, :, D:], 1.0).then_inc(s_one, 1)
                    dve.memset(ACC[:], 0.0).then_inc(s_one, 1)
                    dve.wait_ge(s_one, 2)
                    dve.sem_inc(s_c, 2)
                    dve.wait_ge(s_m, NT)
                    dve.tensor_tensor(OH[:, 0], rowi[:, None, :].to_broadcast([P, J, P]),
                                      REL[:, 0:J][:, :, None].to_broadcast([P, J, P]),
                                      ALU.is_equal).then_inc(s_o, 1)
                    with dve.Fori(0, N_GRP // 2) as i:
                        for u in range(2):
                            g = 2 * i + u
                            one_hot(g + 1, 1 - u)
                            c = Chain(dve, own, i, 2 * (J - NT))
                            c.n = u * (J - NT)
                            for j in range(J):
                                if j % 8 == 0:
                                    _, blk = nc.values_load_multi_w_load_instructions(
                                        BLK[0:1, bass.ds(g + 2, 1), j:j + 8], engines=DVE_ONLY,
                                        min_val=0, max_val=NB - 1)
                                if j % TRI == 0:
                                    dve.wait_ge(s_m, g * NT + j // TRI + 1 + 2 * NT)
                                a = ACC[:, bass.ds(blk[j % 8], 1), 0:D + 1]
                                k = (NT * u + j // TRI) % 2, (j % TRI) * MW
                                add = dve.tensor_tensor(a, psu[:, k[0], k[1]:k[1] + D + 1][:, None, :], a, ALU.add)
                                if j % TRI == TRI - 1:
                                    add.then_inc(s_c, 1)
                                    dve.wait_ge(s_c, g * NT + j // TRI + 3)
                                else:
                                    c.link(add)
            return body

        stage(gather_sums(h_tab, True))

        def hidden(at, block):
            PAIR = 2
            NP2 = NB // PAIR
            HU = 4
            assert (NP2 - 2) % HU == 0
            s_a = sem("d_a", at)
            s_s = sem("d_s", at)
            s_t = sem("d_t", at)
            s_e = sem("d_e", at)
            s_p = sem("d_p", at)
            s_h = sem("d_h", at)
            s_o = sem("d_o", at)
            s_y = sem("d_y", at)
            s_b = sem("d_b", at)
            s_r = sem("d_r", at)
            s_d = sem("d_d", at)
            s_f = sem("d_f", at)
            s_ag = sem("d_ag", at)
            s_at = sem("d_at", at)
            s_ac = sem("d_ac", at)
            own = sem("d_own", at)
            A2 = sb("A2", [P, 2, PAIR, D], F32, at)
            H2 = sb("H2", [P, 2, PAIR, D], F32, at)
            TT = sb("TT", [P, 2, 2 * PAIR * D], F32, at)
            HID = sb("HID", [P, 2, 2, PAIR * P], F32, at)
            Y2 = sb("Y2", [P, 2, PAIR, D], F32, at)
            CNT = sb("CNT", [P, NB], F32, at)
            b2all = sb("b2all", [P, D], F32, at)
            aer = sb("aer", [P, KC, P * HEADS], F32, at)
            pt = ps("pt", [P, 2, 512], at)
            ph = ps("ph", [P, 2, 512], at)
            po = ps("po", [P, 2, 512], at)
            ytab = y_tab.rearrange("(b p) f -> p b f", p=P)

            @block.sync
            def _(sp):
                sp.dma_start(b2all[:], b2.rearrange("(o f) -> o f", o=1).to_broadcast([P, D])).then_inc(s_r, 16)
                sp.sem_inc(s_f, 2)
                with sp.Fori(0, NP2 // 2) as i:
                    for u in range(2):
                        t = 2 * i + u
                        sp.wait_ge(s_y, t + 3)
                        sp.dma_start(ytab[:, bass.ds(t * PAIR, PAIR), :], Y2[:, u]).then_inc(s_d, 16)
                        sp.wait_ge(s_d, 16 * (t + 1))
                        sp.sem_inc(s_f, 1)

            @block.gpsimd
            def _(pool):
                pool.wait_ge(s_r, 16)
                with pool.Fori(0, NP2) as t:
                    hold(pool, s_s, t + 1)
                    pair = bass.ds(t * PAIR, PAIR)
                    pool.tensor_tensor(H[:, pair, 0:D], H[:, pair, 0:D],
                                       b2all[:, None, :].to_broadcast([P, PAIR, D]), ALU.add).then_inc(s_b, 1)
                flat = ae_tab.rearrange("(o e) -> o e", o=1)
                for c in range(KC):
                    pool.indirect_dma_start(aer[:, c, :], None, flat, bass.IndirectOffsetOnAxis(
                        ap=ek4i[:, c:c + 1], axis=1)).then_inc(s_ag, 16)

            @block.scalar
            def _(act):
                def stage_h(t, u):
                    act.copy(H2[:, u], H[:, bass.ds(t * PAIR, PAIR), 0:D]).then_inc(s_s, 1)

                def step(t, u, ahead=True, following=True):
                    if ahead:
                        hold(act, s_t, t + 1)
                        stage_h(t + 2, u)
                    if following:
                        act.wait_ge(s_t, t + 2)
                        act.wait_ge(s_p, t + 1)
                        act.copy(TT[:, 1 - u], pt[:, 1 - u]).then_inc(s_e, 1)
                    act.wait_ge(s_p, t + 2)
                    act.wait_ge(s_o, t + 1)
                    for m in range(2):
                        last = act.activation(HID[:, u, m], ph[:, u, m * 256:(m + 1) * 256], ACT.Relu,
                                              bias=b1c[:, m:m + 1])
                    last.then_inc(s_h, 1)

                stage_h(0, 0)
                stage_h(1, 1)
                act.wait_ge(s_t, 1)
                act.copy(TT[:, 0], pt[:, 0]).then_inc(s_e, 1)
                with act.Fori(0, (NP2 - 2) // HU) as i:
                    for u in range(HU):
                        step(HU * i + u, u % 2)
                step(NP2 - 2, 0, ahead=False)
                step(NP2 - 1, 1, ahead=False, following=False)
                for n in range(KC):
                    act.wait_ge(s_at, n + 1)
                    act.copy(AE[:, :, n * P:(n + 1) * P], pt[:, n % 2].rearrange("p (h k) -> p h k", h=HEADS)
                             ).then_inc(s_ac, 1)

            @block.tensor
            def _(pe):
                def turn(t, u, fresh=False):
                    pe.wait_ge(s_a, t + 1)
                    pe.wait_ge(s_s, t + 1)
                    if not fresh:
                        pe.wait_ge(s_e, t - 1)
                    for n in range(PAIR):
                        pe.transpose(pt[:, u, n * P:n * P + P], A2[:, u, n], ident[:])
                        mm = pe.transpose(pt[:, u, (PAIR + n) * P:(PAIR + n + 1) * P], H2[:, u, n], ident[:])
                    mm.then_inc(s_t, 1)

                def first(t, u):
                    pe.wait_ge(s_e, t + 1)
                    pe.wait_ge(s_h, t)
                    for m in range(2):
                        o = ph[:, u, m * 256:(m + 1) * 256]
                        pe.matmul(o, W1T[:, 0, m * P:m * P + P], TT[:, u, 0:256], start=True, stop=False)
                        mm = pe.matmul(o, W1T[:, 1, m * P:m * P + P], TT[:, u, 256:512], start=False, stop=True)
                    mm.then_inc(s_p, 1)

                def second(t, u):
                    pe.wait_ge(s_h, t + 2)
                    pe.wait_ge(s_y, t + 1)
                    for n in range(PAIR):
                        for m in range(2):
                            mm = pe.matmul(po[:, u, n * 256:(n + 1) * 256], HID[:, u, m, n * P:n * P + P],
                                           W2T[:, m].rearrange("p l o -> p (l o)"), start=(m == 0), stop=(m == 1))
                    mm.then_inc(s_o, 1)

                pe.sem_inc(s_p, 1)
                pe.sem_inc(s_h, 1)
                pe.sem_inc(s_o, 2)
                turn(0, 0, fresh=True)
                turn(1, 1, fresh=True)
                first(0, 0)
                with pe.Fori(0, (NP2 - 2) // HU) as i:
                    for u in range(HU):
                        t = HU * i + u
                        turn(t + 2, u % 2)
                        first(t + 1, (u + 1) % 2)
                        second(t, u % 2)
                first(NP2 - 1, 1)
                second(NP2 - 2, 0)
                second(NP2 - 1, 1)
                pe.wait_ge(s_ag, 16 * KC)
                for n in range(KC):
                    if n >= 2:
                        pe.wait_ge(s_ac, n - 1)
                    row = aer[:, n, :].rearrange("k (e h) -> k h e", h=HEADS)
                    for h in range(HEADS):
                        mm = pe.transpose(pt[:, n % 2, h * P:h * P + P], row[:, h], ident[:])
                    mm.then_inc(s_at, 1)

            @block.vector
            def _(dve):
                c = Chain(dve, own)
                c.link(dve.tensor_copy(CNT[:], ACC[:, :, D]))
                c.link(dve.tensor_scalar(RCNT[:], CNT[:], 1.0, None, ALU.max))
                c.link(dve.reciprocal(RCNT[:], RCNT[:]))
                c.link(dve.tensor_scalar(NOEDGE[:], CNT[:], 0.5, -BIG, ALU.is_lt, ALU.mult))

                def mean(t, u):
                    dve.tensor_tensor(A2[:, u], ACC[:, bass.ds(t * PAIR, PAIR), 0:D],
                                      RCNT[:, bass.ds(t * PAIR, PAIR)][:, :, None].to_broadcast([P, PAIR, D]),
                                      ALU.mult).then_inc(s_a, 1)

                def finish(t, u):
                    o = po[:, u].rearrange("p (n l o) -> p n l o", n=PAIR, l=2)
                    dve.wait_ge(s_o, t + 3)
                    hold(dve, s_f, t + 1)
                    dve.tensor_copy(Y2[:, u], o[:, :, 0])
                    dve.wait_ge(s_b, t + 1)
                    h = H[:, bass.ds(t * PAIR, PAIR), 0:D]
                    dve.tensor_tensor(h, o[:, :, 1], h, ALU.add).then_inc(s_y, 1)

                dve.sem_inc(s_y, 2)
                mean(0, 0)
                mean(1, 1)
                dve.wait_ge(s_t, 1)
                mean(2, 0)

                def step(t, u):
                    dve.wait_ge(s_t, t + 2)
                    mean(t + 3, 1 - u)
                    finish(t, u)
                looped = (NP2 - 3) // HU * HU
                with dve.Fori(0, looped // HU) as i:
                    for u in range(HU):
                        step(HU * i + u, u % 2)
                for t in range(looped, NP2 - 3):
                    step(t, t % 2)
                for t in range(NP2 - 3, NP2):
                    finish(t, t % 2)

        stage(hidden)
        stage(gather_sums(y_tab, False))

        def second_norm(at, block):
            NQ = NB // QUAD
            s_v = sem("s_v", at)
            s_a = sem("s_a", at)
            s_r = sem("s_r", at)
            s_z = sem("s_z", at)
            s_b = sem("s_b", at)
            s_u = sem("s_u", at)
            TEN = 13
            assert NB % TEN == 0
            s_f = sem("s_f", at)
            s_h = sem("s_h", at)
            s_t = sem("s_t", at)
            s_e = sem("s_e", at)
            s_p = sem("s_p", at)
            s_x = sem("s_x", at)
            s_d = sem("s_d", at)
            s_q = sem("s_q", at)
            s_zz = sem("s_zz", at)
            own = sem("s_own", at)
            st = sb("st", [P, NB, 6], F32, at)
            nv = sb("nv", [P, NB], F32, at)
            ms = sb("ms", [P, NB], F32, at)
            sd = sb("sd", [P, NB], F32, at)
            rs = sb("rs", [P, 2, NB], F32, at)
            sh = sb("sh", [P, 2, NB], F32, at)
            U = sb("U", [P, 2, QUAD, D], F32, at)
            V = sb("V", [P, 2, QUAD, D], F32, at)
            HT = sb("HT", [P, 2, QUAD * P], F32, at)
            pt = ps("pt", [P, 2, 512], at)
            pw = ps("pw", [P, 2, 2, 512], at)
            WA = XW + HEADS
            tab = x_tab.rearrange("(b p) f -> p b f", p=P)

            @block.sync
            def _(sp):
                with sp.Fori(0, NQ) as i:
                    sp.wait_ge(s_f, i + 1)
                    quad = bass.ds(i * QUAD, QUAD)
                    sp.dma_start(x_keep[:, quad, :], X[:, quad, :]).then_inc(s_d, 16)
                with sp.Fori(0, NQ) as i:
                    sp.wait_ge(s_x, i + 3)
                    quad = bass.ds(i * QUAD, QUAD)
                    sp.dma_start(tab[:, quad, :], H[:, quad, :]).then_inc(s_d, 16)
                sp.wait_ge(s_d, 32 * NQ)

            def quads(eng, step, n=2):
                with eng.Fori(0, NQ // n) as i:
                    for u in range(n):
                        step(n * i + u, u)
                step(NQ - 1, 0)

            @block.gpsimd
            def _(pool):
                with pool.Fori(0, NQ) as i:
                    x4 = X[:, bass.ds(i * QUAD, QUAD), :]
                    pool.tensor_tensor(x4, x4, bet[:, None, :].to_broadcast([P, QUAD, D]), ALU.add).then_inc(s_b, 1)

            @block.scalar
            def _(act):
                def scaled(out_, in_, b, n, func):
                    one = bass.ds(b, 1)
                    return act.activation(out_, in_, func, bias=sh[:, n, one], scale=rs[:, n, one])

                act.wait_ge(s_v, 1)
                act.activation(sd[:], nv[:], ACT.Sqrt, bias=eps[:], scale=1.0 / D).then_inc(s_a, 1)
                act.wait_ge(s_r, 1)
                with act.Fori(0, NQ) as i:
                    for n in range(QUAD):
                        a = ACC[:, bass.ds(i * QUAD + n, 1), 0:D]
                        last = scaled(a, a, i * QUAD + n, 0, ACT.Identity)
                    last.then_inc(s_z, 1)
                act.wait_ge(s_v, 2)
                act.activation(sd[:], nv[:], ACT.Sqrt, bias=eps[:], scale=1.0 / D).then_inc(s_a, 1)
                act.wait_ge(s_r, 2)

                def step(q, u):
                    act.wait_ge(s_t, q + 1)
                    for n in range(QUAD):
                        last = scaled(V[:, u, n:n + 1], X[:, bass.ds(q * QUAD + n, 1), :], q * QUAD + n, 1, ACT.Relu)
                    last.then_inc(s_h, 1)
                quads(act, step)

            @block.tensor
            def _(pe):
                def turn(q, u):
                    pe.wait_ge(s_h, q + 1)
                    pe.wait_ge(s_e, q + 1)
                    for n in range(QUAD):
                        mm = pe.transpose(pt[:, u, n * P:n * P + P], V[:, u, n], ident[:])
                    mm.then_inc(s_t, 1)

                def product(q, u):
                    pe.wait_ge(s_e, q + 3)
                    pe.wait_ge(s_x, q + 1)
                    for n in range(QUAD):
                        mm = pe.matmul(pw[:, u, n // 2, (n % 2) * WA:(n % 2 + 1) * WA], HT[:, u, n * P:n * P + P],
                                       WX[:], start=True, stop=True)
                    mm.then_inc(s_p, 1)

                pe.sem_inc(s_t, 2)
                pe.sem_inc(s_x, 2)
                pe.sem_inc(s_e, 2)
                pe.sem_inc(s_p, 2)
                turn(0, 0)
                with pe.Fori(0, NQ // 2) as i:
                    for u in range(2):
                        turn(2 * i + u + 1, (u + 1) % 2)
                        product(2 * i + u, u)
                product(NQ - 1, 0)

            @block.vector
            def _(dve):
                wide = [P, QUAD, D]

                c = Chain(dve, own)
                with dve.Fori(0, NB // TEN) as i:
                    k = Chain(dve, s_zz, i, 1)
                    for b in range(TEN):
                        one = bass.ds(i * TEN + b, 1)
                        a = ACC[:, one, 0:D]
                        last = dve.scalar_tensor_tensor(a, a, RCNT[:, one], H[:, one, 0:D], ALU.mult, ALU.add)
                    k.link(last, alone=True)
                    for b in range(TEN):
                        one = bass.ds(i * TEN + b, 1)
                        last = dve.bn_stats(st[:, one, :], ACC[:, one, 0:D])
                    last.then_inc(s_q, 1)
                    k.end()
                dve.wait_ge(s_q, NB // TEN)
                scales(dve, c, st, ms[:], nv[:], rs[:, 0], sh[:, 0], sd[:], s_v, s_a, s_r, 0)

                def step(q, u):
                    quad = bass.ds(q * QUAD, QUAD)
                    dve.wait_ge(s_z, q + 1)
                    dve.tensor_tensor(U[:, u], ACC[:, quad, 0:D], gam[:, None, :].to_broadcast(wide), ALU.mult
                                      ).then_inc(s_u, 1)
                    dve.wait_ge(s_b, q + 1)
                    dve.wait_ge(s_u, q + 1)
                    dve.tensor_tensor(X[:, quad, :], X[:, quad, :], U[:, u], ALU.add).then_inc(s_f, 1)

                def stats(q):
                    hold(dve, s_f, q + 1)
                    for b in range(QUAD):
                        one = bass.ds(q * QUAD + b, 1)
                        last = dve.bn_stats(st[:, one, :], X[:, one, :])
                    last.then_inc(s_q, 1)
                with dve.Fori(0, NQ // 2) as i:
                    step(2 * i, 0)
                    step(2 * i + 1, 1)
                    stats(2 * i)
                    stats(2 * i + 1)
                step(NQ - 1, 0)
                stats(NQ - 1)
                dve.wait_ge(s_q, NB // TEN + NQ)
                scales(dve, c, st, ms[:], nv[:], rs[:, 1], sh[:, 1], sd[:], s_v, s_a, s_r, 1)

                def step(q, u):
                    dve.wait_ge(s_t, q + 3)
                    dve.tensor_copy(HT[:, u], pt[:, u]).then_inc(s_e, 1)

                def store(q, u):
                    dve.wait_ge(s_p, q + 3)
                    o = pw[:, u, :, 0:2 * WA].rearrange("p a (b w) -> p a b w", b=2)
                    for n in range(2):
                        dve.tensor_copy(H[:, bass.ds(q * QUAD + 2 * n, 2), :], o[:, n, :, 0:XW])
                    for n in range(2):
                        last = dve.tensor_copy(ADST[:, bass.ds(q * QUAD + 2 * n, 2), :], o[:, n, :, XW:])
                    last.then_inc(s_x, 1)
                step(0, 0)
                with dve.Fori(0, NQ // 2) as i:
                    for u in range(2):
                        step(2 * i + u + 1, (u + 1) % 2)
                        store(2 * i + u, u)
                store(NQ - 1, 0)
                dve.wait_ge(s_x, NQ + 2)
                dve.tensor_tensor(SELF[:], H[:].rearrange("p b (h c) -> p b h c", h=HEADS)[:, :, :, C_HEAD], ADST[:],
                                  ALU.add)

        stage(second_norm)
        XS.close()

        def attention(at, block):
            R = J * HEADS
            UN = 12
            assert N_GRP % UN == 0
            s_i = sem("a_i", at)
            s_g = [sem(f"a_g{u}", at) for u in range(3)]
            s_o = sem("a_o", at)
            s_m = sem("a_m", at)
            s_c = sem("a_c", at)
            s_kb = sem("a_kb", at)
            s_kc = sem("a_kc", at)
            s_mk = sem("a_mk", at)
            s_tr = sem("a_tr", at)
            s_te = sem("a_te", at)
            s_x = sem("a_x", at)
            s_l = sem("a_l", at)
            s_lt = sem("a_lt", at)
            s_cm = sem("a_cm", at)
            s_row = sem("a_row", at)
            s_cc = sem("a_cc", at)
            s_col = sem("a_col", at)
            s_r = sem("a_r", at)
            s_rt = sem("a_rt", at)
            s_fd = sem("a_fd", at)
            s_f = sem("a_f", at)
            s_fm = sem("a_fm", at)
            s_fx = sem("a_fx", at)
            s_dl = sem("a_dl", at)
            s_p = sem("a_p", at)
            s_ms = sem("a_ms", at)
            s_mp = sem("a_mp", at)
            s_one = sem("a_one", at)
            s_at = sem("a_at", at)
            s_ac = sem("a_ac", at)
            s_ad = sem("a_ad", at)
            s_ae = sem("a_ae", at)
            AD = sb("AD", [P, HEADS, NK], F32, at)
            ADT = sb("ADT", [NB, HEADS, P], F32, at)
            ADG = sb("ADG", [P, J, HEADS], F32, at)
            own = sem("a_own", at)
            idx = sb("idx", [P, 3, J], I32, at)
            G = sb("G", [P, 3, J, XW], F32, at)
            OH = sb("OH", [P, 4, J, P], F32, at)
            OHT = sb("OHT", [P, J, P], F32, at)
            MSG = sb("MSG", [P, 2, J, MW], F32, at)
            KB = sb("KB", [P, HEADS, J], F32, at)
            L = sb("L", [P, HEADS, J], F32, at)
            DL = sb("DL", [P, HEADS, J], F32, at)
            PR = sb("PR", [P, HEADS, J], F32, at)
            KT = sb("KT", [R, P], F32, at)
            MS = sb("MS", [R, P + 1], F32, at)
            FS = sb("FS", [R, P], F32, at)
            LS = sb("LS", [R, P], F32, at)
            FW = sb("FW", [R, P], F32, at)
            CM = sb("CM", [R, P], F32, at)
            rows = sb("rows", [1, 2, HEADS, J], F32, at)
            wa = sb("wa", [1, HEADS, J], F32, at)
            wb = sb("wb", [1, HEADS, J], F32, at)
            cin = sb("cin", [1, HEADS, J], F32, at)
            cbk = sb("cbk", [1, HEADS, J], F32, at)
            aa = sb("aa", [1, HEADS, J], F32, at)
            ab = sb("ab", [1, HEADS, J], F32, at)
            last_m = sb("last_m", [1, HEADS], F32, at)
            f0 = sb("f0", [1, HEADS], F32, at)
            f1 = sb("f1", [1, HEADS], F32, at)
            pt = ps("pt", [P, 2, 512], at)
            pu = ps("pu", [P, 3, 512], at)
            px = ps("px", [P, 512], at)
            pl = ps("pl", [P, 512], at)
            pc = ps("pc", [P, 512], at)
            pk = pt[0:R, 1, 384:512]
            assert J == 15
            ws = sb("ws", [1, J], F32, at)
            OHF = OHT[:].rearrange("p j f -> p (j f)")[0:NB, 0:NK]
            px_l = px[:, 0:R].rearrange("p (h j) -> p h j", h=HEADS)
            pm = pc[:, 192:192 + R].rearrange("p (h j) -> p h j", h=HEADS)
            pf = px[:, 256:256 + HEADS]
            CQ, CW = 4, NK // 4
            NF = -(-J // 4)

            def jh(t):
                return t.rearrange("p h j -> p j h")

            def steps(eng, body):
                with eng.Fori(0, N_GRP // UN) as i:
                    for u in range(UN):
                        body(i, u, UN * i + u)

            @block.gpsimd
            def _(pool):
                def step(i, u, g):
                    pool.wait_ge(s_i, g + 1)
                    hold(pool, s_ms, g + 1)
                    for j in range(J):
                        pool.indirect_dma_start(
                            G[:, u % 3, j, :], None, x_tab, bass.IndirectOffsetOnAxis(
                                ap=idx[:, u % 3, j:j + 1], axis=0)).then_inc(s_g[u % 3], 16)
                steps(pool, step)

            @block.scalar
            def _(act):
                def keys(g):
                    act.copy(KB[:], KEY[:, bass.ds(g * J, J)][:, None, :].to_broadcast([P, HEADS, J])
                             ).then_inc(s_kb, 1)

                def turned(g):
                    act.wait_ge(s_x, g + 1)
                    act.copy(ADG[:].rearrange("p j h -> p h j"), AD[:, :, bass.ds(g * J, J)])
                    for n in range(NF):
                        w = min(4, J - 4 * n)
                        act.wait_ge(s_tr, g * NF + n + 1)
                        if n == NF - 1:
                            act.wait_ge(s_mk, g + 1)
                            act.copy(KT[:], pk).then_inc(s_kc, 1)
                        act.copy(OHT[:, 4 * n:4 * n + w, :].rearrange("p a b -> p (a b)"), pt[:, n % 2, 0:w * P]
                                 ).then_inc(s_te, 1)

                for n in range(2):
                    act.copy(idx[:, n, :], SRC[:, n * J:(n + 1) * J]).then_inc(s_i, 1)
                act.wait_ge(s_at, 1)
                act.copy(ADT[:].rearrange("b h p -> b (h p)"), pl[0:NB, :]).then_inc(s_ac, 1)
                for n in range(HEADS * CQ):
                    act.wait_ge(s_ad, n + 1)
                    act.copy(AD[:, n // CQ, (n % CQ) * CW:(n % CQ + 1) * CW], pu[:, n % 2, 0:CW]).then_inc(s_ae, 1)
                act.wait_ge(s_ae, HEADS * CQ)
                keys(0)
                turned(0)

                def step(i, u, g):
                    act.copy(ws[:], WHOLE[:, bass.ds(g * J, J)])
                    act.wait_ge(s_l, g + 1)
                    act.copy(idx[:, (u + 2) % 3, :], SRC[:, bass.ds((g + 2) * J, J)]).then_inc(s_i, 1)
                    keys(g + 1)
                    turned(g + 1)
                    act.wait_ge(s_fx, g + 1)
                    act.copy(MSG[:, u % 2, :, XW + HEADS:], jh(AE[:, :, bass.ds(g * J, J)]))
                    act.wait_ge(s_fd, g + 1)
                    act.activation(f1[:], f0[:], ACT.Exp).then_inc(s_f, 1)
                    act.wait_ge(s_dl, g + 1)
                    act.activation(PR[:], DL[:], ACT.Exp).then_inc(s_p, 1)
                    act.wait_ge(s_p, g + 2)
                    act.copy(MSG[:, u % 2, :, C_HEAD:XW:HW], jh(PR[:])).then_inc(s_mp, 1)
                steps(act, step)

            @block.tensor
            def _(pe):
                def turn_one_hot(g, u, banks):
                    for n in banks:
                        if n == 0:
                            pe.wait_ge(s_o, g + 1)
                        pe.wait_ge(s_te, g * NF + n + 1)
                        for j in range(4 * n, min(4 * n + 4, J)):
                            mm = pe.transpose(pt[:, n % 2, (j % 4) * P:(j % 4 + 1) * P], OH[:, u % 4, j, :], ident[:])
                        if n == NF - 1:
                            hold(pe, s_kb, g + 1)
                            mm = pe.transpose(pk, KB[:].rearrange("p h j -> p (h j)"), ident[:])
                        mm.then_inc(s_tr, 1)

                def spread(g, chunks):
                    if chunks[0] == 0:
                        pe.wait_ge(s_l, g + 1)
                    for j in chunks:
                        if j % 4 == 0:
                            pe.wait_ge(s_te, g * NF + j // 4 + 3)
                        mm = pe.matmul(px_l[:, :, j], OHT[:, j, :], ADG[:, j, :], start=True, stop=True)
                    if chunks[-1] == J - 1:
                        mm.then_inc(s_x, 1)

                def sums(g, u, banks):
                    for t in banks:
                        pe.wait_ge(s_c, (g + 2) * J + (t + 1) * TRI)
                        for j in range(TRI * t, TRI * t + TRI):
                            k = (NT * (u + 2) + t) % 3, (j % TRI) * MW
                            mm = pe.matmul(pu[:, k[0], k[1]:k[1] + MW], OH[:, u % 4, j, :], MSG[:, u % 2, j, :],
                                           start=True, stop=True)
                        mm.then_inc(s_m, 1)

                pe.sem_inc(s_x, 1)
                for h in range(HEADS):
                    mm = pe.transpose(pl[0:NB, h * P:h * P + P], ADST[:, :, h], ident[:])
                mm.then_inc(s_at, 1)
                pe.wait_ge(s_one, 1)
                pe.wait_ge(s_ac, 1)
                for n in range(HEADS * CQ):
                    if n >= 2:
                        pe.wait_ge(s_ae, n - 1)
                    pe.matmul(pu[:, n % 2, 0:CW], ADT[:, n // CQ, :], OHF[:, (n % CQ) * CW:(n % CQ + 1) * CW],
                              start=True, stop=True).then_inc(s_ad, 1)
                pe.wait_ge(s_ae, HEADS * CQ)
                turn_one_hot(0, 0, range(NF))
                spread(0, range(J))
                sums(-2, -2, range(4))

                def step(i, u, g):
                    hold(pe, s_l, g + 2)
                    pe.transpose(pl[0:R, 0:P], L[:].rearrange("p h j -> p (h j)"), ident[:]).then_inc(s_lt, 1)
                    sums(g - 2, u - 2, (4,))
                    turn_one_hot(g + 1, u + 1, (0,))
                    hold(pe, s_cm, g + 1)
                    pe.matmul(pc[0:1, 0:R], CM[:, 0:1], ident[0:R, 0:R], start=True, stop=True)
                    pe.matmul(pc[0:1, R:2 * R], CM[:, P - 1:P], ident[0:R, 0:R],
                              start=True, stop=True).then_inc(s_row, 1)
                    turn_one_hot(g + 1, u + 1, range(1, NF))
                    pe.wait_ge(s_mp, g + 1)
                    pe.wait_ge(s_ms, g + 3)
                    sums(g - 1, u - 1, (0, 1, 2))
                    pe.wait_ge(s_cc, g + 1)
                    pe.matmul(pc[0:R, 128:129], cin[:].rearrange("o h j -> o (h j)"), ones[0:1, 0:1],
                              start=True, stop=True)
                    pe.matmul(pc[0:R, 129:130], cbk[:].rearrange("o h j -> o (h j)"), ones[0:1, 0:1],
                              start=True, stop=True).then_inc(s_col, 1)
                    spread(g + 1, range(4))
                    hold(pe, s_r, g + 1)
                    pe.transpose(pc[:, 192:192 + R], CM[:], ident[0:R, 0:R]).then_inc(s_rt, 1)
                    spread(g + 1, range(4, J - 1))
                    pe.wait_ge(s_fm, g + 1)
                    pe.matmul(pf, OH[0:1, u % 4, 0, :], f1[:], start=True, stop=True).then_inc(s_fx, 1)
                    spread(g + 1, (J - 1,))
                    sums(g - 1, u - 1, (3,))
                steps(pe, step)
                sums(N_GRP - 2, UN - 2, (4,))
                pe.wait_ge(s_ms, N_GRP + 3)
                pe.wait_ge(s_mp, N_GRP + 1)
                sums(N_GRP - 1, UN - 1, range(NT))

            @block.vector
            def _(dve):
                def one_hot(g, u):
                    dve.tensor_tensor(OH[:, u % 4], rowi[:, None, :].to_broadcast([P, J, P]),
                                      REL[:, bass.ds(g * J, J)][:, :, None].to_broadcast([P, J, P]),
                                      ALU.is_equal).then_inc(s_o, 1)

                def messages(g, u):
                    dve.wait_ge(s_p, g + 2)
                    dve.tensor_tensor(MSG[:, u % 2, :, 0:XW].rearrange(x_l, h=HEADS)[:, :, :, 0:C_HEAD],
                                      G[:, u % 3].rearrange(x_l, h=HEADS)[:, :, :, 0:C_HEAD],
                                      jh(PR[:])[:, :, :, None].to_broadcast([P, J, HEADS, C_HEAD]),
                                      ALU.mult).then_inc(s_ms, 1)

                def masks(g):
                    dve.wait_ge(s_kc, g + 1)
                    dve.tensor_tensor(MS[:, 1:P], KT[:, 0:P - 1], KT[:, 1:P], ALU.subtract)
                    dve.tensor_scalar(FS[:], KT[:], KT[:, 0:1], -1.0, ALU.subtract, ALU.mult)
                    dve.tensor_scalar(LS[:], KT[:], KT[:, P - 1:P], None, ALU.subtract).then_inc(s_mk, 1)

                def blocks(g, at_):
                    _, v = nc.values_load_multi_w_load_instructions(
                        BLK[0:1, bass.ds(g + 2, 1), at_:at_ + 8], engines=DVE_ONLY, min_val=0, max_val=NB - 1)
                    blk[at_:at_ + 8] = v

                def sums(g, u, chunks):
                    for j in chunks:
                        if j % TRI == 0:
                            dve.wait_ge(s_m, (g + 2) * NT + j // TRI + 1)
                        dve.wait_ge(s_c, (g + 2) * J + j + 3 * TRI)
                        a = ACC[:, bass.ds(blk[j], 1), :]
                        k = (NT * (u + 2) + j // TRI) % 3, (j % TRI) * MW
                        dve.tensor_tensor(a, pu[:, k[0], k[1]:k[1] + MW][:, None, :], a, ALU.add).then_inc(s_c, 1)

                def scale(c, g):
                    dve.wait_ge(s_fx, g + 2)
                    dve.wait_ge(s_c, (g + 2) * J + 3 * TRI)
                    a = ACC[:, bass.ds(blk[0], 1), 0:XW].rearrange("p a (h c) -> p (a h) c", h=HEADS)
                    c.mark(dve.scalar_tensor_tensor(a, pf[:, :, None].to_broadcast([P, HEADS, HW]), 1.0, a,
                                                    ALU.add, ALU.mult))

                dve.memset(MS[:], -BIG)
                dve.memset(last_m[:], -BIG)
                dve.memset(aa[:], -BIG)
                dve.memset(ab[:], -BIG)
                dve.memset(wb[:], -BIG)
                dve.memset(OH[:, 2:4], 0.0)
                dve.memset(MSG[:], 0.0)
                dve.memset(G[:, 2], 0.0)
                dve.memset(PR[:], 0.0)
                dve.memset(pf, 0.0)
                dve.tensor_copy(OHF, OHB[0:NB, :])
                dve.memset(ACC[:], 0.0).then_inc(s_one, 1)
                dve.wait_ge(s_one, 1)
                dve.sem_inc(s_c, 3 * TRI)
                dve.sem_inc(s_fx, 1)
                dve.sem_inc(s_te, 2)
                dve.sem_inc(s_mk, 1)
                dve.sem_inc(s_l, 1)
                dve.sem_inc(s_ms, 2)
                dve.sem_inc(s_p, 1)
                dve.sem_inc(s_mp, 1)
                one_hot(0, 0)
                one_hot(1, 1)
                masks(0)
                blk = [None] * 16
                n_own = 9
                blocks(-2, 0)
                sums(-2, -2, range(8))
                flat = "o h j -> o (h j)"
                x_l = "p j (h c) -> p j h c"

                def step(i, u, g):
                    c = Chain(dve, own, i, UN * n_own)
                    c.n = u * n_own
                    before = (g - 1, u - 1)

                    def row(t, at_, n, k=HEADS):
                        return t[:, bass.ds(g * J + at_, n)][:, None, :].to_broadcast([1, k, n])

                    messages(g - 1, u - 1)
                    blocks(g - 2, 8)
                    dve.wait_ge(s_g[u % 3], 16 * J * ((UN // 3) * i + u // 3 + 1))
                    a_src = G[:, u % 3, :, C_HEAD:XW:HW].rearrange("p j h -> p h j")
                    c.mark(dve.tensor_tensor(L[:], a_src, AE[:, :, bass.ds(g * J, J)], ALU.add))
                    sums(g - 2, u - 2, (8,))
                    dve.wait_ge(s_x, g + 2)
                    c.join()
                    c.mark(dve.tensor_tensor(L[:], L[:], px_l, ALU.add))
                    sums(g - 2, u - 2, (9,))
                    c.join()
                    dve.scalar_tensor_tensor(L[:], L[:], SLOPE, L[:], ALU.mult, ALU.max).then_inc(s_l, 1)
                    sums(g - 2, u - 2, (10,))
                    dve.wait_ge(s_lt, g + 1)
                    c.mark(dve.tensor_tensor_scan(FW[:], MS[:, 0:P], pl[0:R, 0:P], -BIG, ALU.add, ALU.max))
                    sums(g - 2, u - 2, (11,))
                    c.join()
                    dve.tensor_tensor_scan(CM[:, ::-1], MS[:, P:0:-1], FW[:, ::-1], -BIG,
                                           ALU.add, ALU.max).then_inc(s_cm, 1)
                    sums(g - 2, u - 2, (12,))
                    one_hot(g + 2, u + 2)
                    blocks(g - 1, 0)
                    sums(g - 2, u - 2, (13,))
                    dve.tensor_tensor(aa[:, :, 1:], row(WHOLE, 0, J - 1), row(LINK, 1, J - 1), ALU.add)
                    dve.tensor_tensor(ab[:, :, 0:J - 1], row(WHOLE, 1, J - 1), row(LINK, 1, J - 1), ALU.add)
                    dve.tensor_tensor(wa[:, :, 0:1], last_m[:, :, None], row(LINK, 0, 1), ALU.add)
                    sums(g - 2, u - 2, (14,))
                    dve.wait_ge(s_row, g + 1)
                    c.link(dve.tensor_copy(rows[:].rearrange("o a h j -> o (a h j)"), pc[0:1, 0:2 * R]))
                    scale(c, g - 1)
                    dve.tensor_tensor(wa[:, :, 1:], rows[:, 1, :, 0:J - 1], row(LINK, 1, J - 1), ALU.add)
                    c.link(dve.tensor_tensor(wb[:, :, 0:J - 1], rows[:, 0, :, 1:], row(LINK, 1, J - 1), ALU.add))
                    dve.tensor_tensor_scan(cin[:].rearrange(flat), aa[:].rearrange(flat), wa[:].rearrange(flat),
                                           -BIG, ALU.add, ALU.max)
                    dve.tensor_tensor_scan(cbk[:].rearrange(flat)[:, ::-1], ab[:].rearrange(flat)[:, ::-1],
                                           wb[:].rearrange(flat)[:, ::-1], -BIG, ALU.add, ALU.max).then_inc(s_cc, 1)
                    sums(*before, (0,))
                    dve.wait_ge(s_i, g + 3)
                    dve.wait_ge(s_cc, g + 1)
                    dve.scalar_tensor_tensor(last_m[:], cin[:, :, J - 1], ws[:, J - 1:J],
                                             rows[:, 1, :, J - 1], ALU.add, ALU.max)
                    c.link(dve.scalar_tensor_tensor(f0[:], cbk[:, :, 0], ws[:, 0:1],
                                                    rows[:, 0, :, 0], ALU.add, ALU.max))
                    c.link(dve.tensor_tensor(f0[:], f0[:], cin[:, :, 0], ALU.max))
                    dve.tensor_tensor(f0[:], cin[:, :, 0], f0[:], ALU.subtract).then_inc(s_fd, 1)
                    dve.wait_ge(s_col, g + 1)
                    c.mark(dve.scalar_tensor_tensor(CM[:], FS[:], pc[0:R, 128:129], CM[:], ALU.add, ALU.max))
                    sums(*before, (1,))
                    c.join()
                    dve.scalar_tensor_tensor(CM[:], LS[:], pc[0:R, 129:130], CM[:], ALU.add, ALU.max).then_inc(s_r, 1)
                    sums(*before, (2, 3))
                    dve.wait_ge(s_f, g + 1)
                    dve.tensor_scalar(f1[:], f1[:], -1.0, None, ALU.add).then_inc(s_fm, 1)
                    sums(*before, (4,))
                    dve.wait_ge(s_rt, g + 1)
                    dve.tensor_tensor(DL[:], L[:], pm, ALU.subtract).then_inc(s_dl, 1)
                    sums(*before, (5,))
                    dve.tensor_tensor(MSG[:, u % 2, :, XW:XW + HEADS], jh(pm),
                                      LAST[:, bass.ds(g * J, J)][:, :, None].to_broadcast([P, J, HEADS]), ALU.mult)
                    sums(*before, (6,))
                    masks(g + 1)
                    sums(*before, (7,))
                    assert c.n == (u + 1) * n_own, (c.n, n_own)
                steps(dve, step)
                c = Chain(dve, own, N_GRP // UN, UN * n_own)
                blocks(N_GRP - 2, 8)
                sums(N_GRP - 2, UN - 2, range(8, J))
                messages(N_GRP - 1, UN - 1)
                blocks(N_GRP - 1, 0)
                blocks(N_GRP - 1, 8)
                scale(c, N_GRP - 1)
                c.join()
                sums(N_GRP - 1, UN - 1, range(J))
        stage(attention)

        def finish(at, block):
            NQ = NB // QUAD
            s_d = sem("f_d", at)
            s_m = sem("f_m", at)
            s_e = sem("f_e", at)
            s_o = sem("f_o", at)
            s_t = sem("f_t", at)
            shape = [P, NB, HEADS]
            sl = sb("sl", shape, F32, at)
            mr = sb("mr", shape, F32, at)
            mx = sb("mx", shape, F32, at)
            de = sb("de", [P, 2, NB, HEADS], F32, at)
            ex = sb("ex", [P, 2, NB, HEADS], F32, at)
            SIX = 6
            assert NQ % SIX == 1
            A = sb("A", [P, SIX, QUAD, D], F32, at)
            B = sb("B", [P, SIX, QUAD, D], F32, at)
            s_b = sem("f_b", at)
            s_ab = sem("f_ab", at)
            s_s = sem("f_s", at)
            X = sb("X", [P, NB, D], F32, at)
            H = sb("H", [P, NB, XW], F32, at)
            s_x = sem("f_x", at)
            s_h = sem("f_h", at)
            Hh = H[:].rearrange("p b (h c) -> p b h c", h=HEADS)
            Ah = ACC[:, :, 0:XW].rearrange("p b (h c) -> p b h c", h=HEADS)

            @block.scalar
            def _(act):
                act.dma_start(H[:], x_tab.rearrange("(b p) f -> p b f", p=P)).then_inc(s_h, 16)
                act.wait_ge(s_m, 1)
                act.activation(ex[:], de[:], ACT.Exp).then_inc(s_e, 1)

            @block.vector
            def _(dve):
                c = Chain(dve, s_o)
                wide = RCNT[:, :, None].to_broadcast(shape)
                c.link(dve.tensor_tensor(sl[:], ACC[:, :, XW + HEADS:], wide, ALU.mult))
                c.link(dve.tensor_tensor(sl[:], sl[:], SELF[:], ALU.add))
                c.link(dve.scalar_tensor_tensor(sl[:], sl[:], SLOPE, sl[:], ALU.mult, ALU.max))
                c.link(dve.tensor_tensor(mr[:], ACC[:, :, XW:XW + HEADS], NOEDGE[:, :, None].to_broadcast(shape), ALU.add))
                c.link(dve.tensor_tensor(mx[:], mr[:], sl[:], ALU.max))
                dve.tensor_tensor(de[:, 0], mr[:], mx[:], ALU.subtract)
                dve.tensor_tensor(de[:, 1], sl[:], mx[:], ALU.subtract).then_inc(s_m, 1)
                dve.wait_ge(s_e, 1)
                c.link(dve.tensor_tensor(mx[:], Ah[:, :, :, C_HEAD], ex[:, 0], ALU.mult))
                c.link(dve.tensor_tensor(mx[:], mx[:], ex[:, 1], ALU.add))
                c.link(dve.reciprocal(mx[:], mx[:]))
                dve.tensor_tensor(ex[:, 0], ex[:, 0], mx[:], ALU.mult)
                c.link(dve.tensor_tensor(ex[:, 1], ex[:, 1], mx[:], ALU.mult), alone=True)
                dve.wait_ge(s_h, 16)

                def by(n, quad):
                    return ex[:, n, quad, :][:, :, :, None].to_broadcast([P, QUAD, HEADS, C_HEAD])

                def heads(t):
                    return t.rearrange("p b (h c) -> p b h c", h=HEADS)

                def steps(first, n):
                    quad = [bass.ds((first + m) * QUAD, QUAD) for m in range(n)]
                    for m in range(n):
                        dve.tensor_tensor(heads(A[:, m]), Ah[:, quad[m], :, 0:C_HEAD], by(0, quad[m]), ALU.mult)
                        dve.tensor_tensor(heads(B[:, m]), Hh[:, quad[m], :, 0:C_HEAD], by(1, quad[m]), ALU.mult
                                          ).then_inc(s_ab, 1)
                    for m in range(n):
                        dve.wait_ge(s_ab, first + m + 1)
                        dve.tensor_tensor(A[:, m], A[:, m], B[:, m], ALU.add).then_inc(s_s, 1)
                    for m in range(n):
                        dve.wait_ge(s_b, first + m + 1)
                        dve.wait_ge(s_s, first + m + 1)
                        dve.tensor_tensor(X[:, quad[m], :], X[:, quad[m], :], A[:, m], ALU.add).then_inc(s_d, 1)
                    dve.wait_ge(s_d, first + n)
                with dve.Fori(0, NQ // SIX) as i:
                    steps(SIX * i, SIX)
                steps(NQ - 1, 1)

            @block.gpsimd
            def _(pool):
                pool.wait_ge(s_x, 16)
                with pool.Fori(0, NQ) as i:
                    x4 = X[:, bass.ds(i * QUAD, QUAD), :]
                    pool.tensor_tensor(x4, x4, bia[:, None, :].to_broadcast([P, QUAD, D]), ALU.add).then_inc(s_b, 1)

            @block.sync
            def _(sp):
                full = N_BLK - 1
                o = out[0:full * P].rearrange("(b p) f -> p b f", p=P)
                sp.dma_start(X[:], x_keep).then_inc(s_x, 16)
                with sp.Fori(0, full // QUAD) as i:
                    sp.wait_ge(s_d, i + 1)
                    quad = bass.ds(i * QUAD, QUAD)
                    sp.dma_start(o[:, quad, :], X[:, quad, :]).then_inc(s_t, 16)
                sp.wait_ge(s_d, NQ)
                sp.dma_start(out[full * P:, :], X[0:TAIL, full, :]).then_inc(s_t, 16)
                sp.wait_ge(s_t, 16 * (full // QUAD + 1))

        stage(finish)


_INS = ["x", "src", "dst", "edge_attr_16", "L0_gnn_W1l", "L0_gnn_W1r", "L0_gnn_b1", "L0_gnn_W2l", "L0_gnn_W2r",
        "L0_gnn_b2", "L0_gnn_gamma", "L0_gnn_beta", "L1_gnn_W", "L1_gnn_W_edge", "L1_gnn_att_src",
        "L1_gnn_att_dst", "L1_gnn_att_edge", "L1_gnn_bias"]


def kernel(**inputs):
    import concourse.bacc as bacc
    from concourse.bass_utils import run_bass_kernel_spmd as run

    nc = bacc.Bacc("TRN2", target_bir_lowering=False, num_devices=1)
    arrays, args = {}, []
    for name in _INS:
        a = np.ascontiguousarray(inputs[name])
        arrays["in_" + name] = a
        args.append(nc.dram_tensor("in_" + name, a.shape, mybir.dt.from_np(a.dtype), kind="ExternalInput").ap())
    result = nc.dram_tensor("out", (N_NODES, D), F32, kind="ExternalOutput").ap()
    build(nc, *args, result)
    r = run(nc, [arrays], core_ids=[0])
    return r.results[0]["out"]
```
